# Optimizing a Trainium2 kernel written in Bass

```python
import numpy as np
import jax
import jax.numpy as jnp

def _softmax(x, axis=-1):
    return jax.nn.softmax(x, axis=axis)

def _gelu(x):
    return jax.nn.gelu(x, approximate=True)

def _silu(x):
    return jax.nn.silu(x)

def _sigmoid(x):
    return jax.nn.sigmoid(x)

def _layernorm(x, axis=-1, eps=1e-05):
    m = jnp.mean(x, axis=axis, keepdims=True)
    v = jnp.var(x, axis=axis, keepdims=True)
    return (x - m) / jnp.sqrt(v + eps)

def _scatter_add(tgt, idx, src, axis=0):
    return tgt.at[idx].add(src)

def _segment_sum(src, seg, n):
    return jax.ops.segment_sum(src, seg, n)
kernel_name = 'mk_flamingo_gated_d2_seqx_r8_10b4d6'

def setup_inputs(seed: int=0):
    np.random.seed(seed)
    _w = jnp.asarray

    def _rec_inputs():
        import jax
        import jax.numpy as jnp
        _rk = jax.random.key(seed)
        x = 7.22e-05 + 1 * jax.random.normal(jax.random.fold_in(_rk, 1), (4, 256, 256), jnp.float32)
        _lenS = 256 - jax.random.randint(jax.random.fold_in(_rk, 7), (4,), 0, max(1, 256 // 4) + 1, jnp.int32)
        _lenS2 = 1601 - jax.random.randint(jax.random.fold_in(_rk, 8), (4,), 0, max(1, 1601 // 4) + 1, jnp.int32)
        _ctx_1024P = jax.random.normal(jax.random.fold_in(_rk, 11), (4, 16, 128), jnp.float32)
        _ctx_1024c = jax.random.dirichlet(jax.random.fold_in(_rk, 511), 0.3 * jnp.ones((16,), jnp.float32), (4, 1601))
        _ctx_1024t = jnp.einsum('bsk,bkd->bsd', _ctx_1024c, _ctx_1024P)
        _ctx_1024t = _ctx_1024t * jax.lax.rsqrt(jnp.mean(jnp.square(_ctx_1024t)) + 1e-12) * 0.953939
        ctx_1024 = -0.000673644 + 1.00013 * (_ctx_1024t + 0.3 * jax.random.normal(jax.random.fold_in(_rk, 611), (4, 1601, 128), jnp.float32))
        _validS = jnp.arange(256)[None, :] < _lenS[:, None]
        _validS2 = jnp.arange(1601)[None, :] < _lenS2[:, None]
        _causal = jnp.tril(jnp.ones((256, 256), dtype=bool))
        mask_BxS2_bf1 = jnp.ones((4, 1601), dtype=bool)
        _g = jax.random.normal(jax.random.fold_in(_rk, 9001), (2, 2), jnp.float32)
        _g = jnp.sign(_g) * jnp.maximum(jnp.abs(_g), 1.0) + (_g == 0) * 1.0
        g_xattn = _g[0]
        g_ffn = _g[1]
        return (x, ctx_1024, mask_BxS2_bf1, g_xattn, g_ffn)
    x, ctx_1024, mask_BxS2_bf1, g_xattn, g_ffn = _rec_inputs()

    def _L0_xattn_setup():
        import jax, jax.numpy as jnp
        import numpy as np
        B, S1, S2, DCA = (2, 256, 128, 16)
        QDIM, KDIM, H = (256, 128, 16)
        HD = QDIM // H
        SCALE = HD ** (-0.5)
        EPS = 1e-06
        DCA_WEIGHT = 1.0

        def _ln(t, w, b):
            m = jnp.mean(t, axis=-1, keepdims=True)
            v = jnp.var(t, axis=-1, keepdims=True)
            return (t - m) * jax.lax.rsqrt(v + EPS) * w + b

        def _attn(q, k, v):
            s = jnp.einsum('bhqd,bhkd->bhqk', q, k) * SCALE
            p = jax.nn.softmax(s, axis=-1)
            return jnp.einsum('bhqk,bhkd->bhqd', p, v)
        key = jax.random.key(seed)
        ks = jax.random.split(key, 8)
        w = lambda k, shape: jax.random.normal(k, shape, jnp.float32) * 0.02
        return {'x': jax.random.normal(ks[0], (B, S1, QDIM), jnp.float32), 'y': jax.random.normal(ks[1], (B, S2 + DCA, KDIM), jnp.float32), 'Wq': w(ks[2], (QDIM, QDIM)), 'bq': jnp.zeros((QDIM,), jnp.float32), 'Wk': w(ks[3], (KDIM, QDIM)), 'bk': jnp.zeros((QDIM,), jnp.float32), 'Wv': w(ks[4], (KDIM, QDIM)), 'bv': jnp.zeros((QDIM,), jnp.float32), 'Wkv_dca': w(ks[5], (KDIM, 2 * QDIM)), 'bkv_dca': jnp.zeros((2 * QDIM,), jnp.float32), 'qn_w': jnp.ones((HD,), jnp.float32), 'qn_b': jnp.zeros((HD,), jnp.float32), 'kn_w': jnp.ones((HD,), jnp.float32), 'kn_b': jnp.zeros((HD,), jnp.float32), 'kn_dca_w': jnp.ones((HD,), jnp.float32), 'kn_dca_b': jnp.zeros((HD,), jnp.float32), 'Wo': w(ks[6], (QDIM, QDIM)), 'bo': jnp.zeros((QDIM,), jnp.float32)}
    _L0_xattn_all = _L0_xattn_setup()
    _L0_xattn_in = {k: v for k, v in _L0_xattn_all.items() if k in ('Wq', 'bq', 'Wk', 'bk', 'Wv', 'bv', 'Wkv_dca', 'bkv_dca', 'qn_w', 'qn_b', 'kn_w', 'kn_b', 'kn_dca_w', 'kn_dca_b', 'Wo', 'bo')}
    del _L0_xattn_all

    def _L0_ffn_setup():
        import jax, jax.numpy as jnp
        import numpy as np
        B, S, EMB = (4, 256, 256)
        LAT, HID = (64, 128)
        E, K = (16, 8)
        SCALE = 2.5

        def _w(key, shape, fan_in):
            return jax.random.normal(key, shape, jnp.float32) * fan_in ** (-0.5)

        def _sqrelu(x):
            return jnp.square(jax.nn.relu(x))
        key = jax.random.key(seed)
        ks = jax.random.split(key, 11)
        return {'x': jax.random.normal(ks[0], (B, S, EMB), jnp.float32), 'sw1': _w(ks[1], (HID, EMB), EMB), 'swg': _w(ks[2], (HID, EMB), EMB), 'sw2': _w(ks[3], (EMB, HID), HID), 'rw1': _w(ks[4], (E, HID, LAT), LAT), 'rwg': _w(ks[5], (E, HID, LAT), LAT), 'rw2': _w(ks[6], (E, LAT, HID), HID), 'Wg': _w(ks[7], (E, EMB), EMB), 'Wdown': _w(ks[8], (LAT, EMB), EMB), 'Wup': _w(ks[9], (EMB, LAT), LAT), 'biases': jnp.zeros((E,), jnp.float32)}
    _L0_ffn_all = _L0_ffn_setup()
    _L0_ffn_in = {k: v for k, v in _L0_ffn_all.items() if k in ('sw1', 'swg', 'sw2', 'rw1', 'rwg', 'rw2', 'Wg', 'Wdown', 'Wup', 'biases')}
    del _L0_ffn_all

    def _L1_xattn_setup():
        import jax, jax.numpy as jnp
        import numpy as np
        N_HEADS = 16
        N_KV_HEADS = 8
        HEAD_DIM = 128
        D_TEXT = 256
        D_VISION = 128
        GROUPS = N_HEADS // N_KV_HEADS
        key = jax.random.key(seed)
        ks = jax.random.split(key, 6)
        B, T_text, T_vis = (4, 256, 72)
        text_hidden = jax.random.normal(ks[0], (B, T_text, D_TEXT), dtype=jnp.float32)
        vision_tokens = jax.random.normal(ks[1], (B, T_vis, D_VISION), dtype=jnp.float32)
        vision_mask = jnp.ones((B, T_vis), dtype=bool)
        s = 0.02
        Wq = jax.random.normal(ks[2], (D_TEXT, N_HEADS * HEAD_DIM), dtype=jnp.float32) * s
        Wk = jax.random.normal(ks[3], (D_VISION, N_KV_HEADS * HEAD_DIM), dtype=jnp.float32) * s
        Wv = jax.random.normal(ks[4], (D_VISION, N_KV_HEADS * HEAD_DIM), dtype=jnp.float32) * s
        Wo = jax.random.normal(ks[5], (N_HEADS * HEAD_DIM, D_TEXT), dtype=jnp.float32) * s
        return {'text_hidden': text_hidden, 'vision_tokens': vision_tokens, 'vision_mask': vision_mask, 'Wq': Wq, 'Wk': Wk, 'Wv': Wv, 'Wo': Wo}
    _L1_xattn_all = _L1_xattn_setup()
    _L1_xattn_in = {k: v for k, v in _L1_xattn_all.items() if k in ('Wq', 'Wk', 'Wv', 'Wo')}
    del _L1_xattn_all

    def _L1_ffn_setup():
        import jax, jax.numpy as jnp
        import numpy as np
        D_MODEL = 256
        D_EXPERT = 1024
        EPS = 1e-08

        def ternary_quant(w):
            scale = jnp.mean(jnp.abs(w)) + EPS
            q = jnp.clip(jnp.round(w / scale), -1.0, 1.0) * scale
            return w + jax.lax.stop_gradient(q - w)
        key = jax.random.key(seed)
        k_x, k_up, k_gate, k_down = jax.random.split(key, 4)
        std_in = 1.0 / np.sqrt(D_MODEL)
        std_exp = 1.0 / np.sqrt(D_EXPERT)
        return {'x': jax.random.normal(k_x, (4, 256, D_MODEL), dtype=jnp.float32), 'W_up': jax.random.normal(k_up, (D_EXPERT, D_MODEL), dtype=jnp.float32) * std_in, 'W_gate': jax.random.normal(k_gate, (D_EXPERT, D_MODEL), dtype=jnp.float32) * std_in, 'W_down': jax.random.normal(k_down, (D_MODEL, D_EXPERT), dtype=jnp.float32) * std_exp}
    _L1_ffn_all = _L1_ffn_setup()
    _L1_ffn_in = {k: v for k, v in _L1_ffn_all.items() if k in ('W_up', 'W_gate', 'W_down')}
    del _L1_ffn_all
    return {'x': x, 'ctx_1024': ctx_1024, 'mask_BxS2_bf1': mask_BxS2_bf1, 'g_xattn': g_xattn, 'g_ffn': g_ffn, 'L0_xattn_Wq': _L0_xattn_in['Wq'], 'L0_xattn_bq': _L0_xattn_in['bq'], 'L0_xattn_Wk': _L0_xattn_in['Wk'], 'L0_xattn_bk': _L0_xattn_in['bk'], 'L0_xattn_Wv': _L0_xattn_in['Wv'], 'L0_xattn_bv': _L0_xattn_in['bv'], 'L0_xattn_Wkv_dca': _L0_xattn_in['Wkv_dca'], 'L0_xattn_bkv_dca': _L0_xattn_in['bkv_dca'], 'L0_xattn_qn_w': _L0_xattn_in['qn_w'], 'L0_xattn_qn_b': _L0_xattn_in['qn_b'], 'L0_xattn_kn_w': _L0_xattn_in['kn_w'], 'L0_xattn_kn_b': _L0_xattn_in['kn_b'], 'L0_xattn_kn_dca_w': _L0_xattn_in['kn_dca_w'], 'L0_xattn_kn_dca_b': _L0_xattn_in['kn_dca_b'], 'L0_xattn_Wo': _L0_xattn_in['Wo'], 'L0_xattn_bo': _L0_xattn_in['bo'], 'L0_ffn_sw1': _L0_ffn_in['sw1'], 'L0_ffn_swg': _L0_ffn_in['swg'], 'L0_ffn_sw2': _L0_ffn_in['sw2'], 'L0_ffn_rw1': _L0_ffn_in['rw1'], 'L0_ffn_rwg': _L0_ffn_in['rwg'], 'L0_ffn_rw2': _L0_ffn_in['rw2'], 'L0_ffn_Wg': _L0_ffn_in['Wg'], 'L0_ffn_Wdown': _L0_ffn_in['Wdown'], 'L0_ffn_Wup': _L0_ffn_in['Wup'], 'L0_ffn_biases': _L0_ffn_in['biases'], 'L1_xattn_Wq': _L1_xattn_in['Wq'], 'L1_xattn_Wk': _L1_xattn_in['Wk'], 'L1_xattn_Wv': _L1_xattn_in['Wv'], 'L1_xattn_Wo': _L1_xattn_in['Wo'], 'L1_ffn_W_up': _L1_ffn_in['W_up'], 'L1_ffn_W_gate': _L1_ffn_in['W_gate'], 'L1_ffn_W_down': _L1_ffn_in['W_down']}

def reference(x, ctx_1024, mask_BxS2_bf1, g_xattn, g_ffn, L0_xattn_Wq, L0_xattn_bq, L0_xattn_Wk, L0_xattn_bk, L0_xattn_Wv, L0_xattn_bv, L0_xattn_Wkv_dca, L0_xattn_bkv_dca, L0_xattn_qn_w, L0_xattn_qn_b, L0_xattn_kn_w, L0_xattn_kn_b, L0_xattn_kn_dca_w, L0_xattn_kn_dca_b, L0_xattn_Wo, L0_xattn_bo, L0_ffn_sw1, L0_ffn_swg, L0_ffn_sw2, L0_ffn_rw1, L0_ffn_rwg, L0_ffn_rw2, L0_ffn_Wg, L0_ffn_Wdown, L0_ffn_Wup, L0_ffn_biases, L1_xattn_Wq, L1_xattn_Wk, L1_xattn_Wv, L1_xattn_Wo, L1_ffn_W_up, L1_ffn_W_gate, L1_ffn_W_down):
    import jax
    import jax.numpy as jnp

    def _L0_xattn_ref(x, y, Wq, bq, Wk, bk, Wv, bv, Wkv_dca, bkv_dca, qn_w, qn_b, kn_w, kn_b, kn_dca_w, kn_dca_b, Wo, bo):
        import jax, jax.numpy as jnp
        import numpy as np
        B, S1, S2, DCA = (2, 256, 128, 16)
        QDIM, KDIM, H = (256, 128, 16)
        HD = QDIM // H
        SCALE = HD ** (-0.5)
        EPS = 1e-06
        DCA_WEIGHT = 1.0

        def _ln(t, w, b):
            m = jnp.mean(t, axis=-1, keepdims=True)
            v = jnp.var(t, axis=-1, keepdims=True)
            return (t - m) * jax.lax.rsqrt(v + EPS) * w + b

        def _attn(q, k, v):
            s = jnp.einsum('bhqd,bhkd->bhqk', q, k) * SCALE
            p = jax.nn.softmax(s, axis=-1)
            return jnp.einsum('bhqk,bhkd->bhqd', p, v)
        b, s1, _ = x.shape
        y_dca = y[:, -DCA:, :]
        y_main = y[:, :-DCA, :]
        kv_dca = (y_dca @ Wkv_dca + bkv_dca).reshape(b, DCA, 2, H, HD)
        k_dca = _ln(kv_dca[:, :, 0], kn_dca_w, kn_dca_b)
        v_dca = kv_dca[:, :, 1]
        s2 = y_main.shape[1]
        q = _ln((x @ Wq + bq).reshape(b, s1, H, HD), qn_w, qn_b)
        kv = jnp.concatenate([y_main @ Wk + bk, y_main @ Wv + bv], axis=-1)
        kv = kv.reshape(b, s2, H, 2 * HD)
        k = _ln(kv[..., :HD], kn_w, kn_b)
        v = kv[..., HD:]
        qT = q.transpose(0, 2, 1, 3)
        ctx = _attn(qT, k.transpose(0, 2, 1, 3), v.transpose(0, 2, 1, 3))
        ctx = ctx.transpose(0, 2, 1, 3).reshape(b, s1, QDIM)
        ctx_dca = _attn(qT, k_dca.transpose(0, 2, 1, 3), v_dca.transpose(0, 2, 1, 3))
        ctx_dca = ctx_dca.transpose(0, 2, 1, 3).reshape(b, s1, QDIM)
        ctx = ctx + DCA_WEIGHT * ctx_dca
        return ctx @ Wo + bo

    def _L0_ffn_ref(x, sw1, swg, sw2, rw1, rwg, rw2, Wg, Wdown, Wup, biases):
        import jax, jax.numpy as jnp
        import numpy as np
        B, S, EMB = (4, 256, 256)
        LAT, HID = (64, 128)
        E, K = (16, 8)
        SCALE = 2.5

        def _w(key, shape, fan_in):
            return jax.random.normal(key, shape, jnp.float32) * fan_in ** (-0.5)

        def _sqrelu(x):
            return jnp.square(jax.nn.relu(x))
        b, s, d = x.shape
        x2 = x.reshape(-1, d)
        shared = x2 @ sw1.T * _sqrelu(x2 @ swg.T) @ sw2.T
        xl = x2 @ Wdown.T
        probas = jax.nn.sigmoid(x2 @ Wg.T)
        _, idx = jax.lax.top_k(probas + biases, K)
        p = jnp.take_along_axis(probas, idx, axis=-1)
        p = p / p.sum(-1, keepdims=True) * SCALE
        T = x2.shape[0]
        w_dense = jnp.zeros((T, E), x2.dtype).at[jnp.arange(T)[:, None], idx].add(p)
        acc = jnp.zeros_like(xl)
        for e in range(E):
            ye = xl @ rw1[e].T * _sqrelu(xl @ rwg[e].T) @ rw2[e].T
            acc = acc + w_dense[:, e:e + 1] * ye
        out = shared + acc @ Wup.T
        return out.reshape(b, s, d)

    def _L1_xattn_ref(text_hidden, vision_tokens, vision_mask, Wq, Wk, Wv, Wo):
        import jax, jax.numpy as jnp
        import numpy as np
        N_HEADS = 16
        N_KV_HEADS = 8
        HEAD_DIM = 128
        D_TEXT = 256
        D_VISION = 128
        GROUPS = N_HEADS // N_KV_HEADS
        B, T_text, _ = text_hidden.shape
        T_vis = vision_tokens.shape[1]
        scale = jnp.float32(np.sqrt(HEAD_DIM))
        q = (text_hidden @ Wq).reshape(B, T_text, N_HEADS, HEAD_DIM).transpose(0, 2, 1, 3)
        k = (vision_tokens @ Wk).reshape(B, T_vis, N_KV_HEADS, HEAD_DIM).transpose(0, 2, 1, 3)
        v = (vision_tokens @ Wv).reshape(B, T_vis, N_KV_HEADS, HEAD_DIM).transpose(0, 2, 1, 3)
        k = jnp.repeat(k, GROUPS, axis=1)
        v = jnp.repeat(v, GROUPS, axis=1)
        scores = jnp.einsum('bhtd,bhsd->bhts', q, k) / scale
        mask = vision_mask[:, None, None, :]
        scores = jnp.where(mask, scores, -jnp.inf)
        attn = jax.nn.softmax(scores, axis=-1)
        attn = jnp.nan_to_num(attn, nan=0.0)
        out = jnp.einsum('bhts,bhsd->bhtd', attn, v)
        out = out.transpose(0, 2, 1, 3).reshape(B, T_text, N_HEADS * HEAD_DIM)
        return out @ Wo

    def _L1_ffn_ref(x, W_up, W_gate, W_down):
        import jax, jax.numpy as jnp
        import numpy as np
        D_MODEL = 256
        D_EXPERT = 1024
        EPS = 1e-08

        def ternary_quant(w):
            scale = jnp.mean(jnp.abs(w)) + EPS
            q = jnp.clip(jnp.round(w / scale), -1.0, 1.0) * scale
            return w + jax.lax.stop_gradient(q - w)
        wu = ternary_quant(W_up)
        wg = ternary_quant(W_gate)
        wd = ternary_quant(W_down)
        up = jnp.einsum('bsd,ed->bse', x, wu)
        gate = jnp.einsum('bsd,ed->bse', x, wg)
        hidden = jax.nn.silu(up) * gate
        return jnp.einsum('bse,de->bsd', hidden, wd)
    x = x + jnp.tanh(g_xattn[0]) * _L0_xattn_ref(_layernorm(x, axis=-1), ctx_1024, L0_xattn_Wq, L0_xattn_bq, L0_xattn_Wk, L0_xattn_bk, L0_xattn_Wv, L0_xattn_bv, L0_xattn_Wkv_dca, L0_xattn_bkv_dca, L0_xattn_qn_w, L0_xattn_qn_b, L0_xattn_kn_w, L0_xattn_kn_b, L0_xattn_kn_dca_w, L0_xattn_kn_dca_b, L0_xattn_Wo, L0_xattn_bo)
    x = x + jnp.tanh(g_ffn[0]) * _L0_ffn_ref(_layernorm(x, axis=-1), L0_ffn_sw1, L0_ffn_swg, L0_ffn_sw2, L0_ffn_rw1, L0_ffn_rwg, L0_ffn_rw2, L0_ffn_Wg, L0_ffn_Wdown, L0_ffn_Wup, L0_ffn_biases)
    x = x + jnp.tanh(g_xattn[1]) * _L1_xattn_ref(_layernorm(x, axis=-1), ctx_1024, mask_BxS2_bf1, L1_xattn_Wq, L1_xattn_Wk, L1_xattn_Wv, L1_xattn_Wo)
    x = x + jnp.tanh(g_ffn[1]) * _L1_ffn_ref(_layernorm(x, axis=-1), L1_ffn_W_up, L1_ffn_W_gate, L1_ffn_W_down)
    return x

_drawn_inputs = setup_inputs


def setup_inputs(seed=0):
    import zlib

    import numpy as np

    out = dict(_drawn_inputs(seed))
    spreads = {'g_ffn': (-1.0, 0.6),
     'L0_xattn_bq': (0.0, 0.344),
     'L0_xattn_bk': (0.0, 0.1),
     'L0_xattn_bv': (0.0, 0.1),
     'L0_xattn_bkv_dca': (0.0, 0.1),
     'L0_xattn_qn_w': (1.0, 0.6),
     'L0_xattn_qn_b': (0.0, 0.362),
     'L0_xattn_kn_w': (1.0, 0.6),
     'L0_xattn_kn_b': (0.0, 0.8),
     'L0_xattn_kn_dca_w': (1.0, 0.6),
     'L0_xattn_kn_dca_b': (0.0, 0.8),
     'L0_xattn_bo': (0.0, 0.1),
     'L0_ffn_biases': (0.0, 0.1)}
    factors = {'L1_xattn_Wq': 8.0, 'L1_xattn_Wk': 8.0}
    for name, (base, spread) in spreads.items():
        noise = np.random.default_rng([zlib.crc32(name.encode()), seed]).standard_normal(out[name].shape)
        drawn = base * np.exp(spread * noise) if base else spread * noise
        out[name] = jnp.asarray(drawn.astype(out[name].dtype))
    for name, factor in factors.items():
        out[name] = (out[name] * factor).astype(out[name].dtype)
    return out
```

```python
from contextlib import ExitStack

import concourse.bass as bass
from concourse import mybir

F32 = mybir.dt.float32
BF16 = mybir.dt.bfloat16
U8 = mybir.dt.uint8
ALU = mybir.AluOpType
ACT = mybir.ActivationFunctionType
AX = mybir.AxisListType

B, S, D, KD = 4, 256, 256, 128
S2, NDCA = 1601, 16
NMAIN = S2 - NDCA
NKT = 13
TAIL = S2 - 12 * 128
TMAIN = NMAIN - 12 * 128
H = 16
NT = B * S // 128
E = 16
SCALE1 = 1.0 / float(128.0 ** 0.5)
NEG = 1e30
INS = ["x", "ctxT", "ctxk", "mrow", "mcol", "mtail", "gates", "wk0", "wv0", "wo0", "bo0", "prm",
       "sw1T", "swgT", "sw2T", "rw1T", "rwgT", "rw2T", "WgT", "WdT", "WuT", "bias_e",
       "wqT1", "wkT1", "wvT1", "wo1", "wup", "wgate", "wdown", "ident", "seld", "rsel"]


class Lane:

    def __init__(self, eng, sem):
        self.eng, self.sem, self.n, self.seen = eng, sem, 0, {}

    def wait(self, *after):
        for t in after:
            if t is None:
                continue
            if isinstance(t, list):
                self.wait(*t)
                continue
            sem, v = t
            if self.seen.get(id(sem), 0) < v:
                self.seen[id(sem)] = v
                self.eng.wait_ge(sem, v)

    def do(self, f, *after, sig=True):
        self.wait(*after)
        ins = f()
        if not sig:
            return None
        self.n += 1
        ins.then_inc(self.sem, 1)
        return (self.sem, self.n)

    def last(self):
        return (self.sem, self.n) if self.n else None


def program(nc, a, out):
    root = ExitStack()
    with root:
        def sem(name):
            return root.enter_context(nc.semaphore(name))

        engines = (("pe", nc.tensor), ("dve", nc.vector), ("act", nc.scalar), ("pool", nc.gpsimd), ("sp", nc.sync))
        pe, dve, act, pool, sp = (Lane(e, sem("s_" + n)) for n, e in engines)
        V, T, A, G = nc.vector, nc.tensor, nc.scalar, nc.gpsimd
        nd = [0]

        def sb(name, shape, dt=F32, stack=root):
            return stack.enter_context(nc.sbuf_tensor(name, shape, dt))

        def load(dst, src, *after, lane=None):
            nd[0] += 1
            s = sem(f"d{nd[0]}")
            lane = lane or sp
            lane.wait(*after)
            eng = nc.sync if lane is sp else nc.gpsimd
            eng.dma_start(dst, src).then_inc(s, 16)
            return (s, 16)

        class Counted:

            def __init__(self, name):
                self.s, self.n = sem(name), 0

            def start(self, dst, src, *after):
                sp.wait(*after)
                self.n += 16
                nc.sync.dma_start(dst, src).then_inc(self.s, 16)
                return (self.s, self.n)

        def mm(out_, lhsT, rhs, *after, start=True, stop=True, sig=True):
            return pe.do(lambda: T.matmul(out_, lhsT, rhs, start=start, stop=stop, skip_group_check=True),
                         *after, sig=sig)

        def tp(out_, in_, idn, *after, sig=True):
            return pe.do(lambda: T.transpose(out_, in_, idn), *after, sig=sig)

        def barrier():
            ts = [l.last() for l in (pe, dve, act, pool)]
            for l in (pe, dve, act, pool, sp):
                l.wait(ts)

        ST = [root.enter_context(nc.psum_tensor(f"ST{i}", [128, 1024], F32)) for i in range(2)]
        MB = [root.enter_context(nc.psum_tensor(f"MB{i}", [128, 512], F32)) for i in range(2)]
        PV = root.enter_context(nc.psum_tensor("PV", [128, 512], F32))
        MI = root.enter_context(nc.psum_tensor("MI", [128, 512], F32))
        HB = [ST[0][:, 0:512], ST[0][:, 512:1024], ST[1][:, 0:512], ST[1][:, 512:1024]]
        BANKS = HB + [MB[0][:, :], MB[1][:, :], PV[:, :], MI[:, :]]
        HBf, MBf, PVf, MIf = [None] * 4, [None] * 2, [None], [None]

        x_sb = sb("x_sb", [128, NT, D])
        idn = sb("idn", [128, 128])
        xnT = sb("xnT", [128, 2, B * S])
        gat = sb("gat", [128, 4])
        tg = sb("tg", [128, 4])
        cst = sb("cst", [128, 4])
        bns = sb("bns", [128, NT, 6])
        mv = sb("mv", [128, NT, 2])
        rst = sb("rst", [128, NT])
        rsq = sb("rsq", [128, NT])
        xn = sb("xn", [128, 2, D])

        t_x = load(x_sb[:, :, :], a["x"].rearrange("(t p) d -> p t d", p=128))
        t_id = load(idn[:, :], a["ident"])
        t_g = load(gat[:, :], a["gates"].partition_broadcast(128))
        t_c0 = pool.do(lambda: G.memset(cst[:, 0:1], 1e-5))
        t_c1 = pool.do(lambda: G.memset(cst[:, 1:2], 1e-6))
        t_tg = act.do(lambda: A.activation(tg[:, :], gat[:, :], ACT.Tanh), t_g)
        x_tok = [t_x] * NT

        def layernorm_T():
            t = None
            for i in range(NT):
                t1 = dve.do(lambda i=i: V.bn_stats(bns[:, i, :], x_sb[:, i, :]), x_tok[i])
                t = dve.do(lambda i=i: V.bn_aggr(mv[:, i, :], bns[:, i, :]), t1)
            t = act.do(lambda: A.activation(rsq[:, :], mv[:, :, 1], ACT.Sqrt, bias=cst[:, 0:1]), t, t_c0)
            tr = dve.do(lambda: V.reciprocal(rst[:, :], rsq[:, :]), t)
            done, xf = [], [None, None]
            for i in range(NT):
                k = i % 2
                t = dve.do(lambda i=i, k=k: V.tensor_scalar(xn[:, k, :], x_sb[:, i, :], mv[:, i, 0:1], rst[:, i:i + 1],
                                                       ALU.subtract, ALU.mult), tr, xf[k])
                tp(MB[k][:, 0:128], xn[:, k, 0:128], idn[:, :], t, t_id, MBf[k], sig=False)
                xf[k] = tp(MB[k][:, 128:256], xn[:, k, 128:256], idn[:, :])
                MBf[k] = act.do(lambda i=i, k=k: A.copy(xnT[:, :, i * 128:(i + 1) * 128],
                                                   MB[k][:, 0:256].rearrange("p (c n) -> p c n", c=2)), xf[k])
                done.append(MBf[k])
            return done

        L0 = ExitStack()
        ctxT = sb("ctxT", [128, B, S2], F32, L0)
        kst = sb("kst", [128, 8, S2], BF16, L0)
        va = sb("va", [128, NKT, H, 32], F32, L0)
        vd = sb("vd", [128, H, 32], F32, L0)
        kc = sb("kc", [128, NKT + 1, D], F32, L0)
        wk = sb("wk", [128, 7, D], F32, L0)
        wkc = sb("wkc", [128, 7, D], F32, L0)
        wv = sb("wv", [128, 4, D], F32, L0)
        wo = sb("wo", [128, 2, D], F32, L0)
        bo = sb("bo", [128, D], F32, L0)
        prm = sb("prm", [128, 12], F32, L0)
        Q = sb("Q", [128, 8, 512], BF16, L0)
        sq = sb("sq", [128, 6, D], F32, L0)
        ss = sb("ss", [128, NKT + 1, H], F32, L0)
        sr = sb("sr", [128, NKT + 1, H], F32, L0)
        sd = sb("sd", [128, NKT + 1, H], F32, L0)
        Xt = sb("Xt", [128, 2, 512], F32, L0)
        kth = sb("kth", [128, 2, S2], BF16, L0)
        ktl = sb("ktl", [128, 2, S2], BF16, L0)
        qth = sb("qth", [128, 512], BF16, L0)
        qtl = sb("qtl", [128, 512], BF16, L0)
        rsf = sb("rsf", [128, 16, 128], F32, L0)
        rsb = sb("rsb", [128, 4, 4, 128], BF16, L0)
        P0 = [sb(f"P0_{i}", [128, 1024], F32, L0) for i in range(3)]
        mxp = sb("mxp", [128, 2, 8, 4], F32, L0)
        mmx = sb("mmx", [128, 2, 16], F32, L0)
        mneg = sb("mneg", [16, 2, 128], BF16, L0)
        oT = sb("oT", [128, 512], F32, L0)
        rec = sb("rec", [128, 16], F32, L0)
        on = sb("on", [128, 16, 16], F32, L0)
        oc = sb("oc", [128, 2, D], F32, L0)
        ocT = sb("ocT", [128, 2, S], F32, L0)
        yo = sb("yo", [128, D], F32, L0)
        wsum = sb("wsum", [128, 112], F32, L0)

        t_wk = load(wk[:, :, :], a["wk0"])
        t_wv = load(wv[:, :, :], a["wv0"])
        t_rs = load(rsf[:, :, :], a["rsel"])
        t_rsb = pool.do(lambda: G.tensor_copy(rsb[:, :, :, :].rearrange("p a b n -> p (a b) n"), rsf[:, :, :]), t_rs)
        t_prm = load(prm[:, :], a["prm"])
        t_ctx = [load(ctxT[:, b, :], a["ctxT"][b]) for b in range(B)]
        t_wo = load(wo[:, :, :], a["wo0"])
        t_bo = load(bo[:, :], a["bo0"].partition_broadcast(128))

        t_q0 = pool.do(lambda: G.memset(Q[:, :, :], 0.0))
        t_va = pool.do(lambda: G.memset(va[:, :, :, :], 0.0))
        t_vd = pool.do(lambda: G.memset(vd[:, :, :], 0.0))
        t_va1 = pool.do(lambda: G.memset(va[:, 0:12, :, 16:17], 1.0), t_va)
        t_va2 = pool.do(lambda: G.memset(va[0:TMAIN, 12, :, 16:17], 1.0), t_va)
        t_vone = dve.do(lambda: V.tensor_scalar(vd[0:TAIL, :, 16:17], va[0:TAIL, 0, :, 16:17], prm[0:TAIL, 8:9], None,
                                                ALU.mult), t_va1, t_vd, t_prm)
        t = dve.do(lambda: V.tensor_reduce(wsum[:, :], wk[:, :, :].rearrange("p a (h d) -> p (a h) d", d=16),
                                           AX.X, ALU.add), t_wk)
        t_wkc = dve.do(lambda: V.scalar_tensor_tensor(
            out=wkc[:, :, :].rearrange("p a (h d) -> p (a h) d", d=16),
            in0=wsum[:, :].unsqueeze(2).to_broadcast([128, 112, 16]), scalar=-1.0 / 16,
            in1=wk[:, :, :].rearrange("p a (h d) -> p (a h) d", d=16), op0=ALU.mult, op1=ALU.add), t)

        xnt = layernorm_T()

        def grp(ap):
            return ap.rearrange("p (h d) -> p h d", d=16)

        state = {"kt": None, "qt": None, "kst": [None], "Q": [None], "va": None, "X": [None, None], "Hh": [None, None], "xi": 0, "bi": 0}

        def nb():
            state["bi"] += 1
            return (state["bi"] - 1) % 4

        def rstd_heads(lo, hi, n, after, sqfree):
            t = after
            for c in range(lo, hi, 6):
                e = min(hi, c + 6)
                t1 = act.do(lambda c=c, e=e: A.activation(sq[0:n, 0:e - c, :], kc[0:n, c:e, :], ACT.Square), t, sqfree)
                sqfree = dve.do(lambda c=c, e=e: V.tensor_reduce(
                    ss[0:n, c:e, :], sq[0:n, 0:e - c, :].rearrange("p k (h d) -> p k h d", d=16),
                    AX.X, ALU.add), t1)
            t1 = act.do(lambda: A.activation(sr[0:n, lo:hi, :], ss[0:n, lo:hi, :], ACT.Sqrt, scale=1.0 / 16,
                                             bias=cst[0:n, 1:2]), sqfree, t_c1)
            t1 = dve.do(lambda: V.reciprocal(sd[0:n, lo:hi, :], sr[0:n, lo:hi, :]), t1)
            v = kc[0:n, lo:hi, :].rearrange("p k (h d) -> p (k h) d", d=16)
            return dve.do(lambda: V.tensor_tensor(v, v, sd[0:n, lo:hi, :].rearrange("p k h -> p (k h)").unsqueeze(2)
                                                  .to_broadcast([n, (hi - lo) * 16, 16]), ALU.mult), t1), sqfree

        def split(bank, fill, n, wcol, hi, lo, after):
            i = state["xi"] % 2
            state["xi"] += 1
            tx = act.do(lambda: A.activation(Xt[:, i, 0:n], bank, ACT.Identity, scale=prm[:, wcol:wcol + 1],
                                             bias=prm[:, wcol + 1:wcol + 2]), fill, t_prm, state["X"][i])
            th = dve.do(lambda: V.tensor_copy(hi, Xt[:, i, 0:n]), tx, after)
            state["X"][i] = tl = dve.do(lambda: V.tensor_tensor(lo, Xt[:, i, 0:n], hi, ALU.subtract), th)
            return tx, tl

        def prep(b):
            free_kst, free_va, free_Q = state["kst"], state["va"], state["Q"]
            kct = []
            for kt in range(NKT + 1):
                n = 128 if kt < 12 else TAIL
                k0 = min(kt, 12) * 128
                w = 1 if kt == NKT else 0
                i = nb()
                mm(HB[i][0:n, 0:256], ctxT[:, b, k0:k0 + n], wkc[:, w, :], t_ctx[b], t_wkc, HBf[i], sig=False)
                t = mm(HB[i][0:n, 256:512], ctxT[:, b, k0:k0 + n], wv[:, w, :], t_wv)
                kct.append(dve.do(lambda n=n, kt=kt, i=i, w=w: V.tensor_tensor(
                    kc[0:n, kt, :], HB[i][0:n, 0:256], wkc[0:n, 4 + w, :], ALU.add), t, free_kst))
                if kt < NKT:
                    m = min(n, 128 if kt < 12 else TMAIN)
                    HBf[i] = dve.do(lambda m=m, kt=kt, i=i: V.tensor_tensor(
                        va[0:m, kt, :, 0:16], grp(HB[i][0:m, 256:512]), grp(wv[0:m, 2, :]), ALU.add),
                        t_va1, t_va2, free_va)
                else:
                    tv = dve.do(lambda n=n, i=i: V.tensor_tensor(vd[0:n, :, 0:16], grp(HB[i][0:n, 256:512]),
                                                            grp(wv[0:n, 3, :]), ALU.add), t_vone, free_va)
                    HBf[i] = dve.do(lambda n=n: V.tensor_scalar(vd[0:n, :, 0:16], vd[0:n, :, 0:16], prm[0:n, 8:9], None,
                                                           ALU.mult), tv)
            vtok = HBf[i]
            t_k12, sf = rstd_heads(0, 12, 128, kct[11], state.get("sq"))
            t_k14, sf = rstd_heads(12, 14, TAIL, kct[13], sf)
            free_kt = state["kt"]
            halves = []
            for hf_ in range(2):
                cs = slice(128 * hf_, 128 * hf_ + 128)
                for c in range(3):
                    i = nb()
                    for j in range(4):
                        fill = tp(HB[i][:, 128 * j:128 * j + 128], kc[:, 4 * c + j, cs], idn[:, :], t_k12, t_id, HBf[i],
                                  sig=(j == 3))
                    w_ = slice(512 * c, 512 * c + 512)
                    HBf[i], t = split(HB[i], fill, 512, 0, kth[:, hf_, w_], ktl[:, hf_, w_], free_kt)
                i = nb()
                fill = tp(HB[i][:, 0:TAIL], kc[0:TAIL, 12, cs], idn[0:TAIL, 0:TAIL], t_k14, HBf[i])
                w_ = slice(1536, NMAIN)
                HBf[i], t = split(HB[i][:, 0:TMAIN], fill, TMAIN, 0, kth[:, hf_, w_], ktl[:, hf_, w_], free_kt)
                i = nb()
                fill = tp(HB[i][:, 0:TAIL], kc[0:TAIL, 13, cs], idn[0:TAIL, 0:TAIL], HBf[i])
                w_ = slice(NMAIN, S2)
                HBf[i], t = split(HB[i][:, TMAIN:TAIL], fill, NDCA, 2, kth[:, hf_, w_], ktl[:, hf_, w_], free_kt)
                halves.append(t)
            ktok = []
            for p in range(8):
                for c in range(4):
                    i = nb()
                    w_ = slice(512 * c, min(512 * c + 512, S2))
                    n = w_.stop - w_.start
                    mm(HB[i][:, 0:n], rsb[:, p % 4, 0, :], kth[:, p // 4, w_], halves[p // 4], t_rsb, HBf[i], start=True,
                       stop=False, sig=False)
                    t = mm(HB[i][:, 0:n], rsb[:, p % 4, 1, :], ktl[:, p // 4, w_], start=False, stop=True)
                    parts = [(0, 512, 10)] if c < 3 else [(0, TMAIN, 10), (TMAIN, TAIL, 11)]
                    for lo, hi, oc_ in parts:
                        o = kst[:, p, 512 * c + lo:512 * c + hi]
                        if c % 2:
                            t1 = dve.do(lambda o=o, i=i, lo=lo, hi=hi, oc_=oc_: V.tensor_scalar(
                                o, HB[i][:, lo:hi], prm[:, oc_:oc_ + 1], None, ALU.add), t, free_kst)
                        else:
                            t1 = act.do(lambda o=o, i=i, lo=lo, hi=hi, oc_=oc_: A.activation(
                                o, HB[i][:, lo:hi], ACT.Identity, bias=prm[:, oc_:oc_ + 1]), t, free_kst)
                    HBf[i] = t1
                    if c == 2:
                        ta = t1
                ktok.append([ta, t1])
            state["kt"] = t
            t_kc_free = fill
            qt_ = []
            for t2 in range(2):
                i = nb()
                tok = b * S + t2 * 128
                mm(HB[i][:, 0:256], xnT[:, 0, tok:tok + 128], wkc[:, 2, :], HBf[i], xnt, start=True, stop=False,
                   sig=False)
                t = mm(HB[i][:, 0:256], xnT[:, 1, tok:tok + 128], wkc[:, 3, :], start=False, stop=True)
                HBf[i] = dve.do(lambda i=i, t2=t2: V.tensor_tensor(kc[:, t2, :], HB[i][:, 0:256], wkc[:, 6, :], ALU.add),
                                t, t_kc_free)
                qt_.append(HBf[i])
            t_q, sf = rstd_heads(0, 2, 128, qt_[1], sf)
            state["sq"] = sf
            i = nb()
            for j in range(4):
                fill = tp(HB[i][:, 128 * j:128 * j + 128], kc[:, j % 2, 128 * (j // 2):128 * (j // 2) + 128], idn[:, :],
                          t_q, HBf[i], sig=(j == 3))
            HBf[i], tq_ = split(HB[i], fill, 512, 4, qth[:, :], qtl[:, :], state["qt"])
            qtok = []
            for pp in range(4):
                i = nb()
                for j in range(2):
                    p = 2 * pp + j
                    w_ = slice(256 * (p // 4), 256 * (p // 4) + 256)
                    o = HB[i][:, 256 * j:256 * j + 256]
                    mm(o, rsb[:, p % 4, 2, :], qth[:, w_], tq_, HBf[i], start=True, stop=False, sig=False)
                    t = mm(o, rsb[:, p % 4, 3, :], qtl[:, w_], start=False, stop=True)
                act.do(lambda i=i, pp=pp: A.copy(Q[0:64, 2 * pp:2 * pp + 2, 0:256],
                                                 HB[i][0:64, :].rearrange("p (a n) -> p a n", a=2)),
                       t, free_Q, t_q0, sig=False)
                HBf[i] = t1 = act.do(lambda i=i, pp=pp: A.copy(Q[64:128, 2 * pp:2 * pp + 2, 256:512],
                                                          HB[i][64:128, :].rearrange("p (a n) -> p a n", a=2)))
                qtok.append(t1)
            state["qt"] = t
            state["kst"] = [fill]
            return ktok, vtok, qtok

        rows = [Counted("s_row0"), Counted("s_row1")]
        bnc = [Counted("s_bn0"), Counted("s_bn1")]
        rowd = [nc.dram_tensor(f"rowd{i}", (16, 128), BF16, kind="Internal").ap() for i in range(2)]
        mi = [0]
        mnf = [None, None]
        mpf = [None, None]

        def max0(qd, ktok, qtok, res):
            g = res["g"] % 2
            last = None
            for u in range(8):
                r, p, q2 = u // 4, 2 * qd + (u // 2) % 2, u % 2
                lhs = Q[:, p, 256 * r + 128 * q2:256 * r + 128 * q2 + 128]
                for c in range(3):
                    i = mi[0] % 2
                    mi[0] += 1
                    t = mm(MB[i][:, :], lhs, kst[:, p, 512 * c:512 * c + 512], MBf[i], ktok[p], qtok[qd])
                    last = MBf[i] = dve.do(lambda u=u, c=c, i=i: V.tensor_reduce(mxp[:, g, u, c:c + 1], MB[i][:, :],
                                                                             AX.X, ALU.max), t, mpf[g])
                    yield
            for r in range(2):
                i = mi[0] % 2
                mi[0] += 1
                for v in range(4):
                    p, q2 = 2 * qd + v // 2, v % 2
                    t = mm(MB[i][:, TAIL * v:TAIL * v + TAIL],
                           Q[:, p, 256 * r + 128 * q2:256 * r + 128 * q2 + 128], kst[:, p, 1536:S2], MBf[i],
                           sig=(v == 3))
                mb = MB[i][:, 0:4 * TAIL].rearrange("p (v n) -> p v n", v=4)
                dve.do(lambda r=r, mb=mb: V.tensor_reduce(mxp[:, g, 4 * r:4 * r + 4, 3], mb[:, :, 0:TMAIN], AX.X,
                                                          ALU.max), t, sig=False)
                last = MBf[i] = dve.do(lambda r=r, mb=mb: V.tensor_reduce(mmx[:, g, 8 * r + 4:8 * r + 8],
                                                                     mb[:, :, TMAIN:TAIL], AX.X, ALU.max), mnf[g])
                yield
            mpf[g] = t = dve.do(lambda: V.tensor_reduce(
                mmx[:, g, :].rearrange("p (r k v) -> p r k v", r=2, k=2)[:, :, 0, :],
                mxp[:, g, :, :].rearrange("p (r v) c -> p r v c", r=2), AX.X, ALU.max), last)
            t = tp(MI[0:16, 0:128], mmx[:, g, :], idn[:, :], t, MIf[0])
            MIf[0] = t = dve.do(lambda: V.tensor_scalar(mneg[:, g, :], MI[0:16, 0:128], -1.0, None, ALU.mult), t, mnf[g])
            yield
            tw_ = bnc[g].start(rowd[g], mneg[:, g, :], t)
            for r in range(2):
                tr = rows[g].start(Q[64 * r + 48:64 * r + 50, 2 * qd:2 * qd + 2, 256 * r:256 * r + 256],
                                   rowd[g][8 * r:8 * r + 8, :].rearrange("(k p t) n -> k p (t n)", k=2, p=2), tw_,
                                   pe.last())
            mnf[g] = tw_
            res["row"] = tr
            yield

        p0f = [None] * 3
        stc = [0]
        pc = [0]

        def attn0(b, qd, rowtok, ktok, vtok, side, rate):
            hist = []
            for kt in range(NKT + 1):
                if kt < NKT:
                    n = 128 if kt < 12 else TAIL
                    i = stc[0] % 2
                    stc[0] += 1
                    for j in range(2):
                        t = mm(ST[i][0:n, 512 * j:512 * j + 512], kst[:, 2 * qd + j, 128 * kt:128 * kt + n],
                               Q[:, 2 * qd + j, :], rowtok, HBf[2 * i], HBf[2 * i + 1], sig=(j == 1))
                    k = pc[0] % 3
                    pc[0] += 1
                    te = act.do(lambda i=i, n=n, k=k: A.activation(P0[k][0:n, :], ST[i][0:n, :], ACT.Exp, scale=0.25),
                                t, p0f[k])
                    HBf[2 * i] = HBf[2 * i + 1] = te
                    hist.append((k, n, te))
                for _ in range(rate):
                    next(side, None)
                if kt >= 1:
                    kp = kt - 1
                    k, n, te = hist[kp]
                    for j in range(4):
                        t = mm(PV[32 * j:32 * j + 32, 0:256], va[0:n, kp, 4 * qd + j, :],
                               P0[k][0:n, 256 * j:256 * j + 256], te, vtok, PVf[0], start=(kp == 0),
                               stop=(kp == NKT - 1), sig=(j == 3))
                    if kp == NKT - 1:
                        for j in range(4):
                            t = mm(PV[32 * j:32 * j + 32, 256:512], vd[0:n, 4 * qd + j, :],
                                   P0[k][0:n, 256 * j:256 * j + 256], sig=(j == 3))
                    p0f[k] = t
            return t

        ocf = [None]
        oTf = [None]

        def out0(b, qd, tpv):
            PVf[0] = t = act.do(lambda: A.copy(oT[:, :], PV[:, :]), tpv, oTf[0])
            yield
            for j in range(4):
                t2 = tp(MI[:, 128 * j:128 * j + 128], oT[:, 128 * j:128 * j + 128], idn[:, :], t, MIf[0], sig=(j == 3))
            oTf[0] = t2
            mv_ = MI[:, :].rearrange("p (g d) -> p g d", d=32)
            tr = dve.do(lambda: V.reciprocal(rec[:, :], mv_[:, :, 16]), t2)
            MIf[0] = tr = dve.do(lambda: V.tensor_tensor(on[:, :, :], mv_[:, :, 0:16],
                                                         rec[:, :].unsqueeze(2).to_broadcast([128, 16, 16]), ALU.mult), tr)
            ov = on[:, :, :].rearrange("p (k t h) d -> p k t (h d)", k=2, t=2)
            t = dve.do(lambda: V.tensor_tensor(oc[:, :, 64 * qd:64 * qd + 64], ov[:, 0, :, :], ov[:, 1, :, :], ALU.add),
                       tr, ocf[0])
            yield
            if qd < 3:
                return
            for dt in range(2):
                for t2 in range(2):
                    tt = tp(MI[:, 256 * dt + 128 * t2:256 * dt + 128 * t2 + 128], oc[:, t2, 128 * dt:128 * dt + 128],
                            idn[:, :], t, MIf[0], sig=(dt + t2 == 2))
            ocf[0] = tt
            MIf[0] = tc = act.do(lambda: A.copy(ocT[:, :, :].rearrange("p c n -> p (c n)"), MI[:, :]), tt)
            yield
            for t2 in range(2):
                for dt in range(2):
                    tt = mm(MI[:, 256 * t2:256 * t2 + 256], ocT[:, dt, 128 * t2:128 * t2 + 128], wo[:, dt, :], tc, t_wo,
                            start=(dt == 0), stop=(dt == 1), sig=(dt == 1))
            yield
            for t2 in range(2):
                MIf[0] = ty = dve.do(lambda t2=t2: V.tensor_tensor(yo[:, :], MI[:, 256 * t2:256 * t2 + 256], bo[:, :],
                                                         ALU.add), tt, t_bo, x_tok[2 * b + t2])
                x_tok[2 * b + t2] = dve.do(lambda t2=t2: V.scalar_tensor_tensor(
                    out=x_sb[:, 2 * b + t2, :], in0=yo[:, :], scalar=tg[:, 0:1], in1=x_sb[:, 2 * b + t2, :],
                    op0=ALU.mult, op1=ALU.add), ty, t_tg)
                if t2 == 0:
                    dve.wait(x_tok[2 * b])
            yield

        def chain(*gens):
            for g in gens:
                if g is not None:
                    yield from g

        gcount = 0
        pending = None
        for b in range(B):
            ktok, vtok, qtok = prep(b)
            res = {"g": gcount}
            gcount += 1
            for _ in max0(0, ktok, qtok, res):
                pass
            for qd in range(4):
                nxt = {"g": gcount}
                mg = None
                if qd < 3:
                    gcount += 1
                    mg = max0(qd + 1, ktok, qtok, nxt)
                side = chain(pending, mg)
                tpv = attn0(b, qd, res["row"], ktok, vtok, side, 3)
                for _ in side:
                    pass
                pending = out0(b, qd, tpv)
                next(pending)
                res = nxt
            state["kst"], state["Q"], state["va"] = [tpv], [tpv], tpv
        for _ in pending:
            pass
        L0.close()
        barrier()

        F0 = ExitStack()
        w1 = sb("w1", [128, 2, 2, 128], F32, F0)
        w2 = sb("w2", [128, D], F32, F0)
        wg_ = sb("wg_", [128, 2, E], F32, F0)
        wd_ = sb("wd_", [128, 2, 128], F32, F0)
        wu_ = sb("wu_", [128, D], F32, F0)
        be = sb("be", [128, E], F32, F0)
        rwf = sb("rwf", [128, 2, E * 128], F32, F0)
        rwh = sb("rwh", [128, 2, E * 128], BF16, F0)
        rwl = sb("rwl", [128, 2, E * 128], BF16, F0)
        rw2 = sb("rw2", [128, E, 64], F32, F0)
        sel = sb("sel", [128, E, 128], BF16, F0)
        amk = sb("amk", [128, 12], F32, F0)
        pr = sb("pr", [128, NT, E], F32, F0)
        pb = sb("pb", [128, NT, E], F32, F0)
        pw = sb("pw", [128, NT, E], F32, F0)
        pw3 = sb("pw3", [128, NT, 4, E], F32, F0)
        m8 = sb("m8", [128, NT, 8], F32, F0)
        sm = sb("sm", [128, NT], F32, F0)
        smr = sb("smr", [128, NT], F32, F0)
        wT = sb("wT", [128, B * S], BF16, F0)
        xlX = sb("xlX", [128, 512], F32, F0)
        xlH = sb("xlH", [128, 512], BF16, F0)
        xl = sb("xl", [128, 2, 512], BF16, F0)
        rr = sb("rr", [128, 2, 512], F32, F0)
        r2 = sb("r2", [128, 2, 512], F32, F0)
        tt_ = sb("tt_", [128, 2, 512], F32, F0)
        hh = sb("hh", [128, 2, 512], F32, F0)
        hsh = sb("hsh", [128, 512], F32, F0)
        accT = sb("accT", [128, 512], F32, F0)

        l_w1 = load(w1[:, :, 0, :], a["sw1T"]), load(w1[:, :, 1, :], a["swgT"])
        l_wd = load(wd_[:, :, :], a["WdT"])
        l_wg = load(wg_[:, :, :], a["WgT"])
        l_be = load(be[:, :], a["bias_e"].partition_broadcast(128))
        l_am = load(amk[:, :], a["prm"])
        l_rw = load(rwf[:, 0, :], a["rw1T"]), load(rwf[:, 1, :], a["rwgT"])
        l_sel = load(xlX[:, 0:128], a["seld"])
        l_r2 = load(rw2[:, :, :], a["rw2T"])
        l_w2 = load(w2[:, :], a["sw2T"])
        l_wu = load(wu_[:, :], a["WuT"])

        xnt = layernorm_T()
        bf = [None] * 8
        bf[4], bf[5] = MBf
        t_rh = act.do(lambda: A.copy(rwh[:, :, :], rwf[:, :, :]), *l_rw)
        t_rl = dve.do(lambda: V.tensor_tensor(rwl[:, :, :], rwf[:, :, :], rwh[:, :, :], ALU.subtract), t_rh)
        t_sel = dve.do(lambda: V.tensor_copy(sel[:, :, :], xlX[:, 0:E].unsqueeze(2).to_broadcast([128, E, 128])), l_sel)
        for i in range(NT):
            for c in range(2):
                t = mm(BANKS[6][:, 16 * i:16 * i + 16], xnT[:, c, 128 * i:128 * i + 128], wg_[:, c, :], l_wg, xnt,
                       start=(c == 0), stop=(c == 1), sig=(c == 1 and i == NT - 1))
        lg = BANKS[6][:, 0:NT * E].rearrange("p (t e) -> p t e", e=E)
        tpr = act.do(lambda: A.activation(pr[:, :, :], lg, ACT.Sigmoid), t)
        bf[6] = tpr
        t = dve.do(lambda: V.tensor_tensor(pb[:, :, :], pr[:, :, :], be[:, :].unsqueeze(1).to_broadcast([128, NT, E]),
                                           ALU.add), tpr, l_be)
        for i in range(NT):
            t1 = dve.do(lambda i=i: V.max(m8[:, i, :], pb[:, i, :]), t)
            t2 = dve.do(lambda i=i: V.match_replace(pw[:, i, :], m8[:, i, :], pb[:, i, :], -3e38), t1)
        t = dve.do(lambda: V.tensor_tensor(pb[:, :, :], pb[:, :, :], pw[:, :, :], ALU.not_equal), t2)
        t = dve.do(lambda: V.tensor_tensor(pr[:, :, :], pb[:, :, :], pr[:, :, :], ALU.mult), t)
        t = dve.do(lambda: V.tensor_reduce(sm[:, :], pr[:, :, :], AX.X, ALU.add), t)
        t = dve.do(lambda: V.reciprocal(smr[:, :], sm[:, :]), t)
        t = dve.do(lambda: V.scalar_tensor_tensor(out=pw[:, :, :], in0=pr[:, :, :], scalar=2.5,
                                                  in1=smr[:, :].unsqueeze(2).to_broadcast([128, NT, E]),
                                                  op0=ALU.mult, op1=ALU.mult), t)
        t0 = dve.do(lambda: V.memset(pw3[:, :, 3, :], 0.0))
        hb = sb("hb", [128, 2, NT, E], BF16, F0)
        t1 = dve.do(lambda: V.tensor_copy(hb[:, 0, :, :], pw[:, :, :]), t)
        t = dve.do(lambda: V.tensor_copy(pw3[:, :, 0, :], hb[:, 0, :, :]), t1)
        t = dve.do(lambda: V.tensor_tensor(pw[:, :, :], pw[:, :, :], pw3[:, :, 0, :], ALU.subtract), t)
        t = dve.do(lambda: V.tensor_copy(hb[:, 1, :, :], pw[:, :, :]), t)
        t = dve.do(lambda: V.tensor_copy(pw3[:, :, 1, :], hb[:, 1, :, :]), t)
        t = dve.do(lambda: V.tensor_tensor(pw3[:, :, 2, :], pw[:, :, :], pw3[:, :, 1, :], ALU.subtract), t)
        t_wz = pool.do(lambda: G.memset(wT[:, :], 0.0))
        for half in range(2):
            for i in range(4):
                tk = 4 * half + i
                tt = tp(MI[0:64, 128 * i:128 * i + 128], pw3[:, tk, :, :].rearrange("p a e -> p (a e)"), idn[:, :], t, t0,
                        bf[7], MIf[0], sig=(i == 3))
            bf[7] = t_wT = act.do(lambda half=half: A.copy(wT[0:64, 512 * half:512 * half + 512], MI[0:64, :]), tt, t_wz)
        HX = {"rr": [None, None], "hh": [None, None]}
        xlf = [None]
        hsf = [None]
        acf = [None]
        for ch in range(2):
            tok = slice(512 * ch, 512 * ch + 512)
            for m in range(2):
                for c in range(2):
                    t = mm(BANKS[m], w1[:, c, m, :], xnT[:, c, tok], *l_w1, bf[m], start=(c == 0), stop=(c == 1),
                           sig=(c == 1))
            tr = act.do(lambda: A.activation(rr[:, 0, :], BANKS[1], ACT.Relu), t, HX["rr"][0])
            bf[1] = tr
            bf[0] = t1 = dve.do(lambda: V.tensor_tensor(tt_[:, 0, :], BANKS[0], rr[:, 0, :], ALU.mult), tr)
            t_hs = dve.do(lambda: V.tensor_tensor(hsh[:, :], tt_[:, 0, :], rr[:, 0, :], ALU.mult), t1, hsf[0])
            HX["rr"][0] = t_hs
            for c in range(2):
                t = mm(BANKS[2], wd_[:, c, :], xnT[:, c, tok], l_wd, bf[2], start=(c == 0), stop=(c == 1), sig=(c == 1))
            bf[2] = t = act.do(lambda: A.copy(xlX[:, :], BANKS[2]), t, t_sel, xlf[0])
            t = dve.do(lambda: V.tensor_copy(xlH[:, :], xlX[:, :]), t)
            t_xl = xlf[0] = dve.do(lambda ch=ch: V.scalar_tensor_tensor(
                out=xl[:, ch, :], in0=xlH[:, :], scalar=amk[:, 9:10], in1=xlX[:, :], op0=ALU.mult, op1=ALU.add), t, l_am)
            down = []
            for e in range(E + 1):
                if e < E:
                    k = e % 2
                    g1, g2, g3 = 3 * k, 3 * k + 1, 3 * k + 2
                    for m, gb in ((1, g2), (0, g1)):
                        mm(BANKS[gb], rwh[:, m, 128 * e:128 * e + 128], xl[:, ch, :], t_xl, t_rh, bf[gb], start=True,
                           stop=False, sig=False)
                        t = mm(BANKS[gb], rwl[:, m, 128 * e:128 * e + 128], xl[:, ch, :], t_rl, start=False, stop=True)
                        if m == 1:
                            tg_ = t
                    tb = mm(BANKS[g3], sel[:, e, :], wT[:, tok], t_sel, t_wT, t_wz, bf[g3])
                    bf[g2] = t1 = act.do(lambda k=k, g2=g2: A.activation(rr[:, k, :], BANKS[g2], ACT.Relu), tg_,
                                         HX["rr"][k])
                    t2 = act.do(lambda k=k: A.activation(r2[:, k, :], rr[:, k, :], ACT.Square), t1)
                    bf[g1] = t3 = dve.do(lambda k=k, g1=g1: V.tensor_tensor(tt_[:, k, :], BANKS[g1], r2[:, k, :],
                                                                       ALU.mult), t2, t)
                    HX["rr"][k] = t3
                    bf[g3] = t4 = dve.do(lambda k=k, g3=g3: V.tensor_tensor(hh[:, k, :], BANKS[g3], tt_[:, k, :],
                                                                       ALU.mult), t3, tb, HX["hh"][k])
                    down.append(t4)
                if e >= 1:
                    ep, k = e - 1, (e - 1) % 2
                    HX["hh"][k] = mm(BANKS[6][0:64, :], rw2[:, ep, :], hh[:, k, :], down[ep], l_r2, bf[6],
                                     start=(ep == 0), stop=(ep == E - 1))
            tz = act.do(lambda: A.copy(accT[0:64, :], BANKS[6][0:64, :]), HX["hh"][(E - 1) % 2], acf[0])
            bf[6] = tz
            for i in range(4):
                tk = 4 * ch + i
                o = BANKS[7][:, 256 * (i % 2):256 * (i % 2) + 256]
                mm(o, hsh[:, 128 * i:128 * i + 128], w2[:, :], t_hs, l_w2, bf[7], start=True, stop=False, sig=False)
                t = mm(o, accT[0:64, 128 * i:128 * i + 128], wu_[0:64, :], tz, l_wu, start=False, stop=True)
                bf[7] = x_tok[tk] = dve.do(lambda o=o, tk=tk: V.scalar_tensor_tensor(
                    out=x_sb[:, tk, :], in0=o, scalar=tg[:, 2:3], in1=x_sb[:, tk, :], op0=ALU.mult, op1=ALU.add),
                    t, x_tok[tk])
            hsf[0] = acf[0] = t
        MBf[0], MBf[1] = bf[4], bf[5]
        F0.close()
        barrier()

        L1 = ExitStack()
        M1 = sb("M1", [128, 2, H, 128], F32, L1)
        N1 = sb("N1", [128, H, D], F32, L1)
        cth = sb("cth", [128, B, S2], BF16, L1)
        ctl = sb("ctl", [128, B, S2], BF16, L1)
        ck = sb("ck", [128, B, NKT, 128], F32, L1)
        mcb = sb("mcb", [128, B, NKT], F32, L1)
        mc8 = sb("mc8", [128, B, 12], U8, L1)
        mt8 = sb("mt8", [128, B], U8, L1)
        mb8 = sb("mb8", [128, S2], U8, L1)
        mbc = sb("mbc", [128, 2, S2], F32, L1)
        W1 = ExitStack()
        wq1 = sb("wq1", [128, H, D], F32, W1)
        wk1 = sb("wk1", [128, 8, 128], F32, W1)
        wv1 = sb("wv1", [128, 8, 128], F32, W1)
        wo1 = sb("wo1", [128, H, D], F32, W1)
        ctf = sb("ctf", [128, 2, S2], F32, W1)
        l_wq = load(wq1[:, :, :], a["wqT1"])
        l_wk = load(wk1[:, :, :], a["wkT1"])
        l_cf = [load(ctf[:, b, :], a["ctxT"][b]) for b in range(2)]
        l_wv = load(wv1[:, :, :], a["wvT1"])
        l_wo = load(wo1[:, :, :], a["wo1"])
        l_mc = load(mc8[:, :, :], a["mcol"])
        l_mt = load(mt8[0:TAIL, :], a["mtail"])
        l_ck = []
        for b in range(B):
            l_ck.append([load(ck[:, b, 0:12, :], a["ctxk"][b, 0:1536, :].rearrange("(k p) d -> p k d", p=128)),
                         load(ck[0:TAIL, b, 12, :], a["ctxk"][b, 1536:S2, :])])
        dve.do(lambda: V.tensor_scalar(mcb[:, :, 0:12], mc8[:, :, :], 1.0, NEG, ALU.subtract, ALU.mult), l_mc)
        dve.do(lambda: V.tensor_scalar(mcb[0:TAIL, :, 12], mt8[0:TAIL, :], 1.0, NEG, ALU.subtract, ALU.mult), l_mt)
        xnt = layernorm_T()
        bf = [None] * 8
        bf[4], bf[5] = MBf
        t_ct = []
        for b in range(B):
            k = b % 2
            if b >= 2:
                l_cf.append(load(ctf[:, k, :], a["ctxT"][b], t_ct[b - 2]))
            th = act.do(lambda b=b, k=k: A.copy(cth[:, b, :], ctf[:, k, :]), l_cf[b])
            t_ct.append(pool.do(lambda b=b, k=k: G.tensor_tensor(ctl[:, b, :], ctf[:, k, :], cth[:, b, :], ALU.subtract),
                                th))
        evs = []
        for h in range(H):
            i = h % 4
            for dt in range(2):
                mm(BANKS[i][:, 128 * dt:128 * dt + 128], wq1[:, h, 128 * dt:128 * dt + 128], wk1[:, h // 2, :], l_wq,
                   l_wk, bf[i], sig=False)
            t = mm(BANKS[i][:, 256:512], wv1[:, h // 2, :], wo1[:, h, :], l_wv, l_wo)
            bf[i] = dve.do(lambda i=i, h=h: V.tensor_copy(M1[:, :, h, :],
                                                     BANKS[i][:, 0:256].rearrange("p (c n) -> p c n", c=2)), t)
            bf[i] = dve.do(lambda i=i, h=h: V.tensor_copy(N1[:, h, :], BANKS[i][:, 256:512]))
        t_MN = bf[i]
        W1.close()
        barrier()
        ones = sb("ones", [128, 128], F32, L1)
        onb = sb("onb", [128, 128], BF16, L1)
        mrw = sb("mrw", [128, 2, 512], BF16, L1)
        mng = sb("mng", [4, 2, 128], BF16, L1)
        qh = sb("qh", [128, 3, 512], BF16, L1)
        ql = sb("ql", [128, 3, 512], BF16, L1)
        junk = sb("junk", [128, 512], BF16, L1)
        mtl = sb("mtl", [128, 4, TAIL], F32, L1)
        mp1 = sb("mp1", [128, 4, 4], F32, L1)
        mm1 = sb("mm1", [128, 4], F32, L1)
        P1 = [sb(f"P1_{i}", [128, 512], F32, L1) for i in range(4)]
        acc = sb("acc", [128, 2, 512], F32, L1)
        dn = sb("dn", [128, 512], F32, L1)
        rc = sb("rc", [128, 512], F32, L1)
        oN = sb("oN", [128, H, S], F32, L1)
        t_on = pool.do(lambda: G.memset(ones[:, :], 1.0))
        t_ob = pool.do(lambda: G.memset(onb[:, :], 1.0))
        t_mr0 = pool.do(lambda: G.memset(mrw[:, :, :], 0.0))

        S1, PV1, DN1, PJ = [BANKS[0], BANKS[1]], [BANKS[2], BANKS[3]], BANKS[6], BANKS[7]
        S1f, PV1f, DN1f, PJf = [None, None], [None, None], [None], [None]
        MBf = [None, None]
        mask_tok = {}
        l_m8 = [None]
        NG = B * 8
        qf = [None] * 3
        qt1 = {}
        row1 = [Counted("s_r1a"), Counted("s_r1b")]
        mrf = [None, None]
        mngf = [None, None]
        rowtok = {}

        def mask_load(b):
            t = load(mb8[:, :], a["mrow"][b:b + 1, :].partition_broadcast(128) if False else a["mrow"][b].partition_broadcast(128), l_m8[0])
            l_m8[0] = mask_tok[b] = dve.do(lambda: V.tensor_scalar(mbc[:, b % 2, :], mb8[:, :], 1.0, NEG, ALU.subtract,
                                                                   ALU.mult), t, mask_tok.get(("free", b)))

        def qproj(g):
            b, r = g // 8, g % 3
            for j in range(2):
                h = 2 * (g % 8) + j
                for dt in range(2):
                    t = mm(PJ[:, 256 * j:256 * j + 256], M1[:, dt, h, :], xnT[:, dt, S * b:S * b + S], PJf[0],
                           start=(dt == 0), stop=(dt == 1), sig=(dt == 1))
                yield
            t1 = act.do(lambda: A.copy(qh[:, r, :], PJ), t, qf[r])
            PJf[0] = t2 = dve.do(lambda: V.tensor_tensor(ql[:, r, :], PJ, qh[:, r, :], ALU.subtract), t1)
            qt1[g] = t2
            yield

        mpc = [None]
        jk = [None]

        def max1(g):
            b, r, par = g // 8, g % 3, g % 2
            if g % 8 == 0:
                mask_load(b)
            last = None
            for u in range(4):
                lhs = qh[:, r, 128 * u:128 * u + 128]
                for c in range(3):
                    i = mi[0] % 2
                    mi[0] += 1
                    t = mm(MB[i][:, :], lhs, cth[:, b, 512 * c:512 * c + 512], MBf[i], qt1[g])
                    last = MBf[i] = dve.do(lambda u=u, c=c, i=i: V.tensor_tensor_reduce(
                        out=junk[:, :], in0=MB[i][:, :], in1=mbc[:, b % 2, 512 * c:512 * c + 512], scale=1.0,
                        scalar=-3e38, op0=ALU.add, op1=ALU.max, accum_out=mp1[:, u, c:c + 1]), t, mask_tok[b], mpc[0],
                        jk[0])
                    jk[0] = last
                    yield
            i = mi[0] % 2
            mi[0] += 1
            for u in range(4):
                t = mm(MB[i][:, TAIL * u:TAIL * u + TAIL], qh[:, r, 128 * u:128 * u + 128], cth[:, b, 1536:S2], MBf[i],
                       sig=(u == 3))
            MBf[i] = t = dve.do(lambda: V.tensor_tensor(
                mtl[:, :, :], MB[i][:, 0:4 * TAIL].rearrange("p (u n) -> p u n", u=4),
                mbc[:, b % 2, 1536:S2].unsqueeze(1).to_broadcast([128, 4, TAIL]), ALU.add), t)
            t = dve.do(lambda: V.tensor_reduce(mp1[:, :, 3], mtl[:, :, :], AX.X, ALU.max), t)
            if g % 8 == 7:
                mask_tok[("free", b + 2)] = t
            mpc[0] = t = dve.do(lambda: V.tensor_reduce(mm1[:, :], mp1[:, :, :], AX.X, ALU.max), t, last)
            t = tp(PJ[0:4, 0:128], mm1[:, :], idn[:, :], t, PJf[0])
            PJf[0] = t = dve.do(lambda: V.tensor_scalar(mng[:, par, :], PJ[0:4, 0:128], -1e20, -1.0, ALU.max, ALU.mult), t,
                                mngf[par])
            yield
            mngf[par] = tw_ = bnc[par].start(rowd[par][0:4, :], mng[:, par, :], t)
            rowtok[g] = row1[par].start(mrw[0:1, par, :], rowd[par][0:4, :].rearrange("(o u) n -> o (u n)", o=1), tw_,
                                        mrf[par], t_mr0)
            yield

        p1f = [None] * 4
        accf = [None, None]
        p1c = [0]

        def attn1(g, side, rate):
            b, r, par = g // 8, g % 3, g % 2
            hist = []
            ta = None
            for kt in range(NKT + 1):
                if kt < NKT:
                    n = 128 if kt < 12 else TAIL
                    i = kt % 2 if False else stc[0] % 2
                    stc[0] += 1
                    ks = slice(128 * kt, 128 * kt + n)
                    o = S1[i][0:n, :]
                    mm(o, cth[:, b, ks], qh[:, r, :], S1f[i], qt1[g], start=True, stop=False, sig=False)
                    mm(o, cth[:, b, ks], ql[:, r, :], start=False, stop=False, sig=False)
                    mm(o, ctl[:, b, ks], qh[:, r, :], start=False, stop=False, sig=False)
                    t = mm(o, onb[:, 0:n], mrw[:, par, :], rowtok[g], start=False, stop=True)
                    k = p1c[0] % 4
                    p1c[0] += 1
                    S1f[i] = te = act.do(lambda k=k, n=n, o=o, kt=kt: A.activation(
                        P1[k][0:n, :], o, ACT.Exp, scale=SCALE1, bias=mcb[0:n, b, kt:kt + 1]), t, p1f[k])
                    hist.append((k, n, te, t))
                    if kt == 1:
                        k0 = hist[0][0]
                        ta = pool.do(lambda k=k, k0=k0: G.tensor_tensor(acc[:, par, :], P1[k0][:, :], P1[k][:, :],
                                                                        ALU.add), te, hist[0][2], accf[par])
                        p1f[k0] = [ta]
                    elif kt > 1:
                        ta = pool.do(lambda k=k, n=n: G.tensor_tensor(acc[0:n, par, :], acc[0:n, par, :], P1[k][0:n, :],
                                                                      ALU.add), te, ta)
                    padd = ta
                    hist[-1] = (k, n, te, padd)
                for _ in range(rate):
                    next(side, None)
                if kt >= 1:
                    kp = kt - 1
                    k, n, te, padd = hist[kp]
                    tpv = mm(PV1[par], ck[0:n, b, kp, :], P1[k][0:n, :], te, l_ck[b], PV1f[par], start=(kp == 0),
                             stop=(kp == NKT - 1))
                    p1f[k] = [tpv, padd if kp else ta]
            qf[r] = mrf[par] = hist and (pe.sem, pe.n)
            return tpv, ta

        oNf = [None]

        def out1(g, tpv, ta):
            b, par = g // 8, g % 2
            t = accf[par] = mm(DN1, ones[:, :], acc[:, par, :], ta, DN1f[0])
            yield
            DN1f[0] = t = dve.do(lambda: V.tensor_scalar(dn[:, :], DN1, 1e-30, None, ALU.max), t)
            t = dve.do(lambda: V.reciprocal(rc[:, :], dn[:, :]), t)
            h = 2 * (g % 8)
            PV1f[par] = t = dve.do(lambda: V.tensor_tensor(oN[:, h:h + 2, :].rearrange("p h n -> p (h n)"), PV1[par],
                                                           rc[:, :], ALU.mult), t, tpv, oNf[0])
            yield
            if g % 8 < 7:
                return
            for t2 in range(2):
                for h in range(H):
                    tt = mm(PJ[:, 0:256], oN[:, h, 128 * t2:128 * t2 + 128], N1[:, h, :], t, PJf[0], start=(h == 0),
                            stop=(h == H - 1), sig=(h == H - 1))
                i = 2 * b + t2
                PJf[0] = x_tok[i] = dve.do(lambda i=i: V.scalar_tensor_tensor(
                    out=x_sb[:, i, :], in0=PJ[:, 0:256], scalar=tg[:, 1:2], in1=x_sb[:, i, :], op0=ALU.mult,
                    op1=ALU.add), tt, x_tok[i])
                yield
            oNf[0] = tt

        for g in range(2):
            for _ in qproj(g):
                pass
        for _ in max1(0):
            pass
        pend = None
        for g in range(NG):
            side = chain(pend, max1(g + 1) if g + 1 < NG else None, qproj(g + 2) if g + 2 < NG else None)
            r_ = attn1(g, side, 2)
            for _ in side:
                pass
            pend = out1(g, *r_)
        for _ in pend:
            pass
        L1.close()
        barrier()

        wr = [sb(f"wr{i}", [128, 2048], F32) for i in range(3)]
        tw = [sb(f"tw{i}", [128, 2048], BF16) for i in range(3)]
        qa = sb("qa", [128, 2048], F32)
        qb_ = sb("qb_", [128, 2048], F32)
        asum = sb("asum", [128, 3], F32)
        sc = sb("sc", [128, 3], F32)
        hs_ = sb("hs_", [128, 3], F32)
        on1 = sb("on1", [128, 128], F32)
        xh = sb("xh", [128, 2, B * S], BF16)
        xlo = sb("xlo", [128, 2, B * S], BF16)
        sg = sb("sg", [128, 2, 512], F32)
        u1 = sb("u1", [128, 2, 512], F32)
        hf = sb("hf", [128, 2, 512], F32)
        hhi = sb("hhi", [128, 8, 512], BF16)
        hlo = sb("hlo", [128, 8, 512], BF16)
        fin = sb("fin", [128, NT, D], F32)
        gs = sb("gs", [128, 1], F32)
        l3 = [load(wr[0][:, :], a["wup"]), load(wr[1][:, :], a["wgate"]), load(wr[2][:, :], a["wdown"])]
        t_o1 = pool.do(lambda: G.memset(on1[:, :], 1.0 / (1024 * 256)))
        for i in range(3):
            t = dve.do(lambda i=i: V.tensor_reduce(asum[:, i:i + 1], wr[i][:, :], AX.X, ALU.add,
                                              apply_absolute_value=True), l3[i])
        t = mm(BANKS[7][:, 0:3], on1[:, :], asum[:, :], t, t_o1)
        t_sc = dve.do(lambda: V.tensor_scalar(sc[:, :], BANKS[7][:, 0:3], 1e-8, None, ALU.add), t)
        t_hp = dve.do(lambda: V.tensor_scalar(hs_[:, :], sc[:, :], 0.5, None, ALU.mult), t_sc)
        t_qb = None
        t_tw = []
        sc2 = sb("sc2", [128, 3], F32)
        t_hn = dve.do(lambda: V.tensor_scalar(sc2[:, :], sc[:, :], -0.5, None, ALU.mult), t_sc)
        for i in range(3):
            t1 = dve.do(lambda i=i: V.tensor_scalar(qa[:, :], wr[i][:, :], hs_[:, i:i + 1], None, ALU.is_gt), t_hp, t_qb)
            t2 = dve.do(lambda i=i: V.tensor_scalar(qb_[:, :], wr[i][:, :], sc2[:, i:i + 1], None, ALU.is_lt), t_hn, t_qb)
            t_qb = pool.do(lambda i=i: G.tensor_tensor(tw[i][:, :], qa[:, :], qb_[:, :], ALU.subtract), t1, t2)
            t_tw.append(t_qb)
        xnt = layernorm_T()
        bf = [None] * 8
        bf[4], bf[5] = MBf
        t_xh = act.do(lambda: A.copy(xh[:, :, :], xnT[:, :, :]), xnt)
        t_xl = dve.do(lambda: V.tensor_tensor(xlo[:, :, :], xnT[:, :, :], xh[:, :, :], ALU.subtract), t_xh)
        t_gs = dve.do(lambda: V.tensor_tensor(gs[:, :], tg[:, 3:4], sc[:, 2:3], ALU.mult), t_sc)
        up = tw[0][:, :].rearrange("p (c e) -> p c e", c=2)
        ga = tw[1][:, :].rearrange("p (c e) -> p c e", c=2)
        dw = tw[2][:, :].rearrange("p (e d) -> p e d", e=8)
        f = {"sg": [None, None], "hf": [None, None], "h": None}
        outd = out.rearrange("b (t p) d -> p (b t) d", p=128)
        stores = []
        for ch in range(2):
            tok = slice(512 * ch, 512 * ch + 512)
            for e in range(8):
                k = e % 2
                b0, b1 = 2 * k, 2 * k + 1
                for w, bk, tw_ in ((up, b0, t_tw[0]), (ga, b1, t_tw[1])):
                    for c in range(2):
                        es = slice(128 * e, 128 * e + 128)
                        mm(BANKS[bk], w[:, c, es], xh[:, c, tok], tw_, t_xh, bf[bk], start=(c == 0), stop=False,
                           sig=False)
                        t = mm(BANKS[bk], w[:, c, es], xlo[:, c, tok], t_xl, start=False, stop=(c == 1), sig=(c == 1))
                    if w is up:
                        tu = t
                t1 = act.do(lambda k=k, b0=b0: A.activation(sg[:, k, :], BANKS[b0], ACT.Sigmoid, scale=sc[:, 0:1]), tu,
                            f["sg"][k])
                bf[b0] = t2 = dve.do(lambda k=k, b0=b0: V.scalar_tensor_tensor(
                    out=u1[:, k, :], in0=BANKS[b0], scalar=sc[:, 0:1], in1=sg[:, k, :], op0=ALU.mult, op1=ALU.mult), t1)
                bf[b1] = t3 = dve.do(lambda k=k, b1=b1: V.scalar_tensor_tensor(
                    out=hf[:, k, :], in0=BANKS[b1], scalar=sc[:, 1:2], in1=u1[:, k, :], op0=ALU.mult, op1=ALU.mult),
                    t2, t, f["hf"][k])
                f["sg"][k] = t3
                t4 = act.do(lambda e=e, k=k: A.copy(hhi[:, e, :], hf[:, k, :]), t3, f["h"])
                f["hf"][k] = t_h = dve.do(lambda e=e, k=k: V.tensor_tensor(hlo[:, e, :], hf[:, k, :], hhi[:, e, :],
                                                                      ALU.subtract), t4)
            for i in range(4):
                tk = 4 * ch + i
                bk = 6 + i % 2
                for e in range(8):
                    for part in (hhi, hlo):
                        t = mm(BANKS[bk][:, 0:256], part[:, e, 128 * i:128 * i + 128], dw[:, e, :], t_h, t_tw[2], bf[bk],
                               start=(e == 0 and part is hhi), stop=(e == 7 and part is hlo),
                               sig=(e == 7 and part is hlo))
                bf[bk] = tf = dve.do(lambda tk=tk, bk=bk: V.scalar_tensor_tensor(
                    out=fin[:, tk, :], in0=BANKS[bk][:, 0:256], scalar=gs[:, 0:1], in1=x_sb[:, tk, :], op0=ALU.mult,
                    op1=ALU.add), t, t_gs)
                stores.append(load(outd[:, tk, :], fin[:, tk, :], tf))
            f["h"] = t
        sp.wait(stores)
        barrier()


def layout(i):
    import numpy as np

    def f(n):
        return np.asarray(i[n])

    def kt(w, c=2):
        return w.reshape(c, 128, -1).transpose(1, 0, 2)

    z, o = np.zeros, np.ones
    g = "L0_xattn_"
    wm = np.concatenate([f(g + "Wk"), f(g + "Wv")], 1).reshape(128, 16, 2, 16)
    bm = np.concatenate([f(g + "bk"), f(g + "bv")], 0).reshape(16, 2, 16)
    wd, bd = f(g + "Wkv_dca"), f(g + "bkv_dca")
    bc = lambda v: np.broadcast_to(v.reshape(1, 1, 256), (128, 1, 256))
    wk0 = np.concatenate([wm[:, :, 0].reshape(128, 1, 256), wd[:, None, 0:256], kt(f(g + "Wq")),
                          bc(bm[:, 0]), bc(bd[0:256]), bc(f(g + "bq"))], 1)
    wv0 = np.concatenate([wm[:, :, 1].reshape(128, 1, 256), wd[:, None, 256:512], bc(bm[:, 1]), bc(bd[256:512])], 1)

    def col(w):
        return np.tile(w, 8)

    fz = z(128, np.float32)
    om, od = fz.copy(), fz.copy()
    om[[48, 112]] = 1
    od[[49, 113]] = 1
    rsel = z((128, 4, 4, 128), np.float32)
    for p in range(4):
        for r in range(2):
            for d in range(16):
                for m, slots in enumerate(((0, 2), (1,), (0, 1), (2,))):
                    for s_ in slots:
                        rsel[16 * (2 * p + r) + d, p, m, 64 * r + 16 * s_ + d] = 1
    ind = (np.arange(128) >= TMAIN).astype(np.float32)
    ahl = np.concatenate([z(64, np.float32), -o(64, np.float32)])
    prm = np.stack([col(f(g + "kn_w")), col(f(g + "kn_b")), col(f(g + "kn_dca_w")), col(f(g + "kn_dca_b")),
                    col(f(g + "qn_w")), col(f(g + "qn_b")), fz, fz, ind, ahl, om, od], 1)
    seld = z((128, 128), np.float32)
    for e in range(16):
        for part in range(3):
            seld[16 * part + e, e] = 1
    ctx = f("ctx_1024")
    mask = f("mask_BxS2_bf1").view(np.uint8)
    mcol = mask[:, :1536].reshape(4, 12, 128).transpose(2, 0, 1)
    h = "L0_ffn_"
    dup = lambda w: np.concatenate([w, w], 0)
    wdT = f(h + "Wdown").T
    j = "L1_xattn_"
    out = {
        "x": f("x").reshape(1024, 256), "ctxT": ctx.transpose(0, 2, 1), "ctxk": ctx, "mrow": mask, "mcol": mcol, "mtail": mask[:, 1536:].T,
        "gates": np.concatenate([f("g_xattn"), f("g_ffn")]),
        "wk0": wk0, "wv0": wv0, "wo0": kt(f(g + "Wo")), "bo0": f(g + "bo"), "prm": prm,
        "sw1T": kt(f(h + "sw1").T), "swgT": kt(f(h + "swg").T), "sw2T": f(h + "sw2").T,
        "rw1T": dup(f(h + "rw1").transpose(2, 0, 1).reshape(64, 2048)),
        "rwgT": dup(f(h + "rwg").transpose(2, 0, 1).reshape(64, 2048)),
        "rw2T": f(h + "rw2").transpose(2, 0, 1), "WgT": kt(f(h + "Wg").T),
        "WdT": kt(np.concatenate([wdT, wdT], 1)), "WuT": dup(f(h + "Wup").T), "bias_e": f(h + "biases"),
        "wqT1": f(j + "Wq").reshape(256, 16, 128).transpose(2, 1, 0),
        "wkT1": f(j + "Wk").reshape(128, 8, 128).transpose(2, 1, 0),
        "wvT1": f(j + "Wv").reshape(128, 8, 128).transpose(2, 1, 0),
        "wo1": f(j + "Wo").reshape(16, 128, 256).transpose(1, 0, 2),
        "wup": kt(f("L1_ffn_W_up").T).reshape(128, 2048), "wgate": kt(f("L1_ffn_W_gate").T).reshape(128, 2048),
        "wdown": kt(f("L1_ffn_W_down").T, 8).reshape(128, 2048),
        "ident": np.eye(128, dtype=np.float32), "seld": seld, "rsel": rsel.reshape(128, 16, 128),
    }
    return {k: np.ascontiguousarray(v) for k, v in out.items()}


def kernel(**inputs):
    import concourse.bacc as _bacc
    from concourse import mybir as _mybir
    from concourse.bass_utils import run_bass_kernel_spmd as _run

    nc = _bacc.Bacc("TRN2", target_bir_lowering=False, num_devices=1)
    laid = layout(inputs)
    arrays, aps = {}, {}
    for name in INS:
        v = laid[name]
        arrays[f"in_{name}"] = v
        aps[name] = nc.dram_tensor(f"in_{name}", v.shape, _mybir.dt.from_np(v.dtype), kind="ExternalInput").ap()
    out = nc.dram_tensor("out_0", (4, 256, 256), _mybir.dt.float32, kind="ExternalOutput").ap()
    program(nc, aps, out)
    r = _run(nc, [arrays], core_ids=[0])
    return r.results[0]["out_0"]
```

```python
from contextlib import ExitStack

import concourse.bass as bass
from concourse import mybir

F32 = mybir.dt.float32
BF16 = mybir.dt.bfloat16
U8 = mybir.dt.uint8
ALU = mybir.AluOpType
ACT = mybir.ActivationFunctionType
AX = mybir.AxisListType

B, S, D, KD = 4, 256, 256, 128
PR0 = [1, 1, 1, 2]
S2, NDCA = 1601, 16
NMAIN = S2 - NDCA
NKT = 13
TAIL = S2 - 12 * 128
TMAIN = NMAIN - 12 * 128
H = 16
NT = B * S // 128
E = 16
SCALE1 = 1.0 / float(128.0 ** 0.5)
NEG = 1e30
INS = ["x", "ctxT", "ctxk", "mrow", "mcol", "mtail", "gates", "wk0", "wv0", "wo0", "bo0", "prm",
       "sw1T", "swgT", "sw2T", "rw1T", "rwgT", "rw2T", "WgT", "WdT", "WuT", "bias_e",
       "wqT1", "wkT1", "wvT1", "wo1", "wup", "wgate", "wdown", "ident", "seld", "rsel"]


class Lane:

    def __init__(self, eng, sem):
        self.eng, self.sem, self.n, self.seen = eng, sem, 0, {}

    def wait(self, *after):
        for t in after:
            if t is None:
                continue
            if isinstance(t, list):
                self.wait(*t)
                continue
            sem, v = t
            if self.seen.get(id(sem), 0) < v:
                self.seen[id(sem)] = v
                self.eng.wait_ge(sem, v)

    def do(self, f, *after, sig=True):
        self.wait(*after)
        ins = f()
        if not sig:
            return None
        self.n += 1
        ins.then_inc(self.sem, 1)
        return (self.sem, self.n)

    def last(self):
        return (self.sem, self.n) if self.n else None


def program(nc, a, out):
    root = ExitStack()
    with root:
        def sem(name):
            return root.enter_context(nc.semaphore(name))

        engines = (("pe", nc.tensor), ("dve", nc.vector), ("act", nc.scalar), ("pool", nc.gpsimd), ("sp", nc.sync))
        pe, dve, act, pool, sp = (Lane(e, sem("s_" + n)) for n, e in engines)
        V, T, A, G = nc.vector, nc.tensor, nc.scalar, nc.gpsimd
        nd = [0]

        def sb(name, shape, dt=F32, stack=root):
            return stack.enter_context(nc.sbuf_tensor(name, shape, dt))

        def load(dst, src, *after, lane=None):
            nd[0] += 1
            s = sem(f"d{nd[0]}")
            lane = lane or sp
            lane.wait(*after)
            eng = nc.sync if lane is sp else nc.gpsimd
            eng.dma_start(dst, src).then_inc(s, 16)
            return (s, 16)

        class Counted:

            def __init__(self, name):
                self.s, self.n = sem(name), 0

            def start(self, dst, src, *after):
                sp.wait(*after)
                self.n += 16
                nc.sync.dma_start(dst, src).then_inc(self.s, 16)
                return (self.s, self.n)

        def mm(out_, lhsT, rhs, *after, start=True, stop=True, sig=True):
            return pe.do(lambda: T.matmul(out_, lhsT, rhs, start=start, stop=stop, skip_group_check=True),
                         *after, sig=sig)

        def tp(out_, in_, idn, *after, sig=True):
            return pe.do(lambda: T.transpose(out_, in_, idn), *after, sig=sig)

        def barrier():
            ts = [l.last() for l in (pe, dve, act, pool)]
            for l in (pe, dve, act, pool, sp):
                l.wait(ts)

        BK = [root.enter_context(nc.psum_tensor(f"BK{i}", [128, 512], F32)) for i in range(8)]
        BANKS = [b_[:, :] for b_ in BK]
        MB = [BK[4], BK[5]]
        MI = BK[7]
        MBf = [None, None]

        x_sb = sb("x_sb", [128, NT, D])
        idn = sb("idn", [128, 128])
        xnT = sb("xnT", [128, 2, B * S])
        gat = sb("gat", [128, 4])
        tg = sb("tg", [128, 4])
        cst = sb("cst", [128, 4])
        bns = sb("bns", [128, NT, 6])
        mv = sb("mv", [128, NT, 2])
        rst = sb("rst", [128, NT])
        rsq = sb("rsq", [128, NT])
        xn = sb("xn", [128, 2, D])

        t_x = load(x_sb[:, :, :], a["x"].rearrange("(t p) d -> p t d", p=128))
        t_id = load(idn[:, :], a["ident"])
        t_g = load(gat[:, :], a["gates"].partition_broadcast(128))
        t_c0 = pool.do(lambda: G.memset(cst[:, 0:1], 1e-5))
        t_c1 = pool.do(lambda: G.memset(cst[:, 1:2], 1e-6))
        t_tg = act.do(lambda: A.activation(tg[:, :], gat[:, :], ACT.Tanh), t_g)
        x_tok = [t_x] * NT

        def layernorm_T():
            t = None
            for i in range(NT):
                t1 = dve.do(lambda i=i: V.bn_stats(bns[:, i, :], x_sb[:, i, :]), x_tok[i])
                t = dve.do(lambda i=i: V.bn_aggr(mv[:, i, :], bns[:, i, :]), t1)
            t = act.do(lambda: A.activation(rsq[:, :], mv[:, :, 1], ACT.Sqrt, bias=cst[:, 0:1]), t, t_c0)
            tr = dve.do(lambda: V.reciprocal(rst[:, :], rsq[:, :]), t)
            done, xf = [], [None, None]
            for i in range(NT):
                k = i % 2
                t = dve.do(lambda i=i, k=k: V.tensor_scalar(xn[:, k, :], x_sb[:, i, :], mv[:, i, 0:1], rst[:, i:i + 1],
                                                       ALU.subtract, ALU.mult), tr, xf[k])
                tp(MB[k][:, 0:128], xn[:, k, 0:128], idn[:, :], t, t_id, MBf[k], sig=False)
                xf[k] = tp(MB[k][:, 128:256], xn[:, k, 128:256], idn[:, :])
                MBf[k] = act.do(lambda i=i, k=k: A.copy(xnT[:, :, i * 128:(i + 1) * 128],
                                                   MB[k][:, 0:256].rearrange("p (c n) -> p c n", c=2)), xf[k])
                done.append(MBf[k])
            return done

        L0 = ExitStack()
        ctxT = sb("ctxT", [128, 2, S2], F32, L0)
        kst = sb("kst", [128, 2, 8, S2], BF16, L0)
        va = sb("va", [128, 2, NKT, H, 17], F32, L0)
        vd = sb("vd", [128, 2, H, 17], F32, L0)
        kc = sb("kc", [128, NKT + 3, D], F32, L0)
        wk = sb("wk", [128, 7, D], F32, L0)
        wv = sb("wv", [128, 4, D], F32, L0)
        wo = sb("wo", [128, 2, D], F32, L0)
        bo = sb("bo", [128, D], F32, L0)
        prm = sb("prm", [128, 12], F32, L0)
        Q = sb("Q", [128, 2, 8, 512], BF16, L0)
        sq = sb("sq", [128, 8, D], F32, L0)
        ss = sb("ss", [128, NKT + 3, H], F32, L0)
        Xt = sb("Xt", [128, 2, 512], F32, L0)
        kth = sb("kth", [128, S2], BF16, L0)
        ktl = sb("ktl", [128, S2], BF16, L0)
        qth = sb("qth", [128, 512], BF16, L0)
        qtl = sb("qtl", [128, 512], BF16, L0)
        rsb = sb("rsb", [128, 4, 4, 128], BF16, L0)
        NP = 6
        P0 = [sb(f"P0_{i}", [128, 512], F32, L0) for i in range(NP)]
        mxp = sb("mxp", [128, 2, 8, 4], F32, L0)
        mmx = sb("mmx", [128, 2, 16], F32, L0)
        mneg = sb("mneg", [16, 2, 128], BF16, L0)
        oT = sb("oT", [128, 512], F32, L0)
        rec = sb("rec", [128, 16], F32, L0)
        on = sb("on", [128, 16, 16], F32, L0)
        oc = sb("oc", [128, 2, D], F32, L0)
        ocT = sb("ocT", [128, 2, S], F32, L0)
        yo = sb("yo", [128, D], F32, L0)
        wsum = sb("wsum", [128, 112], F32, L0)
        rsf = sq[:, :, :].rearrange("p a (b n) -> p (a b) n", n=128)

        t_wk = load(wk[:, :, :], a["wk0"])
        t_ctx = {0: load(ctxT[:, 0, :], a["ctxT"][0])}
        t_wv = load(wv[:, :, :], a["wv0"])
        t_prm = load(prm[:, :], a["prm"])
        t_rs = load(rsf, a["rsel"])
        t_ctx[1] = load(ctxT[:, 1, :], a["ctxT"][1])
        t_wo = load(wo[:, :, :], a["wo0"])
        t_bo = load(bo[:, :], a["bo0"].partition_broadcast(128))

        wk3 = wk[:, :, :].rearrange("p a (h d) -> p (a h) d", d=16)
        t = dve.do(lambda: V.tensor_reduce(wsum[:, :], wk3, AX.X, ALU.add), t_wk)
        t_wkc = dve.do(lambda: V.scalar_tensor_tensor(
            out=wk3, in0=wsum[:, :].unsqueeze(2).to_broadcast([128, 112, 16]), scalar=-1.0 / 16, in1=wk3,
            op0=ALU.mult, op1=ALU.add), t)
        t_rsb = act.do(lambda: A.copy(rsb[:, :, :, :].rearrange("p a b n -> p (a b) n"), rsf), t_rs)
        t_va = []
        for i in range(2):
            t_va.append(pool.do(lambda: G.memset(va[:, i, 0:12, :, 16:17], 1.0)))
            t = pool.do(lambda: G.memset(va[:, i, 12, :, :], 0.0))
            t_va.append(pool.do(lambda: G.memset(va[0:TMAIN, i, 12, :, 16:17], 1.0), t))
        t_q0 = pool.do(lambda: G.memset(Q[:, :, :, :], 0.0))
        t_ss = pool.do(lambda: G.memset(ss[:, :, :], 16.0))
        t_pv0 = dve.do(lambda: V.memset(BK[6][:, :], 0.0))
        t_vone = []
        for i in range(2):
            t_vone.append(dve.do(lambda: V.tensor_scalar(vd[0:TAIL, i, :, 16:17], va[0:TAIL, i, 0, :, 16:17],
                                                         prm[0:TAIL, 8:9], None, ALU.mult), t_va, t_prm))

        xnt = layernorm_T()

        def grp(ap):
            return ap.rearrange("p (h d) -> p h d", d=16)

        fr = {"bank": {}, "X": [None, None], "xi": 0, "bi": 0, "sq": [t_rsb, t_rsb], "si": 0, "kt": None, "qt": None,
              "kc": None, "kcq": None, "ss": t_ss, "kst": [None, None], "va": [None, None], "Q": [None, None],
              "ctx": [None, None], "PV": t_pv0}
        ktok, qtok, vtok, rowtok0 = {}, {}, {}, {}

        def prep(b, banks):
            par = b % 2
            if b >= 2:
                t_ctx[b] = load(ctxT[:, par, :], a["ctxT"][b], fr["ctx"][par])

            def bank():
                i = banks[fr["bi"] % len(banks)]
                fr["bi"] += 1
                return i, BK[i], fr["bank"].get(i)

            def stats(lo, hi, n, t):
                k = fr["si"] % 2
                fr["si"] += 1
                s4 = sq[0:n, 4 * k:4 * k + hi - lo, :]
                t1 = act.do(lambda: A.activation(s4, kc[0:n, lo:hi, :], ACT.Square), t, fr["sq"][k])
                yield
                fr["sq"][k] = dve.do(lambda: V.tensor_reduce(
                    ss[0:n, lo:hi, :], s4.rearrange("p k (h d) -> p k h d", d=16), AX.X, ALU.add), t1, fr["ss"])
                return fr["sq"][k]

            st = []
            for kt in range(NKT + 1):
                n = 128 if kt < 12 else TAIL
                k0 = min(kt, 12) * 128
                w = 1 if kt == NKT else 0
                i, bk, bf_ = bank()
                mm(bk[0:n, 0:256], ctxT[:, par, k0:k0 + n], wk[:, w, :], t_ctx[b], t_wkc, bf_, sig=False)
                t = fr["ctx"][par] = mm(bk[0:n, 256:512], ctxT[:, par, k0:k0 + n], wv[:, w, :], t_wv)
                tk = dve.do(lambda: V.tensor_tensor(kc[0:n, kt, :], bk[0:n, 0:256], wk[0:n, 4 + w, :], ALU.add), t,
                            fr["kc"])
                if kt < NKT:
                    m = 128 if kt < 12 else TMAIN
                    tv = dve.do(lambda: V.tensor_tensor(va[0:m, par, kt, :, 0:16], grp(bk[0:m, 256:512]),
                                                        grp(wv[0:m, 2, :]), ALU.add), t_va, fr["va"][par])
                    fr["bank"][i] = tv
                else:
                    tv = dve.do(lambda: V.tensor_tensor(vd[0:n, par, :, 0:16], grp(bk[0:n, 256:512]),
                                                        grp(wv[0:n, 3, :]), ALU.add), t_vone, fr["va"][par])
                    fr["bank"][i] = tv
                    tv = dve.do(lambda: V.tensor_scalar(vd[0:n, par, :, 0:16], vd[0:n, par, :, 0:16], prm[0:n, 8:9],
                                                        None, ALU.mult), tv)
                if kt in (3, 7, 11):
                    st.append((yield from stats(kt - 3, kt + 1, 128, tk)))
                elif kt == NKT:
                    st.append((yield from stats(12, 14, TAIL, tk)))
                yield
            vtok[b] = tv
            for t2 in range(2):
                i, bk, bf_ = bank()
                tok = b * S + t2 * 128
                mm(bk[:, 0:256], xnT[:, 0, tok:tok + 128], wk[:, 2, :], bf_, xnt, start=True, stop=False, sig=False)
                t = mm(bk[:, 0:256], xnT[:, 1, tok:tok + 128], wk[:, 3, :], start=False, stop=True)
                fr["bank"][i] = t = dve.do(lambda: V.tensor_tensor(kc[:, 14 + t2, :], bk[:, 0:256], wk[:, 6, :],
                                                                   ALU.add), t, fr["kcq"])
                yield
            st.append((yield from stats(14, 16, 128, t)))
            yield
            t = act.do(lambda: A.activation(ss[:, :, :], ss[:, :, :], ACT.Sqrt, scale=1.0 / 16, bias=cst[:, 1:2]), st,
                       t_c1)
            t_r = dve.do(lambda: V.reciprocal(ss[:, :, :], ss[:, :, :]), t)
            yield

            def scaled(lo, hi, n):
                v = kc[0:n, lo:hi, :].rearrange("p k (h d) -> p (k h) d", d=16)
                return pool.do(lambda: G.tensor_tensor(
                    v, v, ss[0:n, lo:hi, :].rearrange("p k h -> p (k h)").unsqueeze(2)
                    .to_broadcast([n, (hi - lo) * 16, 16]), ALU.mult), t_r)

            tq = scaled(14, 16, 128)
            tks = [scaled(0, 4, 128), scaled(4, 8, 128), scaled(8, 12, 128)]
            tke = fr["ss"] = scaled(12, 14, TAIL)
            yield

            def scale_out(bk, i, fill, n, wcol):
                k = fr["xi"] % 2
                fr["xi"] += 1
                fr["bank"][i] = tx = act.do(lambda: A.activation(
                    Xt[:, k, 0:n], bk, ACT.Identity, scale=prm[:, wcol:wcol + 1], bias=prm[:, wcol + 1:wcol + 2]), fill,
                    t_prm, fr["X"][k])
                return k, n, tx

            def split(x_, hi, lo, after):
                k, n, tx = x_
                th = dve.do(lambda: V.tensor_copy(hi, Xt[:, k, 0:n]), tx, after)
                eng, ob = (pool, G) if n > 100 else (dve, V)
                fr["X"][k] = eng.do(lambda: ob.tensor_tensor(lo, Xt[:, k, 0:n], hi, ALU.subtract), th)
                return fr["X"][k]

            i, bk, bf_ = bank()
            for j in range(4):
                fill = tp(bk[:, 128 * j:128 * j + 128], kc[:, 14 + j % 2, 128 * (j // 2):128 * (j // 2) + 128], idn[:, :],
                          tq, t_id, bf_, sig=(j == 3))
            fr["kcq"] = fill
            x_ = scale_out(bk[:, :], i, fill, 512, 4)
            yield
            tqs = split(x_, qth[:, :], qtl[:, :], fr["qt"])
            yield
            for hf_ in range(2):
                cs = slice(128 * hf_, 128 * hf_ + 128)
                ht = []
                for c in range(3):
                    i, bk, bf_ = bank()
                    for j in range(4):
                        fill = tp(bk[:, 128 * j:128 * j + 128], kc[:, 4 * c + j, cs], idn[:, :], tks[c], t_id, bf_,
                                  sig=(j == 3))
                    w_ = slice(512 * c, 512 * c + 512)
                    x_ = scale_out(bk[:, :], i, fill, 512, 0)
                    yield
                    ht.append(split(x_, kth[:, w_], ktl[:, w_], fr["kt"]))
                i, bk, bf_ = bank()
                tp(bk[:, 0:TAIL], kc[0:TAIL, 12, cs], idn[0:TAIL, 0:TAIL], tke, bf_)
                fill = fr["kc"] = tp(bk[:, 128:128 + TAIL], kc[0:TAIL, 13, cs], idn[0:TAIL, 0:TAIL])
                xm = scale_out(bk[:, 0:TMAIN], i, fill, TMAIN, 0)
                xd = scale_out(bk[:, 128 + TMAIN:128 + TAIL], i, fill, NDCA, 2)
                yield
                w_ = slice(1536, NMAIN)
                ht.append(split(xm, kth[:, w_], ktl[:, w_], fr["kt"]))
                w_ = slice(NMAIN, S2)
                ht.append(split(xd, kth[:, w_], ktl[:, w_], fr["kt"]))
                yield
                for p in range(4 * hf_, 4 * hf_ + 4):
                    if p % 2 == 0:
                        i, bk, bf_ = bank()
                        for j in range(2):
                            w_ = slice(256 * hf_, 256 * hf_ + 256)
                            o = bk[:, 256 * j:256 * j + 256]
                            mm(o, rsb[:, (p + j) % 4, 2, :], qth[:, w_], tqs, t_rsb, bf_, start=True, stop=False,
                               sig=False)
                            t = mm(o, rsb[:, (p + j) % 4, 3, :], qtl[:, w_], start=False, stop=True)
                        fr["qt"] = t
                        act.do(lambda: A.copy(Q[0:64, par, p:p + 2, 0:256],
                                              bk[0:64, :].rearrange("p (a n) -> p a n", a=2)), t, fr["Q"][par], t_q0,
                               sig=False)
                        fr["bank"][i] = qtok[b, p // 2] = act.do(lambda: A.copy(
                            Q[64:128, par, p:p + 2, 256:512], bk[64:128, :].rearrange("p (a n) -> p a n", a=2)))
                        yield
                    two = []
                    for c in range(4):
                        i, bk, bf_ = bank()
                        w_ = slice(512 * c, min(512 * c + 512, S2))
                        n = w_.stop - w_.start
                        mm(bk[:, 0:n], rsb[:, p % 4, 0, :], kth[:, w_], ht, bf_, start=True, stop=False, sig=False)
                        t = mm(bk[:, 0:n], rsb[:, p % 4, 1, :], ktl[:, w_], start=False, stop=True)
                        for lo, hi, col in ([(0, 512, 10)] if c < 3 else [(0, TMAIN, 10), (TMAIN, TAIL, 11)]):
                            o = kst[:, par, p, 512 * c + lo:512 * c + hi]
                            if c == 3 or (c == 1 and p % 2):
                                t1 = dve.do(lambda: V.tensor_scalar(o, bk[:, lo:hi], prm[:, col:col + 1], None,
                                                                    ALU.add), t, fr["kst"][par])
                            else:
                                t1 = act.do(lambda: A.activation(o, bk[:, lo:hi], ACT.Identity,
                                                                 bias=prm[:, col:col + 1]), t, fr["kst"][par])
                        fr["bank"][i] = t1
                        two.append(t1)
                        if c == 3:
                            ktok[b, p] = two
                        yield
                fr["kt"] = t

        rows = [Counted("s_row0"), Counted("s_row1")]
        bnc = [Counted("s_bn0"), Counted("s_bn1")]
        rowd = [nc.dram_tensor(f"rowd{i}", (16, 128), BF16, kind="Internal").ap() for i in range(2)]
        mi = [0]
        mnf = [None, None]
        mpf = [None, None]

        def max0(b, qd, need):
            gi = 4 * b + qd
            g, par = gi % 2, b % 2
            need(b, 2 * qd + 1)
            last = None
            for u in range(8):
                r, p, q2 = u // 4, 2 * qd + (u // 2) % 2, u % 2
                lhs = Q[:, par, p, 256 * r + 128 * q2:256 * r + 128 * q2 + 128]
                for c in range(3):
                    i = mi[0] % 2
                    mi[0] += 1
                    t = mm(MB[i][:, :], lhs, kst[:, par, p, 512 * c:512 * c + 512], MBf[i], ktok[b, p], qtok[b, qd])
                    last = MBf[i] = dve.do(lambda: V.tensor_reduce(mxp[:, g, u, c:c + 1], MB[i][:, :], AX.X, ALU.max),
                                           t, mpf[g])
                    yield
            for r in range(2):
                i = mi[0] % 2
                mi[0] += 1
                for v in range(4):
                    p, q2 = 2 * qd + v // 2, v % 2
                    t = mm(MB[i][:, TAIL * v:TAIL * v + TAIL],
                           Q[:, par, p, 256 * r + 128 * q2:256 * r + 128 * q2 + 128], kst[:, par, p, 1536:S2], MBf[i],
                           sig=(v == 3))
                mb = MB[i][:, 0:4 * TAIL].rearrange("p (v n) -> p v n", v=4)
                dve.do(lambda: V.tensor_reduce(mxp[:, g, 4 * r:4 * r + 4, 3], mb[:, :, 0:TMAIN], AX.X, ALU.max), t,
                       sig=False)
                last = MBf[i] = dve.do(lambda: V.tensor_reduce(mmx[:, g, 8 * r + 4:8 * r + 8], mb[:, :, TMAIN:TAIL],
                                                               AX.X, ALU.max), mnf[g])
                yield
            tq_ = t
            mpf[g] = t = dve.do(lambda: V.tensor_reduce(
                mmx[:, g, :].rearrange("p (r k v) -> p r k v", r=2, k=2)[:, :, 0, :],
                mxp[:, g, :, :].rearrange("p (r v) c -> p r v c", r=2), AX.X, ALU.max), last)
            yield
            t = tp(BK[7][0:16, 0:128], mmx[:, g, :], idn[:, :], t, fr["bank"].get(7))
            fr["bank"][7] = t = dve.do(lambda: V.tensor_scalar(mneg[:, g, :], BK[7][0:16, 0:128], -1.0, None, ALU.mult),
                                       t, mnf[g])
            mnf[g] = tw_ = bnc[g].start(rowd[g], mneg[:, g, :], t)
            for r in range(2):
                rowtok0[b, qd] = rows[g].start(
                    Q[64 * r + 48:64 * r + 50, par, 2 * qd:2 * qd + 2, 256 * r:256 * r + 256],
                    rowd[g][8 * r:8 * r + 8, :].rearrange("(k p t) n -> k p (t n)", k=2, p=2), tw_, tq_)
            yield

        S0 = [BK[0], BK[1], BK[2]]
        p0f = [None] * NP
        stc = [0]
        pc = [0]
        hist = []

        def scores0(s_):
            b, qd, kt = s_ // 52, (s_ // 13) % 4, s_ % 13
            n = 128 if kt < 12 else TAIL
            two = []
            for j in range(2):
                i = stc[0] % 3
                stc[0] += 1
                p = 2 * qd + j
                t = mm(S0[i][0:n, :], kst[:, b % 2, p, 128 * kt:128 * kt + n], Q[:, b % 2, p, :], rowtok0[b, qd],
                       fr["bank"].get(i))
                k = pc[0] % NP
                pc[0] += 1
                te = act.do(lambda: A.activation(P0[k][0:n, :], S0[i][0:n, :], ACT.Exp, scale=0.25), t, p0f[k])
                fr["bank"][i] = te
                two.append((k, n, te))
            if s_ % 52 == 51:
                fr["kst"][b % 2] = fr["Q"][b % 2] = t
            hist.append(two)

        def value0(s_):
            b, qd, kp = s_ // 52, (s_ // 13) % 4, s_ % 13
            for j in range(4):
                k, n, te = hist[s_][j // 2]
                w_ = slice(256 * (j % 2), 256 * (j % 2) + 256)
                t = mm(BK[6][32 * j:32 * j + 17, 0:256], va[0:n, b % 2, kp, 4 * qd + j, :], P0[k][0:n, w_], te, vtok[b],
                       fr["PV"], start=(kp == 0), stop=(kp == NKT - 1))
                p0f[k] = t
                if kp == NKT - 1 and j % 2 == 1:
                    for jj in (j - 1, j):
                        w_ = slice(256 * (jj % 2), 256 * (jj % 2) + 256)
                        t = mm(BK[6][32 * jj:32 * jj + 17, 256:512], vd[0:n, b % 2, 4 * qd + jj, :], P0[k][0:n, w_])
                    p0f[k] = t
            if s_ % 52 == 51:
                fr["va"][b % 2] = t
            return t

        ocf = [None]
        oTf = [None]

        def out0(b, qd, tpv):
            fr["PV"] = t = act.do(lambda: A.copy(oT[:, :], BK[6][:, :]), tpv, oTf[0])
            yield
            MI_ = BK[7]
            for j in range(4):
                t2 = tp(MI_[:, 128 * j:128 * j + 128], oT[:, 128 * j:128 * j + 128], idn[:, :], t, fr["bank"].get(7),
                        sig=(j == 3))
            oTf[0] = t2
            mv_ = MI_[:, :].rearrange("p (g d) -> p g d", d=32)
            tr = dve.do(lambda: V.reciprocal(rec[:, :], mv_[:, :, 16]), t2)
            fr["bank"][7] = tr = dve.do(lambda: V.tensor_tensor(
                on[:, :, :], mv_[:, :, 0:16], rec[:, :].unsqueeze(2).to_broadcast([128, 16, 16]), ALU.mult), tr)
            ov = on[:, :, :].rearrange("p (k t h) d -> p k t (h d)", k=2, t=2)
            t = dve.do(lambda: V.tensor_tensor(oc[:, :, 64 * qd:64 * qd + 64], ov[:, 0, :, :], ov[:, 1, :, :], ALU.add),
                       tr, ocf[0])
            yield
            if qd < 3:
                return
            for dt in range(2):
                for t2 in range(2):
                    tt = tp(MI_[:, 256 * dt + 128 * t2:256 * dt + 128 * t2 + 128], oc[:, t2, 128 * dt:128 * dt + 128],
                            idn[:, :], t, fr["bank"].get(7), sig=(dt + t2 == 2))
            ocf[0] = tt
            fr["bank"][7] = tc = act.do(lambda: A.copy(ocT[:, :, :].rearrange("p c n -> p (c n)"), MI_[:, :]), tt)
            yield
            for t2 in range(2):
                for dt in range(2):
                    tt = mm(MI_[:, 256 * t2:256 * t2 + 256], ocT[:, dt, 128 * t2:128 * t2 + 128], wo[:, dt, :], tc, t_wo,
                            fr["bank"].get(7), start=(dt == 0), stop=(dt == 1), sig=(dt == 1))
            ty = None
            for t2 in range(2):
                i = 2 * b + t2
                ty = fr["bank"][7] = dve.do(lambda: V.tensor_tensor(yo[:, :], MI_[:, 256 * t2:256 * t2 + 256], bo[:, :],
                                                                    ALU.add), tt, t_bo, ty and x_tok[i - 1])
                x_tok[i] = dve.do(lambda: V.scalar_tensor_tensor(
                    out=x_sb[:, i, :], in0=yo[:, :], scalar=tg[:, 0:1], in1=x_sb[:, i, :], op0=ALU.mult, op1=ALU.add),
                    ty, t_tg, xnt)
            yield

        def chain(*gens):
            for g in gens:
                if g is not None:
                    yield from g

        preps = {0: prep(0, [0, 1, 2, 3, 7])}

        def need(b, p):
            while (b, p) not in ktok:
                next(preps[b])

        LEAD, LAG0 = 17, 2
        NS0 = 16 * NKT
        mxs = chain(*[max0(g // 4, g % 4, need) for g in range(16)])
        og = iter(())
        for s_ in range(-LEAD, NS0 + LAG0):
            kt = s_ % 13
            b, qd = s_ // 52, (s_ // 13) % 4
            if s_ >= 0 and s_ < NS0:
                while (b, qd) not in rowtok0:
                    next(mxs)
                if kt == 0 and qd == 0:
                    for _ in preps[b]:
                        pass
                    if b + 1 < B:
                        preps[b + 1] = prep(b + 1, [3, 7])
                scores0(s_)
                for _ in range(PR0[s_ % 4]):
                    if b + 1 < B:
                        next(preps[b + 1], None)
            elif s_ < 0:
                next(preps[0], None)
                next(preps[0], None)
            for _ in range(3 if kt % 13 == 6 else 2):
                next(mxs, None)
            if LAG0 <= s_:
                t = value0(s_ - LAG0)
                sv = s_ - LAG0
                if sv % 13 == 12:
                    for _ in og:
                        pass
                    og = out0(sv // 52, (sv // 13) % 4, t)
                    next(og)
                else:
                    next(og, None)
        for _ in og:
            pass
        L0.close()
        barrier()

        F0 = ExitStack()
        w1 = sb("w1", [128, 2, 2, 128], F32, F0)
        w2 = sb("w2", [128, D], F32, F0)
        wg_ = sb("wg_", [128, 2, E], F32, F0)
        wd_ = sb("wd_", [128, 2, 128], F32, F0)
        wu_ = sb("wu_", [128, D], F32, F0)
        be = sb("be", [128, E], F32, F0)
        rwf = sb("rwf", [128, 2, E * 128], F32, F0)
        rwh = sb("rwh", [128, 2, E * 128], BF16, F0)
        rwl = sb("rwl", [128, 2, E * 128], BF16, F0)
        rw2 = sb("rw2", [128, E, 64], F32, F0)
        sel = sb("sel", [128, E, 128], BF16, F0)
        amk = sb("amk", [128, 12], F32, F0)
        pr = sb("pr", [128, NT, E], F32, F0)
        pb = sb("pb", [128, NT, E], F32, F0)
        pw = sb("pw", [128, NT, E], F32, F0)
        pw3 = sb("pw3", [128, NT, 4, E], F32, F0)
        m8 = sb("m8", [128, NT, 8], F32, F0)
        sm = sb("sm", [128, NT], F32, F0)
        smr = sb("smr", [128, NT], F32, F0)
        wT = sb("wT", [128, B * S], BF16, F0)
        xlX = sb("xlX", [128, 512], F32, F0)
        xlH = sb("xlH", [128, 512], BF16, F0)
        xl = sb("xl", [128, 2, 512], BF16, F0)
        rr = sb("rr", [128, 2, 512], F32, F0)
        r2 = sb("r2", [128, 2, 512], F32, F0)
        tt_ = sb("tt_", [128, 2, 512], F32, F0)
        hh = sb("hh", [128, 2, 512], F32, F0)
        hsh = sb("hsh", [128, 512], F32, F0)
        accT = sb("accT", [128, 512], F32, F0)

        l_w1 = load(w1[:, :, 0, :], a["sw1T"]), load(w1[:, :, 1, :], a["swgT"])
        l_wd = load(wd_[:, :, :], a["WdT"])
        l_wg = load(wg_[:, :, :], a["WgT"])
        l_be = load(be[:, :], a["bias_e"].partition_broadcast(128))
        l_am = load(amk[:, :], a["prm"])
        l_rw = load(rwf[:, 0, :], a["rw1T"]), load(rwf[:, 1, :], a["rwgT"])
        l_sel = load(xlX[:, 0:128], a["seld"])
        l_r2 = load(rw2[:, :, :], a["rw2T"])
        l_w2 = load(w2[:, :], a["sw2T"])
        l_wu = load(wu_[:, :], a["WuT"])

        xnt = layernorm_T()
        bf = [None] * 8
        bf[4], bf[5] = MBf
        t_rh = act.do(lambda: A.copy(rwh[:, :, :], rwf[:, :, :]), *l_rw)
        t_rl = dve.do(lambda: V.tensor_tensor(rwl[:, :, :], rwf[:, :, :], rwh[:, :, :], ALU.subtract), t_rh)
        t_sel = dve.do(lambda: V.tensor_copy(sel[:, :, :], xlX[:, 0:E].unsqueeze(2).to_broadcast([128, E, 128])), l_sel)
        for i in range(NT):
            for c in range(2):
                t = mm(BANKS[6][:, 16 * i:16 * i + 16], xnT[:, c, 128 * i:128 * i + 128], wg_[:, c, :], l_wg, xnt,
                       start=(c == 0), stop=(c == 1), sig=(c == 1 and i == NT - 1))
        lg = BANKS[6][:, 0:NT * E].rearrange("p (t e) -> p t e", e=E)
        tpr = act.do(lambda: A.activation(pr[:, :, :], lg, ACT.Sigmoid), t)
        bf[6] = tpr
        t = dve.do(lambda: V.tensor_tensor(pb[:, :, :], pr[:, :, :], be[:, :].unsqueeze(1).to_broadcast([128, NT, E]),
                                           ALU.add), tpr, l_be)
        for i in range(NT):
            t1 = dve.do(lambda i=i: V.max(m8[:, i, :], pb[:, i, :]), t)
            t2 = dve.do(lambda i=i: V.match_replace(pw[:, i, :], m8[:, i, :], pb[:, i, :], -3e38), t1)
        t = dve.do(lambda: V.tensor_tensor(pb[:, :, :], pb[:, :, :], pw[:, :, :], ALU.not_equal), t2)
        t = dve.do(lambda: V.tensor_tensor(pr[:, :, :], pb[:, :, :], pr[:, :, :], ALU.mult), t)
        t = dve.do(lambda: V.tensor_reduce(sm[:, :], pr[:, :, :], AX.X, ALU.add), t)
        t = dve.do(lambda: V.reciprocal(smr[:, :], sm[:, :]), t)
        t = dve.do(lambda: V.scalar_tensor_tensor(out=pw[:, :, :], in0=pr[:, :, :], scalar=2.5,
                                                  in1=smr[:, :].unsqueeze(2).to_broadcast([128, NT, E]),
                                                  op0=ALU.mult, op1=ALU.mult), t)
        t0 = dve.do(lambda: V.memset(pw3[:, :, 3, :], 0.0))
        hb = sb("hb", [128, 2, NT, E], BF16, F0)
        t1 = dve.do(lambda: V.tensor_copy(hb[:, 0, :, :], pw[:, :, :]), t)
        t = dve.do(lambda: V.tensor_copy(pw3[:, :, 0, :], hb[:, 0, :, :]), t1)
        t = dve.do(lambda: V.tensor_tensor(pw[:, :, :], pw[:, :, :], pw3[:, :, 0, :], ALU.subtract), t)
        t = dve.do(lambda: V.tensor_copy(hb[:, 1, :, :], pw[:, :, :]), t)
        t = dve.do(lambda: V.tensor_copy(pw3[:, :, 1, :], hb[:, 1, :, :]), t)
        t = dve.do(lambda: V.tensor_tensor(pw3[:, :, 2, :], pw[:, :, :], pw3[:, :, 1, :], ALU.subtract), t)
        t_wz = pool.do(lambda: G.memset(wT[:, :], 0.0))
        for half in range(2):
            for i in range(4):
                tk = 4 * half + i
                tt = tp(MI[0:64, 128 * i:128 * i + 128], pw3[:, tk, :, :].rearrange("p a e -> p (a e)"), idn[:, :], t, t0,
                        bf[7], sig=(i == 3))
            bf[7] = t_wT = act.do(lambda half=half: A.copy(wT[0:64, 512 * half:512 * half + 512], MI[0:64, :]), tt, t_wz)
        HX = {"rr": [None, None], "hh": [None, None]}
        xlf = [None]
        hsf = [None]
        acf = [None]
        for ch in range(2):
            tok = slice(512 * ch, 512 * ch + 512)
            for m in range(2):
                for c in range(2):
                    t = mm(BANKS[m], w1[:, c, m, :], xnT[:, c, tok], *l_w1, bf[m], start=(c == 0), stop=(c == 1),
                           sig=(c == 1))
            tr = act.do(lambda: A.activation(rr[:, 0, :], BANKS[1], ACT.Relu), t, HX["rr"][0])
            bf[1] = tr
            bf[0] = t1 = dve.do(lambda: V.tensor_tensor(tt_[:, 0, :], BANKS[0], rr[:, 0, :], ALU.mult), tr)
            t_hs = dve.do(lambda: V.tensor_tensor(hsh[:, :], tt_[:, 0, :], rr[:, 0, :], ALU.mult), t1, hsf[0])
            HX["rr"][0] = t_hs
            for c in range(2):
                t = mm(BANKS[2], wd_[:, c, :], xnT[:, c, tok], l_wd, bf[2], start=(c == 0), stop=(c == 1), sig=(c == 1))
            bf[2] = t = act.do(lambda: A.copy(xlX[:, :], BANKS[2]), t, t_sel, xlf[0])
            t = dve.do(lambda: V.tensor_copy(xlH[:, :], xlX[:, :]), t)
            t_xl = xlf[0] = dve.do(lambda ch=ch: V.scalar_tensor_tensor(
                out=xl[:, ch, :], in0=xlH[:, :], scalar=amk[:, 9:10], in1=xlX[:, :], op0=ALU.mult, op1=ALU.add), t, l_am)
            down = []
            for e in range(E + 1):
                if e < E:
                    k = e % 2
                    g1, g2, g3 = 3 * k, 3 * k + 1, 3 * k + 2
                    for m, gb in ((1, g2), (0, g1)):
                        mm(BANKS[gb], rwh[:, m, 128 * e:128 * e + 128], xl[:, ch, :], t_xl, t_rh, bf[gb], start=True,
                           stop=False, sig=False)
                        t = mm(BANKS[gb], rwl[:, m, 128 * e:128 * e + 128], xl[:, ch, :], t_rl, start=False, stop=True)
                        if m == 1:
                            tg_ = t
                    tb = mm(BANKS[g3], sel[:, e, :], wT[:, tok], t_sel, t_wT, t_wz, bf[g3])
                    bf[g2] = t1 = act.do(lambda k=k, g2=g2: A.activation(rr[:, k, :], BANKS[g2], ACT.Relu), tg_,
                                         HX["rr"][k])
                    t2 = act.do(lambda k=k: A.activation(r2[:, k, :], rr[:, k, :], ACT.Square), t1)
                    bf[g1] = t3 = dve.do(lambda k=k, g1=g1: V.tensor_tensor(tt_[:, k, :], BANKS[g1], r2[:, k, :],
                                                                       ALU.mult), t2, t)
                    HX["rr"][k] = t3
                    bf[g3] = t4 = dve.do(lambda k=k, g3=g3: V.tensor_tensor(hh[:, k, :], BANKS[g3], tt_[:, k, :],
                                                                       ALU.mult), t3, tb, HX["hh"][k])
                    down.append(t4)
                if e >= 1:
                    ep, k = e - 1, (e - 1) % 2
                    HX["hh"][k] = mm(BANKS[6][0:64, :], rw2[:, ep, :], hh[:, k, :], down[ep], l_r2, bf[6],
                                     start=(ep == 0), stop=(ep == E - 1))
            tz = act.do(lambda: A.copy(accT[0:64, :], BANKS[6][0:64, :]), HX["hh"][(E - 1) % 2], acf[0])
            bf[6] = tz
            for i in range(4):
                tk = 4 * ch + i
                o = BANKS[7][:, 256 * (i % 2):256 * (i % 2) + 256]
                mm(o, hsh[:, 128 * i:128 * i + 128], w2[:, :], t_hs, l_w2, bf[7], start=True, stop=False, sig=False)
                t = mm(o, accT[0:64, 128 * i:128 * i + 128], wu_[0:64, :], tz, l_wu, start=False, stop=True)
                bf[7] = x_tok[tk] = dve.do(lambda o=o, tk=tk: V.scalar_tensor_tensor(
                    out=x_sb[:, tk, :], in0=o, scalar=tg[:, 2:3], in1=x_sb[:, tk, :], op0=ALU.mult, op1=ALU.add),
                    t, x_tok[tk])
            hsf[0] = acf[0] = t
        MBf[0], MBf[1] = bf[4], bf[5]
        F0.close()
        barrier()

        L1 = ExitStack()
        M1 = sb("M1", [128, 2, H, 128], F32, L1)
        N1 = sb("N1", [128, H, D], F32, L1)
        cth = sb("cth", [128, B, S2], BF16, L1)
        ctl = sb("ctl", [128, B, S2], BF16, L1)
        ckh = sb("ckh", [128, B, NKT, 128], BF16, L1)
        ckl = sb("ckl", [128, B, NKT, 128], BF16, L1)
        mcb = sb("mcb", [128, B, NKT], F32, L1)
        mc8 = sb("mc8", [128, B, 12], U8, L1)
        mt8 = sb("mt8", [128, B], U8, L1)
        mb8 = sb("mb8", [128, S2], U8, L1)
        mbc = sb("mbc", [128, 2, S2], F32, L1)
        W1 = ExitStack()
        wq1 = sb("wq1", [128, H, D], F32, W1)
        wk1 = sb("wk1", [128, 8, 128], F32, W1)
        wv1 = sb("wv1", [128, 8, 128], F32, W1)
        wo1 = sb("wo1", [128, H, D], F32, W1)
        ctf = sb("ctf", [128, 2, S2], F32, W1)
        ckf = sb("ckf", [128, 2, NKT, 128], F32, W1)
        l_wq = load(wq1[:, :, :], a["wqT1"])
        l_wk = load(wk1[:, :, :], a["wkT1"])
        l_cf = [load(ctf[:, b, :], a["ctxT"][b]) for b in range(2)]
        l_wv = load(wv1[:, :, :], a["wvT1"])
        l_wo = load(wo1[:, :, :], a["wo1"])
        l_mc = load(mc8[:, :, :], a["mcol"])
        l_mt = load(mt8[0:TAIL, :], a["mtail"])
        l_ck = []
        dve.do(lambda: V.tensor_scalar(mcb[:, :, 0:12], mc8[:, :, :], 1.0, NEG, ALU.subtract, ALU.mult), l_mc)
        dve.do(lambda: V.tensor_scalar(mcb[0:TAIL, :, 12], mt8[0:TAIL, :], 1.0, NEG, ALU.subtract, ALU.mult), l_mt)
        xnt = layernorm_T()
        bf = [None] * 8
        bf[4], bf[5] = MBf
        t_ct = []
        for b in range(B):
            k = b % 2
            if b >= 2:
                l_cf.append(load(ctf[:, k, :], a["ctxT"][b], t_ct[b - 2]))
            th = act.do(lambda b=b, k=k: A.copy(cth[:, b, :], ctf[:, k, :]), l_cf[b])
            t_ct.append(pool.do(lambda b=b, k=k: G.tensor_tensor(ctl[:, b, :], ctf[:, k, :], cth[:, b, :], ALU.subtract),
                                th))
            lk = [load(ckf[:, k, 0:12, :], a["ctxk"][b, 0:1536, :].rearrange("(k p) d -> p k d", p=128),
                       l_ck[b - 2] if b >= 2 else None),
                  load(ckf[0:TAIL, k, 12, :], a["ctxk"][b, 1536:S2, :])]
            tk = []
            for m, kk in ((128, slice(0, 12)), (TAIL, slice(12, 13))):
                th = act.do(lambda: A.copy(ckh[0:m, b, kk, :], ckf[0:m, k, kk, :]), lk)
                tk.append(dve.do(lambda: V.tensor_tensor(ckl[0:m, b, kk, :], ckf[0:m, k, kk, :], ckh[0:m, b, kk, :],
                                                         ALU.subtract), th))
            l_ck.append(tk)
        for h in range(H):
            i = h % 4
            for dt in range(2):
                mm(BANKS[i][:, 128 * dt:128 * dt + 128], wq1[:, h, 128 * dt:128 * dt + 128], wk1[:, h // 2, :], l_wq,
                   l_wk, bf[i], sig=False)
            t = mm(BANKS[i][:, 256:512], wv1[:, h // 2, :], wo1[:, h, :], l_wv, l_wo)
            bf[i] = dve.do(lambda i=i, h=h: V.tensor_copy(M1[:, :, h, :],
                                                     BANKS[i][:, 0:256].rearrange("p (c n) -> p c n", c=2)), t)
            bf[i] = dve.do(lambda i=i, h=h: V.tensor_copy(N1[:, h, :], BANKS[i][:, 256:512]))
        t_MN = bf[i]
        W1.close()
        barrier()
        ones = sb("ones", [128, 128], F32, L1)
        onb = sb("onb", [128, 128], BF16, L1)
        mrw = sb("mrw", [128, 2, 512], BF16, L1)
        mng = sb("mng", [4, 2, 128], BF16, L1)
        qh = sb("qh", [128, 3, 512], BF16, L1)
        ql = sb("ql", [128, 3, 512], BF16, L1)
        junk = sb("junk", [128, 512], BF16, L1)
        mtl = sb("mtl", [128, 4, TAIL], F32, L1)
        mp1 = sb("mp1", [128, 4, 4], F32, L1)
        mm1 = sb("mm1", [128, 4], F32, L1)
        NR = 5
        P1 = [sb(f"P1_{i}", [128, 512], F32, L1) for i in range(NR)]
        Ph = [sb(f"Ph_{i}", [128, 512], BF16, L1) for i in range(NR)]
        Pl = [sb(f"Pl_{i}", [128, 512], BF16, L1) for i in range(NR)]
        acc = sb("acc", [128, 2, 512], F32, L1)
        dn = sb("dn", [128, 8], F32, L1)
        dg = sb("dg", [128, 4, 128], F32, L1)
        rc = sb("rc", [128, 512], F32, L1)
        oN = sb("oN", [128, H, S], F32, L1)
        t_on = pool.do(lambda: G.memset(ones[:, :], 1.0))
        t_ob = pool.do(lambda: G.memset(onb[:, :], 1.0))
        t_mr0 = pool.do(lambda: G.memset(mrw[:, :, :], 0.0))

        S1, PV1, DN1, PJ = [BANKS[0], BANKS[1]], [BANKS[2], BANKS[3]], BANKS[6], BANKS[7]
        S1f, PV1f, DN1f, PJf = [None, None], [None, None], [None], [None]
        MBf = [None, None]
        mask_tok = {}
        l_m8 = [None]
        NG = B * 8
        qf = [None] * 3
        qt1 = {}
        row1 = [Counted("s_r1a"), Counted("s_r1b")]
        mrf = [None, None]
        mngf = [None, None]
        rowtok = {}

        def mask_load(b):
            t = load(mb8[:, :], a["mrow"][b:b + 1, :].partition_broadcast(128) if False else a["mrow"][b].partition_broadcast(128), l_m8[0])
            l_m8[0] = mask_tok[b] = dve.do(lambda: V.tensor_scalar(mbc[:, b % 2, :], mb8[:, :], 1.0, NEG, ALU.subtract,
                                                                   ALU.mult), t, mask_tok.get(("free", b)))

        def qproj(g):
            b, r = g // 8, g % 3
            for j in range(2):
                h = 2 * (g % 8) + j
                for dt in range(2):
                    t = mm(PJ[:, 256 * j:256 * j + 256], M1[:, dt, h, :], xnT[:, dt, S * b:S * b + S], PJf[0],
                           start=(dt == 0), stop=(dt == 1), sig=(dt == 1))
                yield
            t1 = act.do(lambda: A.copy(qh[:, r, :], PJ), t, qf[r])
            PJf[0] = t2 = dve.do(lambda: V.tensor_tensor(ql[:, r, :], PJ, qh[:, r, :], ALU.subtract), t1)
            qt1[g] = t2
            yield

        mpc = [None]
        jk = [None]

        def max1(g):
            b, r, par = g // 8, g % 3, g % 2
            if g % 8 == 0:
                mask_load(b)
            last = None
            for u in range(4):
                lhs = qh[:, r, 128 * u:128 * u + 128]
                for c in range(3):
                    i = mi[0] % 2
                    mi[0] += 1
                    t = mm(MB[i][:, :], lhs, cth[:, b, 512 * c:512 * c + 512], MBf[i], qt1[g])
                    last = MBf[i] = dve.do(lambda u=u, c=c, i=i: V.tensor_tensor_reduce(
                        out=junk[:, :], in0=MB[i][:, :], in1=mbc[:, b % 2, 512 * c:512 * c + 512], scale=1.0,
                        scalar=-3e38, op0=ALU.add, op1=ALU.max, accum_out=mp1[:, u, c:c + 1]), t, mask_tok[b], mpc[0],
                        jk[0])
                    jk[0] = last
                    yield
            i = mi[0] % 2
            mi[0] += 1
            for u in range(4):
                t = mm(MB[i][:, TAIL * u:TAIL * u + TAIL], qh[:, r, 128 * u:128 * u + 128], cth[:, b, 1536:S2], MBf[i],
                       sig=(u == 3))
            MBf[i] = t = dve.do(lambda: V.tensor_tensor(
                mtl[:, :, :], MB[i][:, 0:4 * TAIL].rearrange("p (u n) -> p u n", u=4),
                mbc[:, b % 2, 1536:S2].unsqueeze(1).to_broadcast([128, 4, TAIL]), ALU.add), t)
            t = dve.do(lambda: V.tensor_reduce(mp1[:, :, 3], mtl[:, :, :], AX.X, ALU.max), t)
            if g % 8 == 7:
                mask_tok[("free", b + 2)] = t
            mpc[0] = t = dve.do(lambda: V.tensor_reduce(mm1[:, :], mp1[:, :, :], AX.X, ALU.max), t, last)
            t = tp(PJ[0:4, 0:128], mm1[:, :], idn[:, :], t, PJf[0])
            PJf[0] = t = dve.do(lambda: V.tensor_scalar(mng[:, par, :], PJ[0:4, 0:128], -1e20, -1.0, ALU.max, ALU.mult), t,
                                mngf[par])
            yield
            mngf[par] = tw_ = bnc[par].start(rowd[par][0:4, :], mng[:, par, :], t)
            rowtok[g] = row1[par].start(mrw[0:1, par, :], rowd[par][0:4, :].rearrange("(o u) n -> o (u n)", o=1), tw_,
                                        mrf[par], t_mr0)
            yield

        p1f = [None] * NR
        phf = [None] * NR
        LAG = 3
        accf = [None, None]
        p1c = [0]
        rcf = [None]
        MR = [2, 2, 2, 1, 1, 1, 1, 1, 1, 1, 1, 2, 2]

        def scores1(g, kt):
            b, r, par = g // 8, g % 3, g % 2
            n = 128 if kt < 12 else TAIL
            i = stc[0] % 2
            stc[0] += 1
            ks = slice(128 * kt, 128 * kt + n)
            o = S1[i][0:n, :]
            mm(o, cth[:, b, ks], qh[:, r, :], S1f[i], qt1[g], start=True, stop=False, sig=False)
            mm(o, cth[:, b, ks], ql[:, r, :], start=False, stop=False, sig=False)
            mm(o, ctl[:, b, ks], qh[:, r, :], start=False, stop=False, sig=False)
            t = mm(o, onb[:, 0:n], mrw[:, par, :], rowtok[g], start=False, stop=True)
            if kt == NKT - 1:
                qf[r] = mrf[par] = t
            k = p1c[0] % NR
            p1c[0] += 1
            S1f[i] = te = act.do(lambda: A.activation(
                P1[k][0:n, :], o, ACT.Exp, scale=SCALE1, bias=mcb[0:n, b, kt:kt + 1]), t, p1f[k])
            th = act.do(lambda: A.copy(Ph[k][0:n, :], P1[k][0:n, :]), te, phf[k])
            if kt == 1:
                k0, te0 = hist[-1][0], hist[-1][3]
                accd[g] = hist[-1][4] = pool.do(lambda: G.tensor_tensor(acc[:, par, :], P1[k0][:, :], P1[k][:, :],
                                                                        ALU.add), te, te0, accf[par])
            elif kt > 1:
                accd[g] = pool.do(lambda: G.tensor_tensor(acc[0:n, par, :], acc[0:n, par, :], P1[k][0:n, :], ALU.add),
                                  te, accd[g])
            hist.append([k, n, th, te, accd.get(g)])

        def rest1(s_):
            k, n, th, te, tad = hist[s_]
            if s_ % 13 in (2, 5, 8, 11):
                tl = pool.do(lambda: G.tensor_tensor(Pl[k][0:n, :], P1[k][0:n, :], Ph[k][0:n, :], ALU.subtract), th,
                             phf[k])
            else:
                tl = dve.do(lambda: V.tensor_tensor(Pl[k][0:n, :], P1[k][0:n, :], Ph[k][0:n, :], ALU.subtract), th,
                            phf[k])
            hist[s_][2] = tl
            p1f[k] = [tl, tad]

        def value1(s_):
            g, kp = s_ // NKT, s_ % NKT
            b, par = g // 8, g % 2
            k, n, tl, te, _ = hist[s_]
            mm(PV1[par], ckh[0:n, b, kp, :], Ph[k][0:n, :], tl, l_ck[b], PV1f[par], start=(kp == 0), stop=False,
               sig=False)
            mm(PV1[par], ckl[0:n, b, kp, :], Ph[k][0:n, :], start=False, stop=False, sig=False)
            phf[k] = pvt[g] = mm(PV1[par], ckh[0:n, b, kp, :], Pl[k][0:n, :], start=False, stop=(kp == NKT - 1))

        hist, accd, pvt = [], {}, {}
        oNf = [None]
        dgf = [None]

        def out1(g):
            b, par = g // 8, g % 2
            ta = accd[g]
            for u in range(4):
                t = mm(DN1[:, 128 * u:128 * u + 128], acc[:, par, 128 * u:128 * u + 128], ones[:, :], ta, DN1f[0],
                       sig=(u == 3))
            accf[par] = t
            t = dve.do(lambda: V.tensor_scalar(dn[:, 0:4], DN1.rearrange("p (u n) -> p u n", u=4)[:, :, 0], 1e-30, None,
                                               ALU.max), t)
            DN1f[0] = t
            t = dve.do(lambda: V.reciprocal(dn[:, 4:8], dn[:, 0:4]), t)
            t = pool.do(lambda: G.tensor_tensor(dg[:, :, :], idn[:, :].unsqueeze(1).to_broadcast([128, 4, 128]),
                                                dn[:, 4:8].unsqueeze(2).to_broadcast([128, 4, 128]), ALU.mult), t, dgf[0])
            yield
            yield
            dgf[0] = t = mm(DN1, ones[:, :], dg[:, :, :].rearrange("p u n -> p (u n)"), t, DN1f[0])
            DN1f[0] = t = act.do(lambda: A.copy(rc[:, :], DN1), t, rcf[0])
            yield
            h = 2 * (g % 8)
            PV1f[par] = rcf[0] = t = dve.do(lambda: V.tensor_tensor(
                oN[:, h:h + 2, :].rearrange("p h n -> p (h n)"), PV1[par], rc[:, :], ALU.mult), t, pvt[g], oNf[0])
            yield
            if g % 8 < 7:
                return
            for t2 in range(2):
                for h in range(H):
                    tt = mm(PJ[:, 0:256], oN[:, h, 128 * t2:128 * t2 + 128], N1[:, h, :], t, PJf[0], start=(h == 0),
                            stop=(h == H - 1), sig=(h == H - 1))
                i = 2 * b + t2
                PJf[0] = x_tok[i] = dve.do(lambda: V.scalar_tensor_tensor(
                    out=x_sb[:, i, :], in0=PJ[:, 0:256], scalar=tg[:, 1:2], in1=x_sb[:, i, :], op0=ALU.mult,
                    op1=ALU.add), tt, x_tok[i])
                yield
            oNf[0] = tt

        for g in range(2):
            for _ in qproj(g):
                pass
        for _ in max1(0):
            pass
        NS = NG * NKT
        mg = og = iter(())
        for s_ in range(NS + LAG + 1):
            g, kt = s_ // NKT, s_ % NKT
            if kt == 0:
                for _ in mg:
                    pass
                mg = chain(max1(g + 1) if g + 1 < NG else None, qproj(g + 2) if g + 2 < NG else None)
            if kt == LAG + 1 and s_ > NKT:
                for _ in og:
                    pass
                og = out1(g - 1)
            if s_ < NS:
                scores1(g, kt)
            if 1 <= s_ <= NS:
                rest1(s_ - 1)
            for _ in range(MR[kt]):
                next(mg, None)
            if kt > LAG:
                next(og, None)
            if LAG <= s_ < NS + LAG:
                value1(s_ - LAG)
        for _ in og:
            pass
        for _ in out1(NG - 1):
            pass
        L1.close()
        barrier()

        wr = [sb(f"wr{i}", [128, 2048], F32) for i in range(3)]
        tw = [sb(f"tw{i}", [128, 2048], BF16) for i in range(3)]
        qa = sb("qa", [128, 2048], F32)
        qb_ = sb("qb_", [128, 2048], F32)
        asum = sb("asum", [128, 3], F32)
        sc = sb("sc", [128, 3], F32)
        hs_ = sb("hs_", [128, 3], F32)
        on1 = sb("on1", [128, 128], F32)
        xh = sb("xh", [128, 2, B * S], BF16)
        xlo = sb("xlo", [128, 2, B * S], BF16)
        sg = sb("sg", [128, 2, 512], F32)
        u1 = sb("u1", [128, 2, 512], F32)
        hf = sb("hf", [128, 2, 512], F32)
        hhi = sb("hhi", [128, 8, 512], BF16)
        hlo = sb("hlo", [128, 8, 512], BF16)
        fin = sb("fin", [128, NT, D], F32)
        gs = sb("gs", [128, 1], F32)
        l3 = [load(wr[0][:, :], a["wup"]), load(wr[1][:, :], a["wgate"]), load(wr[2][:, :], a["wdown"])]
        t_o1 = pool.do(lambda: G.memset(on1[:, :], 1.0 / (1024 * 256)))
        for i in range(3):
            t = dve.do(lambda i=i: V.tensor_reduce(asum[:, i:i + 1], wr[i][:, :], AX.X, ALU.add,
                                              apply_absolute_value=True), l3[i])
        t = mm(BANKS[7][:, 0:3], on1[:, :], asum[:, :], t, t_o1)
        t_sc = dve.do(lambda: V.tensor_scalar(sc[:, :], BANKS[7][:, 0:3], 1e-8, None, ALU.add), t)
        t_hp = dve.do(lambda: V.tensor_scalar(hs_[:, :], sc[:, :], 0.5, None, ALU.mult), t_sc)
        t_qb = None
        t_tw = []
        sc2 = sb("sc2", [128, 3], F32)
        t_hn = dve.do(lambda: V.tensor_scalar(sc2[:, :], sc[:, :], -0.5, None, ALU.mult), t_sc)
        for i in range(3):
            t1 = dve.do(lambda i=i: V.tensor_scalar(qa[:, :], wr[i][:, :], hs_[:, i:i + 1], None, ALU.is_gt), t_hp, t_qb)
            t2 = dve.do(lambda i=i: V.tensor_scalar(qb_[:, :], wr[i][:, :], sc2[:, i:i + 1], None, ALU.is_lt), t_hn, t_qb)
            t_qb = pool.do(lambda i=i: G.tensor_tensor(tw[i][:, :], qa[:, :], qb_[:, :], ALU.subtract), t1, t2)
            t_tw.append(t_qb)
        xnt = layernorm_T()
        bf = [None] * 8
        bf[4], bf[5] = MBf
        t_xh = act.do(lambda: A.copy(xh[:, :, :], xnT[:, :, :]), xnt)
        t_xl = dve.do(lambda: V.tensor_tensor(xlo[:, :, :], xnT[:, :, :], xh[:, :, :], ALU.subtract), t_xh)
        t_gs = dve.do(lambda: V.tensor_tensor(gs[:, :], tg[:, 3:4], sc[:, 2:3], ALU.mult), t_sc)
        up = tw[0][:, :].rearrange("p (c e) -> p c e", c=2)
        ga = tw[1][:, :].rearrange("p (c e) -> p c e", c=2)
        dw = tw[2][:, :].rearrange("p (e d) -> p e d", e=8)
        f = {"sg": [None, None], "hf": [None, None], "h": None}
        outd = out.rearrange("b (t p) d -> p (b t) d", p=128)
        stores = []
        for ch in range(2):
            tok = slice(512 * ch, 512 * ch + 512)
            for e in range(8):
                k = e % 2
                b0, b1 = 2 * k, 2 * k + 1
                for w, bk, tw_ in ((up, b0, t_tw[0]), (ga, b1, t_tw[1])):
                    for c in range(2):
                        es = slice(128 * e, 128 * e + 128)
                        mm(BANKS[bk], w[:, c, es], xh[:, c, tok], tw_, t_xh, bf[bk], start=(c == 0), stop=False,
                           sig=False)
                        t = mm(BANKS[bk], w[:, c, es], xlo[:, c, tok], t_xl, start=False, stop=(c == 1), sig=(c == 1))
                    if w is up:
                        tu = t
                t1 = act.do(lambda k=k, b0=b0: A.activation(sg[:, k, :], BANKS[b0], ACT.Sigmoid, scale=sc[:, 0:1]), tu,
                            f["sg"][k])
                bf[b0] = t2 = dve.do(lambda k=k, b0=b0: V.scalar_tensor_tensor(
                    out=u1[:, k, :], in0=BANKS[b0], scalar=sc[:, 0:1], in1=sg[:, k, :], op0=ALU.mult, op1=ALU.mult), t1)
                bf[b1] = t3 = dve.do(lambda k=k, b1=b1: V.scalar_tensor_tensor(
                    out=hf[:, k, :], in0=BANKS[b1], scalar=sc[:, 1:2], in1=u1[:, k, :], op0=ALU.mult, op1=ALU.mult),
                    t2, t, f["hf"][k])
                f["sg"][k] = t3
                t4 = act.do(lambda e=e, k=k: A.copy(hhi[:, e, :], hf[:, k, :]), t3, f["h"])
                f["hf"][k] = t_h = dve.do(lambda e=e, k=k: V.tensor_tensor(hlo[:, e, :], hf[:, k, :], hhi[:, e, :],
                                                                      ALU.subtract), t4)
            for i in range(4):
                tk = 4 * ch + i
                bk = 6 + i % 2
                for e in range(8):
                    for part in (hhi, hlo):
                        t = mm(BANKS[bk][:, 0:256], part[:, e, 128 * i:128 * i + 128], dw[:, e, :], t_h, t_tw[2], bf[bk],
                               start=(e == 0 and part is hhi), stop=(e == 7 and part is hlo),
                               sig=(e == 7 and part is hlo))
                bf[bk] = tf = dve.do(lambda tk=tk, bk=bk: V.scalar_tensor_tensor(
                    out=fin[:, tk, :], in0=BANKS[bk][:, 0:256], scalar=gs[:, 0:1], in1=x_sb[:, tk, :], op0=ALU.mult,
                    op1=ALU.add), t, t_gs)
                stores.append(load(outd[:, tk, :], fin[:, tk, :], tf))
            f["h"] = t
        sp.wait(stores)
        barrier()


def layout(i):
    import numpy as np

    def f(n):
        return np.asarray(i[n])

    def kt(w, c=2):
        return w.reshape(c, 128, -1).transpose(1, 0, 2)

    z, o = np.zeros, np.ones
    g = "L0_xattn_"
    wm = np.concatenate([f(g + "Wk"), f(g + "Wv")], 1).reshape(128, 16, 2, 16)
    bm = np.concatenate([f(g + "bk"), f(g + "bv")], 0).reshape(16, 2, 16)
    wd, bd = f(g + "Wkv_dca"), f(g + "bkv_dca")
    bc = lambda v: np.broadcast_to(v.reshape(1, 1, 256), (128, 1, 256))
    wk0 = np.concatenate([wm[:, :, 0].reshape(128, 1, 256), wd[:, None, 0:256], kt(f(g + "Wq")),
                          bc(bm[:, 0]), bc(bd[0:256]), bc(f(g + "bq"))], 1)
    wv0 = np.concatenate([wm[:, :, 1].reshape(128, 1, 256), wd[:, None, 256:512], bc(bm[:, 1]), bc(bd[256:512])], 1)

    def col(w):
        return np.tile(w, 8)

    fz = z(128, np.float32)
    om, od = fz.copy(), fz.copy()
    om[[48, 112]] = 1
    od[[49, 113]] = 1
    rsel = z((128, 4, 4, 128), np.float32)
    for p in range(4):
        for r in range(2):
            for d in range(16):
                for m, slots in enumerate(((0, 2), (1,), (0, 1), (2,))):
                    for s_ in slots:
                        rsel[16 * (2 * p + r) + d, p, m, 64 * r + 16 * s_ + d] = 1
    ind = (np.arange(128) >= TMAIN).astype(np.float32)
    ahl = np.concatenate([z(64, np.float32), -o(64, np.float32)])
    prm = np.stack([col(f(g + "kn_w")), col(f(g + "kn_b")), col(f(g + "kn_dca_w")), col(f(g + "kn_dca_b")),
                    col(f(g + "qn_w")), col(f(g + "qn_b")), fz, fz, ind, ahl, om, od], 1)
    seld = z((128, 128), np.float32)
    for e in range(16):
        for part in range(3):
            seld[16 * part + e, e] = 1
    ctx = f("ctx_1024")
    mask = f("mask_BxS2_bf1").view(np.uint8)
    mcol = mask[:, :1536].reshape(4, 12, 128).transpose(2, 0, 1)
    h = "L0_ffn_"
    dup = lambda w: np.concatenate([w, w], 0)
    wdT = f(h + "Wdown").T
    j = "L1_xattn_"
    out = {
        "x": f("x").reshape(1024, 256), "ctxT": ctx.transpose(0, 2, 1), "ctxk": ctx, "mrow": mask, "mcol": mcol, "mtail": mask[:, 1536:].T,
        "gates": np.concatenate([f("g_xattn"), f("g_ffn")]),
        "wk0": wk0, "wv0": wv0, "wo0": kt(f(g + "Wo")), "bo0": f(g + "bo"), "prm": prm,
        "sw1T": kt(f(h + "sw1").T), "swgT": kt(f(h + "swg").T), "sw2T": f(h + "sw2").T,
        "rw1T": dup(f(h + "rw1").transpose(2, 0, 1).reshape(64, 2048)),
        "rwgT": dup(f(h + "rwg").transpose(2, 0, 1).reshape(64, 2048)),
        "rw2T": f(h + "rw2").transpose(2, 0, 1), "WgT": kt(f(h + "Wg").T),
        "WdT": kt(np.concatenate([wdT, wdT], 1)), "WuT": dup(f(h + "Wup").T), "bias_e": f(h + "biases"),
        "wqT1": f(j + "Wq").reshape(256, 16, 128).transpose(2, 1, 0),
        "wkT1": f(j + "Wk").reshape(128, 8, 128).transpose(2, 1, 0),
        "wvT1": f(j + "Wv").reshape(128, 8, 128).transpose(2, 1, 0),
        "wo1": f(j + "Wo").reshape(16, 128, 256).transpose(1, 0, 2),
        "wup": kt(f("L1_ffn_W_up").T).reshape(128, 2048), "wgate": kt(f("L1_ffn_W_gate").T).reshape(128, 2048),
        "wdown": kt(f("L1_ffn_W_down").T, 8).reshape(128, 2048),
        "ident": np.eye(128, dtype=np.float32), "seld": seld, "rsel": rsel.reshape(128, 16, 128),
    }
    return {k: np.ascontiguousarray(v) for k, v in out.items()}


def kernel(**inputs):
    import concourse.bacc as _bacc
    from concourse import mybir as _mybir
    from concourse.bass_utils import run_bass_kernel_spmd as _run

    nc = _bacc.Bacc("TRN2", target_bir_lowering=False, num_devices=1)
    laid = layout(inputs)
    arrays, aps = {}, {}
    for name in INS:
        v = laid[name]
        arrays[f"in_{name}"] = v
        aps[name] = nc.dram_tensor(f"in_{name}", v.shape, _mybir.dt.from_np(v.dtype), kind="ExternalInput").ap()
    out = nc.dram_tensor("out_0", (4, 256, 256), _mybir.dt.float32, kind="ExternalOutput").ap()
    program(nc, aps, out)
    r = _run(nc, [arrays], core_ids=[0])
    return r.results[0]["out_0"]
```

```python
from contextlib import ExitStack

import concourse.bass as bass
from concourse import mybir

F32 = mybir.dt.float32
BF16 = mybir.dt.bfloat16
U8 = mybir.dt.uint8
ALU = mybir.AluOpType
ACT = mybir.ActivationFunctionType
AX = mybir.AxisListType

B, S, D, KD = 4, 256, 256, 128
PR0 = [1, 1, 1, 2]
FOLD0 = 4
WST = 2
QK = (5, 7, 10, 12, 13)
LEAD = 19
SPK = 1
MW = 1
QW = 2
LEAD1 = 6
ITEMS1 = 15 + MW + QW
S2, NDCA = 1601, 16
NMAIN = S2 - NDCA
NKT = 13
TAIL = S2 - 12 * 128
TMAIN = NMAIN - 12 * 128
H = 16
NT = B * S // 128
E = 16
SCALE1 = 1.0 / float(128.0 ** 0.5)
NEG = 1e30
INS = ["x", "ctxT", "ctxk", "mrow", "mcol", "mtail", "gates", "wk0", "wv0", "wo0", "bo0", "prm",
       "sw1T", "swgT", "sw2T", "rw1T", "rwgT", "rw2T", "WgT", "WdT", "WuT", "bias_e",
       "wqT1", "wkT1", "wvT1", "wo1", "wup", "wgate", "wdown", "ident", "seld", "rsel"]


class Lane:

    def __init__(self, eng, sem):
        self.eng, self.sem, self.n, self.seen = eng, sem, 0, {}

    def wait(self, *after):
        for t in after:
            if t is None:
                continue
            if isinstance(t, list):
                self.wait(*t)
                continue
            sem, v = t
            if self.seen.get(id(sem), 0) < v:
                self.seen[id(sem)] = v
                self.eng.wait_ge(sem, v)

    def do(self, f, *after, sig=True):
        self.wait(*after)
        ins = f()
        if not sig:
            return None
        self.n += 1
        ins.then_inc(self.sem, 1)
        return (self.sem, self.n)

    def last(self):
        return (self.sem, self.n) if self.n else None


def program(nc, a, out):
    root = ExitStack()
    with root:
        def sem(name):
            return root.enter_context(nc.semaphore(name))

        engines = (("pe", nc.tensor), ("dve", nc.vector), ("act", nc.scalar), ("pool", nc.gpsimd), ("sp", nc.sync))
        pe, dve, act, pool, sp = (Lane(e, sem("s_" + n)) for n, e in engines)
        V, T, A, G = nc.vector, nc.tensor, nc.scalar, nc.gpsimd
        nd = [0]

        arena = root.enter_context(nc.sbuf_tensor("arena", [128, 207 * 256], F32))

        class Region:

            def __init__(self, lo, hi=207 * 1024):
                self.at, self.hi = lo, hi

        keep = Region(0)

        def sb(name, shape, dt=F32, region=keep):
            n = 1
            for v in shape[1:]:
                n *= v
            size = (n * {F32: 4, BF16: 2, U8: 1}[dt] + 63) // 64 * 64
            lo = region.at
            region.at += size
            assert region.at <= region.hi, (name, region.at, region.hi)
            t_ = arena[0:shape[0], lo // 4:(lo + size) // 4]
            if dt != F32:
                t_ = t_.bitcast(dt)
            t_ = t_[:, 0:n]
            if len(shape) > 2:
                ax = "abcde"[:len(shape) - 1]
                t_ = t_.rearrange(f"p ({' '.join(ax)}) -> p {' '.join(ax)}", **dict(zip(ax, shape[1:])))
            return t_

        def load(dst, src, *after, lane=None):
            nd[0] += 1
            s = sem(f"d{nd[0]}")
            lane = lane or sp
            lane.wait(*after)
            eng = nc.sync if lane is sp else nc.gpsimd
            eng.dma_start(dst, src).then_inc(s, 16)
            return (s, 16)

        class Counted:

            def __init__(self, name):
                self.s, self.n = sem(name), 0

            def start(self, dst, src, *after):
                sp.wait(*after)
                self.n += 16
                nc.sync.dma_start(dst, src).then_inc(self.s, 16)
                return (self.s, self.n)

        def mm(out_, lhsT, rhs, *after, start=True, stop=True, sig=True):
            return pe.do(lambda: T.matmul(out_, lhsT, rhs, start=start, stop=stop, skip_group_check=True),
                         *after, sig=sig)

        def tp(out_, in_, idn, *after, sig=True):
            return pe.do(lambda: T.transpose(out_, in_, idn), *after, sig=sig)

        def barrier():
            ts = [l.last() for l in (pe, dve, act, pool)]
            for l in (pe, dve, act, pool, sp):
                l.wait(ts)

        BK = [root.enter_context(nc.psum_tensor(f"BK{i}", [128, 512], F32)) for i in range(8)]
        BANKS = [b_[:, :] for b_ in BK]
        MB = [BK[4], BK[5]]
        MI = BK[7]
        MBf = [None, None]

        x_sb = sb("x_sb", [128, NT, D])
        idn = sb("idn", [128, 128])
        xnT = sb("xnT", [128, 2, B * S])
        gat = sb("gat", [128, 4])
        tg = sb("tg", [128, 4])
        cst = sb("cst", [128, 4])
        bns = sb("bns", [128, NT, 6])
        mv = sb("mv", [128, NT, 2])
        rst = sb("rst", [128, NT])
        rsq = sb("rsq", [128, NT])
        xn = sb("xn", [128, 2, D])

        t_c0 = pool.do(lambda: G.memset(cst[:, 0:1], 1e-5))
        t_c1 = pool.do(lambda: G.memset(cst[:, 1:2], 1e-6))
        xnf = [None]

        def ln_batch(b, hold, key, done, buf=None, free=None):
            buf, free = (xn, xnf) if buf is None else (buf, free)
            sl = slice(2 * b, 2 * b + 2)
            t = None
            for i in (2 * b, 2 * b + 1):
                t1 = dve.do(lambda: V.bn_stats(bns[:, i, :], x_sb[:, i, :]), x_tok[i], free[0])
                t = dve.do(lambda: V.bn_aggr(mv[:, i, :], bns[:, i, :]), t1)
            t = act.do(lambda: A.activation(rsq[:, sl], mv[:, sl, 1], ACT.Sqrt, bias=cst[:, 0:1]), t, t_c0)
            yield
            tr = dve.do(lambda: V.reciprocal(rst[:, sl], rsq[:, sl]), t)
            for k, i in enumerate((2 * b, 2 * b + 1)):
                t = dve.do(lambda: V.tensor_scalar(buf[:, k, :], x_sb[:, i, :], mv[:, i, 0:1], rst[:, i:i + 1],
                                                   ALU.subtract, ALU.mult), tr, free[0])
            yield
            for k in range(2):
                for c in range(2):
                    j = 2 * c + k
                    t1 = tp(BK[7][:, 128 * j:128 * j + 128], buf[:, k, 128 * c:128 * c + 128], idn[:, :], t, hold[key],
                            t_id, sig=(k + c == 2))
            free[0] = t1
            hold[key] = done[b] = act.do(lambda: A.copy(xnT[:, :, 256 * b:256 * b + 256],
                                                        BK[7][:, :].rearrange("p (c n) -> p c n", c=2)), t1)
            yield

        KB = 1024
        base = keep.at
        MN, CT, RAW, W1 = Region(base, 54 * KB), Region(54 * KB, 80 * KB), Region(80 * KB, 107 * KB), Region(107 * KB, 148 * KB)
        F0, CF = Region(148 * KB, 200 * KB), Region(200 * KB)
        L0a, L0b = Region(base, 80 * KB), Region(80 * KB)
        kst0 = sb("kst0", [128, 8, S2], BF16, L0b)
        ctxT = sb("ctxT", [128, 2, S2], F32, L0b)
        kst1 = sb("kst1", [128, 8, S2], BF16, L0b)
        kst = [kst0, kst1]
        va = sb("va", [128, 2, NKT, H, 17], F32, L0a)
        vd = sb("vd", [128, 2, H, 17], F32, L0a)
        kc = sb("kc", [128, NKT + 3, D], F32, L0b)
        wk = sb("wk", [128, 7, D], F32, L0a)
        wv = sb("wv", [128, 4, D], F32, L0a)
        wo = sb("wo", [128, 2, D], F32, L0a)
        bo = sb("bo", [128, D], F32, L0a)
        prm = sb("prm", [128, 12], F32, L0b)
        Q = sb("Q", [128, 2, 8, 512], BF16, L0b)
        sq = sb("sq", [128, 8, D], F32, L0b)
        ss = sb("ss", [128, NKT + 3, H], F32, L0b)
        Xt = sb("Xt", [128, 2, 512], F32, L0b)
        kth = sb("kth", [128, S2], BF16, L0b)
        ktl = sb("ktl", [128, S2], BF16, L0b)
        qth = sb("qth", [128, 512], BF16, L0b)
        qtl = sb("qtl", [128, 512], BF16, L0b)
        rsb = sb("rsb", [128, 4, 4, 128], BF16, L0b)
        NP = 8
        P0 = [sb(f"P0_{i}", [128, 512], F32, L0a) for i in range(NP)]
        mxp = sb("mxp", [128, 2, 8, 4], F32, L0b)
        mmx = sb("mmx", [128, 2, 16], F32, L0b)
        mneg = sb("mneg", [16, 2, 128], BF16, L0b)
        oT = sb("oT", [128, 512], F32, L0b)
        rec = sb("rec", [128, 16], F32, L0a)
        on = sb("on", [128, 16, 16], F32, L0a)
        oc = sb("oc", [128, 2, D], F32, L0b)
        ocT = sb("ocT", [128, 2, S], F32, L0b)
        yo = wv[:, 3, :]
        wsum = on[:, 0:7, :].rearrange("p a n -> p (a n)")
        rsf = sq[:, :, :].rearrange("p a (b n) -> p (a b) n", n=128)

        t_wk = load(wk[:, :, :], a["wk0"])
        t_ctx = {0: load(ctxT[:, 0, :], a["ctxT"][0])}
        t_wv = load(wv[:, :, :], a["wv0"])
        t_prm = load(prm[:, :], a["prm"])
        xv = a["x"].rearrange("(t p) d -> p t d", p=128)
        x_tok = [load(x_sb[:, 0:2, :], xv[:, 0:2, :])] * 2
        t_id = load(idn[:, :], a["ident"])
        t_g = load(gat[:, :], a["gates"].partition_broadcast(128))
        t_tg = act.do(lambda: A.activation(tg[:, :], gat[:, :], ACT.Tanh), t_g)
        t_rs = load(rsf, a["rsel"])
        t_ctx[1] = load(ctxT[:, 1, :], a["ctxT"][1])
        for b in range(1, B):
            x_tok += [load(x_sb[:, 2 * b:2 * b + 2, :], xv[:, 2 * b:2 * b + 2, :])] * 2
        t_wo = load(wo[:, :, :], a["wo0"])
        t_bo = load(bo[:, :], a["bo0"].partition_broadcast(128))

        t_wkc = []
        for lo, hi in ((0, 2), (2, 7)):
            wk3 = wk[:, lo:hi, :].rearrange("p a (h d) -> p (a h) d", d=16)
            ws = wsum[:, 16 * lo:16 * hi]
            t = dve.do(lambda: V.tensor_reduce(ws, wk3, AX.X, ALU.add), t_wk)
            t_wkc.append(dve.do(lambda: V.scalar_tensor_tensor(
                out=wk3, in0=ws.unsqueeze(2).to_broadcast([128, 16 * (hi - lo), 16]), scalar=-1.0 / 16, in1=wk3,
                op0=ALU.mult, op1=ALU.add), t))
        t_rsb = act.do(lambda: A.copy(rsb[:, :, :, :].rearrange("p a b n -> p (a b) n"), rsf), t_rs)
        t_va = []
        for i in range(2):
            t_va.append(pool.do(lambda: G.memset(va[:, i, 0:12, :, 16:17], 1.0)))
            t = pool.do(lambda: G.memset(va[:, i, 12, :, :], 0.0))
            t_va.append(pool.do(lambda: G.memset(va[0:TMAIN, i, 12, :, 16:17], 1.0), t))
        t_q0 = pool.do(lambda: G.memset(Q[:, :, :, :], 0.0))
        t_ss = pool.do(lambda: G.memset(ss[:, :, :], 16.0))
        t_pv0 = dve.do(lambda: V.memset(BK[6][:, :], 0.0))
        t_vone = []
        for i in range(2):
            t_vone.append(dve.do(lambda: V.tensor_scalar(vd[0:TAIL, i, :, 16:17], va[0:TAIL, i, 0, :, 16:17],
                                                         prm[0:TAIL, 8:9], None, ALU.mult), t_va, t_prm))

        lnx = {}

        def grp(ap):
            return ap.rearrange("p (h d) -> p h d", d=16)

        fr = {"bank": {7: None}, "X": [None, None], "xi": 0, "bi": 0, "sq": [t_rsb, t_rsb], "si": 0, "kt": None, "qt": None,
              "kc": None, "kcq": None, "ss": t_ss, "kst": [None, None], "va": [None, None], "Q": [None, None],
              "ctx": [None, None], "PV": t_pv0}
        ktok, qtok, vtok, rowtok0 = {}, {}, {}, {}

        def prep(b, banks):
            par = b % 2
            if b >= 2:
                t_ctx[b] = load(ctxT[:, par, :], a["ctxT"][b], fr["ctx"][par])

            def bank():
                i = banks[fr["bi"] % len(banks)]
                fr["bi"] += 1
                return i, BK[i], fr["bank"].get(i)

            def stats(lo, hi, n, t):
                k = fr["si"] % 2
                fr["si"] += 1
                s4 = sq[0:n, 4 * k:4 * k + hi - lo, :]
                t1 = act.do(lambda: A.activation(s4, kc[0:n, lo:hi, :], ACT.Square), t, fr["sq"][k])
                yield
                if b == 0:
                    fr["sq"][k] = dve.do(lambda: V.tensor_reduce(
                        ss[0:n, lo:hi, :], s4.rearrange("p k (h d) -> p k h d", d=16), AX.X, ALU.add), t1, fr["ss"])
                    return fr["sq"][k]
                sv = s4.rearrange("p k (h d) -> p (k h) d", d=16)
                for w in (8, 4, 2):
                    t1 = pool.do(lambda: G.tensor_tensor(sv[:, :, 0:w], sv[:, :, 0:w], sv[:, :, w:2 * w], ALU.add), t1)
                fr["sq"][k] = pool.do(lambda: G.tensor_tensor(
                    ss[0:n, lo:hi, :].rearrange("p k h -> p (k h)").unsqueeze(2), sv[:, :, 0:1], sv[:, :, 1:2], ALU.add),
                    t1, fr["ss"])
                return fr["sq"][k]

            def queries():
                yield from ln_batch(b, fr["bank"], 7, lnx, kc[:, 14:16, :], [fr["kcq"]])
                for t2 in range(2):
                    i, bk, bf_ = bank()
                    tok = b * S + t2 * 128
                    mm(bk[:, 0:256], xnT[:, 0, tok:tok + 128], wk[:, 2, :], bf_, lnx[b], t_wkc[1], start=True, stop=False, sig=False)
                    t = mm(bk[:, 0:256], xnT[:, 1, tok:tok + 128], wk[:, 3, :], start=False, stop=True)
                    fr["bank"][i] = t = dve.do(lambda: V.tensor_tensor(kc[:, 14 + t2, :], bk[:, 0:256], wk[:, 6, :],
                                                                       ALU.add), t, fr["kcq"])
                    tq0.append(t)
                    yield

            st, tq0 = [], []
            qs = queries()
            for kt in range(NKT + 1):
                n = 128 if kt < 12 else TAIL
                k0 = min(kt, 12) * 128
                w = 1 if kt == NKT else 0
                i, bk, bf_ = bank()
                mm(bk[0:n, 0:256], ctxT[:, par, k0:k0 + n], wk[:, w, :], t_ctx[b], t_wkc[0], bf_, sig=False)
                t = fr["ctx"][par] = mm(bk[0:n, 256:512], ctxT[:, par, k0:k0 + n], wv[:, w, :], t_wv)
                tk = dve.do(lambda: V.tensor_tensor(kc[0:n, kt, :], bk[0:n, 0:256], wk[0:n, 4 + w, :], ALU.add), t, t_wkc[1],
                            fr["kc"])
                if kt < NKT:
                    m = 128 if kt < 12 else TMAIN
                    tv = act.do(lambda: A.copy(va[0:m, par, kt, :, 0:16], grp(bk[0:m, 256:512])), t, t_va,
                                fr["va"][par], tk)
                    fr["bank"][i] = vtok[b] = tv
                else:
                    tv = dve.do(lambda: V.tensor_scalar(vd[0:n, par, :, 0:16], grp(bk[0:n, 256:512]), prm[0:n, 8:9],
                                                        None, ALU.mult), t, t_vone, fr["va"][par], vtok.get(b))
                    fr["bank"][i] = tv
                if kt in (3, 7, 11):
                    st.append((yield from stats(kt - 3, kt + 1, 128, tk)))
                elif kt == NKT:
                    st.append((yield from stats(12, 14, TAIL, tk)))
                yield
                if kt in QK:
                    next(qs, None)
            vtok[b] = [vtok[b], tv]
            for _ in qs:
                yield
            t = tq0[-1]
            st.append((yield from stats(14, 16, 128, t)))
            for _ in range(WST if b else 1):
                yield
            t = act.do(lambda: A.activation(ss[:, :, :], ss[:, :, :], ACT.Sqrt, scale=1.0 / 16, bias=cst[:, 1:2]), st,
                       t_c1)
            if b:
                yield
            def scaled(lo, hi, n, t_r):
                v = kc[0:n, lo:hi, :].rearrange("p k (h d) -> p (k h) d", d=16)
                eng, ob = (pool, G) if b else (dve, V)
                return eng.do(lambda: ob.tensor_tensor(
                    v, v, ss[0:n, lo:hi, :].rearrange("p k h -> p (k h)").unsqueeze(2)
                    .to_broadcast([n, (hi - lo) * 16, 16]), ALU.mult), t_r)

            sc_ = []
            for lo, hi, n in ((14, 16, 128), (0, 4, 128), (4, 8, 128), (8, 12, 128), (12, 14, TAIL)):
                t_r = dve.do(lambda: V.reciprocal(ss[:, lo:hi, :], ss[:, lo:hi, :]), t)
                sc_.append(scaled(lo, hi, n, t_r))
                yield
            tq, tks, tke = sc_[0], sc_[1:4], sc_[4]
            fr["ss"] = tke

            def scale_out(bk, i, fill, n, wcol):
                k = fr["xi"] % 2
                fr["xi"] += 1
                fr["bank"][i] = tx = act.do(lambda: A.activation(
                    Xt[:, k, 0:n], bk, ACT.Identity, scale=prm[:, wcol:wcol + 1], bias=prm[:, wcol + 1:wcol + 2]), fill,
                    t_prm, fr["X"][k])
                return k, n, tx

            def split(x_, hi, lo, after):
                k, n, tx = x_
                th = dve.do(lambda: V.tensor_copy(hi, Xt[:, k, 0:n]), tx, after)
                eng, ob = (pool, G) if n > 100 and (b or k == SPK) else (dve, V)
                fr["X"][k] = eng.do(lambda: ob.tensor_tensor(lo, Xt[:, k, 0:n], hi, ALU.subtract), th)
                return fr["X"][k]

            i, bk, bf_ = bank()
            for j in range(4):
                fill = tp(bk[:, 128 * j:128 * j + 128], kc[:, 14 + j % 2, 128 * (j // 2):128 * (j // 2) + 128], idn[:, :],
                          tq, t_id, bf_, sig=(j == 3))
            fr["kcq"] = fill
            x_ = scale_out(bk[:, :], i, fill, 512, 4)
            yield
            tqs = split(x_, qth[:, :], qtl[:, :], fr["qt"])
            yield
            for hf_ in range(2):
                cs = slice(128 * hf_, 128 * hf_ + 128)
                ht = []
                for c in range(3):
                    i, bk, bf_ = bank()
                    for j in range(4):
                        fill = tp(bk[:, 128 * j:128 * j + 128], kc[:, 4 * c + j, cs], idn[:, :], tks[c], t_id, bf_,
                                  sig=(j == 3))
                    w_ = slice(512 * c, 512 * c + 512)
                    x_ = scale_out(bk[:, :], i, fill, 512, 0)
                    yield
                    ht.append(split(x_, kth[:, w_], ktl[:, w_], fr["kt"]))
                i, bk, bf_ = bank()
                tp(bk[:, 0:TAIL], kc[0:TAIL, 12, cs], idn[0:TAIL, 0:TAIL], tke, bf_)
                fill = fr["kc"] = tp(bk[:, 128:128 + TAIL], kc[0:TAIL, 13, cs], idn[0:TAIL, 0:TAIL])
                xm = scale_out(bk[:, 0:TMAIN], i, fill, TMAIN, 0)
                xd = scale_out(bk[:, 128 + TMAIN:128 + TAIL], i, fill, NDCA, 2)
                yield
                w_ = slice(1536, NMAIN)
                ht.append(split(xm, kth[:, w_], ktl[:, w_], fr["kt"]))
                w_ = slice(NMAIN, S2)
                ht.append(split(xd, kth[:, w_], ktl[:, w_], fr["kt"]))
                yield
                for p in range(4 * hf_, 4 * hf_ + 4):
                    if p % 2 == 0:
                        i, bk, bf_ = bank()
                        for j in range(2):
                            w_ = slice(256 * hf_, 256 * hf_ + 256)
                            o = bk[:, 256 * j:256 * j + 256]
                            mm(o, rsb[:, (p + j) % 4, 2, :], qth[:, w_], tqs, t_rsb, bf_, start=True, stop=False,
                               sig=False)
                            t = mm(o, rsb[:, (p + j) % 4, 3, :], qtl[:, w_], start=False, stop=True)
                        fr["qt"] = t
                        act.do(lambda: A.copy(Q[0:64, par, p:p + 2, 0:256],
                                              bk[0:64, :].rearrange("p (a n) -> p a n", a=2)), t, fr["Q"][par], t_q0,
                               sig=False)
                        fr["bank"][i] = qtok[b, p // 2] = act.do(lambda: A.copy(
                            Q[64:128, par, p:p + 2, 256:512], bk[64:128, :].rearrange("p (a n) -> p a n", a=2)))
                        yield
                    two = []
                    for c in range(4):
                        i, bk, bf_ = bank()
                        w_ = slice(512 * c, min(512 * c + 512, S2))
                        n = w_.stop - w_.start
                        mm(bk[:, 0:n], rsb[:, p % 4, 0, :], kth[:, w_], ht, bf_, start=True, stop=False, sig=False)
                        t = mm(bk[:, 0:n], rsb[:, p % 4, 1, :], ktl[:, w_], start=False, stop=True)
                        for lo, hi, col in ([(0, 512, 10)] if c < 3 else [(0, TMAIN, 10), (TMAIN, TAIL, 11)]):
                            o = kst[par][:, p, 512 * c + lo:512 * c + hi]
                            if c == 3 or (c == 1 and p % 2):
                                t1 = dve.do(lambda: V.tensor_scalar(o, bk[:, lo:hi], prm[:, col:col + 1], None,
                                                                    ALU.add), t, fr["kst"][par])
                            else:
                                t1 = act.do(lambda: A.activation(o, bk[:, lo:hi], ACT.Identity,
                                                                 bias=prm[:, col:col + 1]), t, fr["kst"][par])
                        fr["bank"][i] = t1
                        two.append(t1)
                        if c == 3:
                            ktok[b, p] = two
                        yield
                fr["kt"] = t

        rows = [Counted("s_row0"), Counted("s_row1")]
        bnc = [Counted("s_bn0"), Counted("s_bn1")]
        rowd = [nc.dram_tensor(f"rowd{i}", (16, 128), BF16, kind="Internal").ap() for i in range(2)]
        mi = [0]
        mnf = [None, None]
        mpf = [None, None]

        def max0(b, qd, need):
            gi = 4 * b + qd
            g, par = gi % 2, b % 2
            need(b, 2 * qd + 1)
            last = None
            for u in range(8):
                r, p, q2 = u // 4, 2 * qd + (u // 2) % 2, u % 2
                lhs = Q[:, par, p, 256 * r + 128 * q2:256 * r + 128 * q2 + 128]
                for c in range(3):
                    i = mi[0] % 2
                    mi[0] += 1
                    t = mm(MB[i][:, :], lhs, kst[par][:, p, 512 * c:512 * c + 512], MBf[i], ktok[b, p], qtok[b, qd])
                    last = MBf[i] = dve.do(lambda: V.tensor_reduce(mxp[:, g, u, c:c + 1], MB[i][:, :], AX.X, ALU.max),
                                           t, mpf[g])
                    yield
            for r in range(2):
                i = mi[0] % 2
                mi[0] += 1
                for v in range(4):
                    p, q2 = 2 * qd + v // 2, v % 2
                    t = mm(MB[i][:, TAIL * v:TAIL * v + TAIL],
                           Q[:, par, p, 256 * r + 128 * q2:256 * r + 128 * q2 + 128], kst[par][:, p, 1536:S2], MBf[i],
                           sig=(v == 3))
                mb = MB[i][:, 0:4 * TAIL].rearrange("p (v n) -> p v n", v=4)
                dve.do(lambda: V.tensor_reduce(mxp[:, g, 4 * r:4 * r + 4, 3], mb[:, :, 0:TMAIN], AX.X, ALU.max), t,
                       sig=False)
                last = MBf[i] = dve.do(lambda: V.tensor_reduce(mmx[:, g, 8 * r + 4:8 * r + 8], mb[:, :, TMAIN:TAIL],
                                                               AX.X, ALU.max), mnf[g])
                yield
            tq_ = t
            mpf[g] = t = dve.do(lambda: V.tensor_reduce(
                mmx[:, g, :].rearrange("p (r k v) -> p r k v", r=2, k=2)[:, :, 0, :],
                mxp[:, g, :, :].rearrange("p (r v) c -> p r v c", r=2), AX.X, ALU.max), last)
            yield
            yield
            t = tp(BK[7][0:16, 0:128], mmx[:, g, :], idn[:, :], t, fr["bank"].get(7))
            fr["bank"][7] = t = dve.do(lambda: V.tensor_scalar(mneg[:, g, :], BK[7][0:16, 0:128], -1.0, None, ALU.mult),
                                       t, mnf[g])
            mnf[g] = tw_ = bnc[g].start(rowd[g], mneg[:, g, :], t)
            for r in range(2):
                rowtok0[b, qd] = rows[g].start(
                    Q[64 * r + 48:64 * r + 50, par, 2 * qd:2 * qd + 2, 256 * r:256 * r + 256],
                    rowd[g][8 * r:8 * r + 8, :].rearrange("(k p t) n -> k p (t n)", k=2, p=2), tw_, tq_)
            yield

        S0 = [BK[0], BK[1], BK[2]]
        p0f = [None] * NP
        stc = [0]
        pc = [0]
        hist = []

        def scores0(s_):
            b, qd, kt = s_ // 52, (s_ // 13) % 4, s_ % 13
            n = 128 if kt < 12 else TAIL
            two = []
            for j in range(2):
                i = stc[0] % 3
                stc[0] += 1
                p = 2 * qd + j
                t = mm(S0[i][0:n, :], kst[b % 2][:, p, 128 * kt:128 * kt + n], Q[:, b % 2, p, :], rowtok0[b, qd],
                       fr["bank"].get(i))
                k = pc[0] % NP
                pc[0] += 1
                te = act.do(lambda: A.activation(P0[k][0:n, :], S0[i][0:n, :], ACT.Exp, scale=0.25), t, p0f[k])
                fr["bank"][i] = te
                two.append((k, n, te))
            if s_ % 52 == 51:
                fr["kst"][b % 2] = fr["Q"][b % 2] = t
            hist.append(two)

        def value0(s_, between):
            b, qd, kp = s_ // 52, (s_ // 13) % 4, s_ % 13
            for j in range(4):
                if j == 2:
                    between()
                k, n, te = hist[s_][j // 2]
                w_ = slice(256 * (j % 2), 256 * (j % 2) + 256)
                t = mm(BK[6][32 * j:32 * j + 17, 0:256], va[0:n, b % 2, kp, 4 * qd + j, :], P0[k][0:n, w_], te, vtok[b],
                       fr["PV"], start=(kp == 0), stop=(kp == NKT - 1))
                p0f[k] = t
                if kp == NKT - 1 and j % 2 == 1:
                    for jj in (j - 1, j):
                        w_ = slice(256 * (jj % 2), 256 * (jj % 2) + 256)
                        t = mm(BK[6][32 * jj:32 * jj + 17, 256:512], vd[0:n, b % 2, 4 * qd + jj, :], P0[k][0:n, w_])
                    p0f[k] = t
            if s_ % 52 == 51:
                fr["va"][b % 2] = t
            return t

        t_bv = pool.do(lambda: G.tensor_tensor(wv[:, 2, :], wv[:, 2, :], wv[:, 3, :], ALU.add), t_wv)
        ocf = [None]
        oTf = [None]

        def out0(b, qd, tpv):
            fr["PV"] = t = act.do(lambda: A.copy(oT[:, :], BK[6][:, :]), tpv, oTf[0])
            yield
            MI_ = BK[7]
            for j in range(4):
                t2 = tp(MI_[:, 128 * j:128 * j + 128], oT[:, 128 * j:128 * j + 128], idn[:, :], t, fr["bank"].get(7),
                        sig=(j == 3))
            oTf[0] = t2
            mv_ = MI_[:, :].rearrange("p (g d) -> p g d", d=32)
            tr = dve.do(lambda: V.reciprocal(rec[:, :], mv_[:, :, 16]), t2)
            fr["bank"][7] = tr = dve.do(lambda: V.tensor_tensor(
                on[:, :, :], mv_[:, :, 0:16], rec[:, :].unsqueeze(2).to_broadcast([128, 16, 16]), ALU.mult), tr)
            ov = on[:, :, :].rearrange("p (k t h) d -> p k t (h d)", k=2, t=2)
            os_ = oc[:, :, 64 * qd:64 * qd + 64]
            t = dve.do(lambda: V.tensor_tensor(os_, ov[:, 0, :, :], ov[:, 1, :, :], ALU.add), tr, ocf[0])
            t = dve.do(lambda: V.tensor_tensor(os_, os_, wv[:, 2:3, 64 * qd:64 * qd + 64].to_broadcast([128, 2, 64]),
                                                ALU.add), t, t_bv)
            yield
            if qd < 3:
                return
            for dt in range(2):
                for t2 in range(2):
                    tt = tp(MI_[:, 256 * dt + 128 * t2:256 * dt + 128 * t2 + 128], oc[:, t2, 128 * dt:128 * dt + 128],
                            idn[:, :], t, fr["bank"].get(7), sig=(dt + t2 == 2))
            ocf[0] = tt
            fr["bank"][7] = tc = act.do(lambda: A.copy(ocT[:, :, :].rearrange("p c n -> p (c n)"), MI_[:, :]), tt)
            yield
            for t2 in range(2):
                for dt in range(2):
                    tt = mm(MI_[:, 256 * t2:256 * t2 + 256], ocT[:, dt, 128 * t2:128 * t2 + 128], wo[:, dt, :], tc, t_wo,
                            fr["bank"].get(7), start=(dt == 0), stop=(dt == 1), sig=(dt == 1))
            ty = None
            for t2 in range(2):
                i = 2 * b + t2
                ty = fr["bank"][7] = dve.do(lambda: V.tensor_tensor(yo, MI_[:, 256 * t2:256 * t2 + 256], bo[:, :],
                                                                    ALU.add), tt, t_bo, t_bv, ty and x_tok[i - 1])
                x_tok[i] = dve.do(lambda: V.scalar_tensor_tensor(
                    out=x_sb[:, i, :], in0=yo, scalar=tg[:, 0:1], in1=x_sb[:, i, :], op0=ALU.mult, op1=ALU.add),
                    ty, t_tg, lnx[b])
            yield

        def chain(*gens):
            for g in gens:
                if g is not None:
                    yield from g

        w1 = sb("w1", [128, 2, 2, 128], F32, RAW)
        w2 = sb("w2", [128, D], F32, RAW)
        wg_ = sb("wg_", [128, 2, E], F32, RAW)
        wd_ = sb("wd_", [128, 2, 128], F32, RAW)
        wu_ = sb("wu_", [128, D], F32, RAW)
        be = sb("be", [128, E], F32, RAW)
        rwf = sb("rwf", [128, 2, E * 128], F32, RAW)
        rw2 = sb("rw2", [128, E, 64], F32, RAW)
        amk = sb("amk", [128, 12], F32, RAW)
        seF = sb("seF", [128, 128], F32, RAW)

        def moe_loads(*after):
            sp.wait(*after)
            l_w1 = load(w1[:, :, 0, :], a["sw1T"]), load(w1[:, :, 1, :], a["swgT"])
            l_wd = load(wd_[:, :, :], a["WdT"])
            l_wg = load(wg_[:, :, :], a["WgT"])
            l_be = load(be[:, :], a["bias_e"].partition_broadcast(128))
            l_am = load(amk[:, :], a["prm"])
            l_rw = load(rwf[:, 0, :], a["rw1T"]), load(rwf[:, 1, :], a["rwgT"])
            l_sel = load(seF[:, :], a["seld"])
            l_r2 = load(rw2[:, :, :], a["rw2T"])
            l_w2 = load(w2[:, :], a["sw2T"])
            l_wu = load(wu_[:, :], a["WuT"])
            return l_w1, l_wd, l_wg, l_be, l_am, l_rw, l_sel, l_r2, l_w2, l_wu

        rwh = sb("rwh", [128, 2, E * 128], BF16, F0)
        sel = sb("sel", [128, E, 128], BF16, F0)
        hb = sb("hb", [128, 2, NT, E], BF16, F0)
        pr = sb("pr", [128, NT, E], F32, F0)
        pb = sb("pb", [128, NT, E], F32, F0)
        pw = sb("pw", [128, NT, E], F32, F0)
        pw3 = sb("pw3", [128, NT, 4, E], F32, F0)
        m8 = sb("m8", [128, NT, 8], F32, F0)
        sm = sb("sm", [128, NT], F32, F0)
        smr = sb("smr", [128, NT], F32, F0)
        wT = sb("wT", [128, B * S], BF16, F0)
        xlX = sb("xlX", [128, 512], F32, F0)
        xlH = sb("xlH", [128, 512], BF16, F0)
        xl = sb("xl", [128, 2, 512], BF16, F0)
        rr = sb("rr", [128, 2, 512], F32, F0)
        r2 = sb("r2", [128, 2, 512], F32, F0)
        rwl = sb("rwl", [128, 2, E * 128], BF16, F0)
        tt_ = sb("tt_", [128, 2, 512], F32, F0)
        hh = sb("hh", [128, 3, 512], F32, F0)

        def router_parts(l_rw):
            old = [pe.last(), act.last(), dve.last()]
            t_rh = pool.do(lambda: G.tensor_copy(rwh[:, :, :], rwf[:, :, :]), *l_rw, old)
            return t_rh, pool.do(lambda: G.tensor_tensor(rwl[:, :, :], rwf[:, :, :], rwh[:, :, :], ALU.subtract), t_rh)

        preps = {0: prep(0, [0, 1, 2, 3, 7])}

        def need(b, p):
            while (b, p) not in ktok:
                next(preps[b])

        LAG0 = 3
        NS0 = 16 * NKT
        mxs = chain(*[max0(g // 4, g % 4, need) for g in range(16)])
        og, nmx, ln0 = iter(()), [0], {}

        def maxima(half):
            while nmx[0] * 26 < (2 * (s_ + LEAD) + half) * 29:
                next(mxs, None)
                nmx[0] += 1

        for s_ in range(-LEAD, NS0 + LAG0):
            kt = s_ % 13
            b, qd = s_ // 52, (s_ // 13) % 4
            if s_ >= 0 and s_ < NS0:
                while (b, qd) not in rowtok0:
                    next(mxs)
                    nmx[0] += 1
                if kt == 0 and qd == 0:
                    for _ in preps[b]:
                        pass
                    if b == B - 1:
                        lf = moe_loads(fr["kst"][0], fr["ctx"][0])
                        t_rh, t_rl = router_parts(lf[5])
                    if b + 1 < B:
                        preps[b + 1] = prep(b + 1, [3, 7])
                scores0(s_)
                for _ in range(PR0[s_ % 4]):
                    if b + 1 < B:
                        next(preps[b + 1], None)
            elif s_ < 0:
                next(preps[0], None)
                next(preps[0], None)
            maxima(1)
            if LAG0 <= s_:
                t = value0(s_ - LAG0, lambda: maxima(2))
                sv = s_ - LAG0
                if sv % 13 == 12:
                    for _ in og:
                        pass
                    bv, qv = sv // 52, (sv // 13) % 4
                    og = chain(out0(bv, qv, t), ln_batch(bv, fr["bank"], 7, ln0) if qv == 3 else None)
                    next(og)
                else:
                    next(og, None)
            maxima(2)
        for _ in og:
            pass
        barrier()

        l_w1, l_wd, l_wg, l_be, l_am, l_rw, l_sel, l_r2, l_w2, l_wu = lf

        bf = [None] * 8
        M1 = sb("M1", [128, 2, H, 128], F32, MN)
        N1 = sb("N1", [128, H, D], F32, MN)
        cth = sb("cth", [128, B, S2], BF16, CT)
        ctl = sb("ctl", [128, B, S2], BF16, CT)
        wq1 = sb("wq1", [128, H, D], F32, W1)
        wk1 = sb("wk1", [128, 8, 128], F32, W1)
        wv1 = sb("wv1", [128, 8, 128], F32, W1)
        wo1 = sb("wo1", [128, H, D], F32, W1)
        rwv = rwf[:, :, :].rearrange("p a n -> p (a n)")
        ctf = [sb("ctf", [128, S2], F32, CF), rwv[:, 0:S2]]
        hsh = rwv[:, 2048:3072].rearrange("p (a n) -> p a n", a=2)
        l_wk = load(wk1[:, :, :], a["wkT1"])
        l_wv = load(wv1[:, :, :], a["wvT1"])
        l_wq = load(wq1[:, :, :], a["wqT1"])
        l_wo = load(wo1[:, :, :], a["wo1"])
        t_ct = []

        def fold(hs):
            for h in hs:
                for dt in range(2):
                    mm(BANKS[7][:, 128 * dt:128 * dt + 128], wq1[:, h, 128 * dt:128 * dt + 128], wk1[:, h // 2, :], l_wq,
                       l_wk, bf[7], sig=False)
                t = mm(BANKS[7][:, 256:512], wv1[:, h // 2, :], wo1[:, h, :], l_wv, l_wo)
                act.do(lambda: A.copy(M1[:, :, h, :], BANKS[7][:, 0:256].rearrange("p (c n) -> p c n", c=2)), t)
                bf[7] = act.do(lambda: A.copy(N1[:, h, :], BANKS[7][:, 256:512]))
                yield

        def context():
            t_ct = {}
            lc = {0: load(ctf[0], a["ctxT"][0])}
            for b in range(B):
                if b + 1 < B:
                    lc[b + 1] = load(ctf[(b + 1) % 2], a["ctxT"][b + 1], t_ct.get(b - 1), t_rl)
                for _ in range(4):
                    yield
                th = dve.do(lambda: V.tensor_copy(cth[:, b, :], ctf[b % 2]), lc[b])
                t_ct[b] = pool.do(lambda: G.tensor_tensor(ctl[:, b, :], ctf[b % 2], cth[:, b, :], ALU.subtract), th)
                yield

        t_sel = dve.do(lambda: V.tensor_copy(sel[:, :, :], seF[:, 0:E].unsqueeze(2).to_broadcast([128, E, 128])), l_sel)
        for i in range(NT):
            for c in range(2):
                t = mm(BANKS[6][:, 16 * i:16 * i + 16], xnT[:, c, 128 * i:128 * i + 128], wg_[:, c, :], l_wg, ln0[i // 2],
                       start=(c == 0), stop=(c == 1), sig=(c == 1 and i == NT - 1))
        lg = BANKS[6][:, 0:NT * E].rearrange("p (t e) -> p t e", e=E)
        tpr = act.do(lambda: A.activation(pr[:, :, :], lg, ACT.Sigmoid), t)
        bf[6] = tpr
        t_z3 = dve.do(lambda: V.memset(pw3[:, :, 3, :], 0.0))
        t_wz = dve.do(lambda: V.memset(wT[:, :], 0.0))
        t = dve.do(lambda: V.tensor_tensor(pb[:, :, :], pr[:, :, :], be[:, :].unsqueeze(1).to_broadcast([128, NT, E]),
                                           ALU.add), tpr, l_be)
        side = fold(range(H))
        t8 = [dve.do(lambda: V.max(m8[:, i, :], pb[:, i, :]), t) for i in range(NT)]
        HX = {"rr": [None, None], "hh": [None] * 3}
        t_xl, t_hs, xlf = [None, None], [None, None], None
        for ch in range(2):
            tok = slice(512 * ch, 512 * ch + 512)
            kb = 3 * ch
            for c in range(2):
                t = mm(BANKS[kb + 2], wd_[:, c, :], xnT[:, c, tok], l_wd, start=(c == 0), stop=(c == 1), sig=(c == 1))
            for m in (1, 0):
                for c in range(2):
                    tm = mm(BANKS[kb + m], w1[:, c, m, :], xnT[:, c, tok], *l_w1, start=(c == 0), stop=(c == 1),
                            sig=(c == 1))
                if m == 1:
                    tr = tm
            bf[kb + 2] = t = act.do(lambda: A.copy(xlX[:, :], BANKS[kb + 2]), t, xlf)
            bf[kb + 1] = tr = act.do(lambda: A.activation(r2[:, ch, :], BANKS[kb + 1], ACT.Relu), tr)
            t = dve.do(lambda: V.tensor_copy(xlH[:, :], xlX[:, :]), t)
            t_xl[ch] = xlf = dve.do(lambda: V.scalar_tensor_tensor(
                out=xl[:, ch, :], in0=xlH[:, :], scalar=amk[:, 9:10], in1=xlX[:, :], op0=ALU.mult, op1=ALU.add), t, l_am)
            bf[kb] = t1 = dve.do(lambda: V.tensor_tensor(tt_[:, ch, :], BANKS[kb], r2[:, ch, :], ALU.mult), tr, tm)
            t_hs[ch] = HX["rr"][ch] = pool.do(lambda: G.tensor_tensor(hsh[:, ch, :], tt_[:, ch, :], r2[:, ch, :],
                                                                      ALU.mult), t1, t_rl)
            if ch == 0:
                t9 = [dve.do(lambda: V.match_replace(pw[:, i, :], m8[:, i, :], pb[:, i, :], -3e38), t8[i])
                      for i in range(NT)]
                t = dve.do(lambda: V.tensor_tensor(pb[:, :, :], pb[:, :, :], pw[:, :, :], ALU.not_equal), t9[-1])
                t = dve.do(lambda: V.tensor_tensor(pr[:, :, :], pb[:, :, :], pr[:, :, :], ALU.mult), t)
                t = dve.do(lambda: V.tensor_reduce(sm[:, :], pr[:, :, :], AX.X, ALU.add), t)
                t = dve.do(lambda: V.reciprocal(smr[:, :], sm[:, :]), t)
                t_pw = dve.do(lambda: V.scalar_tensor_tensor(out=pw[:, :, :], in0=pr[:, :, :], scalar=2.5,
                                                             in1=smr[:, :].unsqueeze(2).to_broadcast([128, NT, E]),
                                                             op0=ALU.mult, op1=ALU.mult), t)
        for _ in range(FOLD0):
            next(side)
        t1 = dve.do(lambda: V.tensor_copy(hb[:, 0, :, :], pw[:, :, :]), t_pw)
        t = dve.do(lambda: V.tensor_copy(pw3[:, :, 0, :], hb[:, 0, :, :]), t1)
        t = dve.do(lambda: V.tensor_tensor(pw[:, :, :], pw[:, :, :], pw3[:, :, 0, :], ALU.subtract), t)
        t = dve.do(lambda: V.tensor_copy(hb[:, 1, :, :], pw[:, :, :]), t)
        t = dve.do(lambda: V.tensor_copy(pw3[:, :, 1, :], hb[:, 1, :, :]), t)
        t = dve.do(lambda: V.tensor_tensor(pw3[:, :, 2, :], pw[:, :, :], pw3[:, :, 1, :], ALU.subtract), t)
        t_wT = [None, None]
        for half in range(2):
            for i in range(4):
                tk = 4 * half + i
                tt = tp(BK[6][0:64, 128 * i:128 * i + 128], pw3[:, tk, :, :].rearrange("p a e -> p (a e)"), idn[:, :],
                        t, t_z3, bf[6], sig=(i == 3))
            bf[6] = t_wT[half] = act.do(lambda: A.copy(wT[0:64, 512 * half:512 * half + 512], BK[6][0:64, :]), tt, t_wz)
        ln1, t_ac = {}, [None, None]

        def up(e, ch):
            k = e % 2
            g1, g2, g3 = 3 * k, 3 * k + 1, 3 * k + 2
            for m, gb in ((1, g2), (0, g1)):
                mm(BANKS[gb], rwh[:, m, 128 * e:128 * e + 128], xl[:, ch, :], t_xl[ch], t_rh, bf[gb], start=True,
                   stop=False, sig=False)
                t = mm(BANKS[gb], rwl[:, m, 128 * e:128 * e + 128], xl[:, ch, :], t_rl, start=False, stop=True)
                if m == 1:
                    tg_ = t
            tb = mm(BANKS[g3], sel[:, e, :], wT[:, 512 * ch:512 * ch + 512], t_sel, t_wT[ch], t_wz, bf[g3])
            bf[g2] = t1 = act.do(lambda: A.activation(rr[:, k, :], BANKS[g2], ACT.Relu), tg_, HX["rr"][k])
            t2 = act.do(lambda: A.activation(r2[:, k, :], rr[:, k, :], ACT.Square), t1)
            bf[g1] = HX["rr"][k] = t3 = dve.do(lambda: V.tensor_tensor(tt_[:, k, :], BANKS[g1], r2[:, k, :], ALU.mult),
                                               t2, t)
            s3 = (16 * ch + e) % 3
            bf[g3] = t4 = dve.do(lambda: V.tensor_tensor(hh[:, s3, :], BANKS[g3], tt_[:, k, :], ALU.mult), t3, tb,
                                 HX["hh"][s3])
            return t4

        def tail(ch, banks):
            for i in range(4):
                bk, off = banks[i]
                o = BANKS[bk][:, off:off + 256]
                mm(o, hsh[:, ch, 128 * i:128 * i + 128], w2[:, :], t_hs[ch], l_w2, bf[bk], start=True, stop=False,
                   sig=False)
                t = mm(o, xlX[0:64, 128 * i:128 * i + 128], wu_[0:64, :], t_ac[ch], l_wu, start=False, stop=True)
                tk = 4 * ch + i
                bf[bk] = x_tok[tk] = dve.do(lambda: V.scalar_tensor_tensor(
                    out=x_sb[:, tk, :], in0=o, scalar=tg[:, 2:3], in1=x_sb[:, tk, :], op0=ALU.mult, op1=ALU.add),
                    t, x_tok[tk])
                yield
            HX["acc"] = t

        hist0, ctx_side = [], context()
        for s_ in range(2 * E + 2):
            if s_ < 2 * E:
                hist0.append(up(s_ % E, s_ // E))
            if s_ >= 2:
                p, k = s_ - 2, (s_ - 2) % 3
                HX["hh"][k] = mm(BANKS[6][0:64, :], rw2[:, p % E, :], hh[:, k, :], hist0[p], l_r2, bf[6],
                                 start=(p % E == 0), stop=(p % E == E - 1))
                if p % E == E - 1:
                    ch = p // E
                    bf[6] = t_ac[ch] = act.do(lambda: A.copy(xlX[0:64, :], BANKS[6][0:64, :]), HX["hh"][k],
                                              HX.get("acc"), xlf)
                    if ch == 0:
                        side = chain(side, tail(0, [(7, 0), (7, 256)] * 2), ln_batch(0, bf, 7, ln1),
                                     ln_batch(1, bf, 7, ln1))
            next(side, None)
            next(ctx_side, None)
        for _ in chain(side, ctx_side, tail(1, [(i, 0) for i in range(4)])):
            pass
        barrier()

        CK, L1 = Region(80 * KB, 107 * KB), Region(107 * KB)
        ckh = sb("ckh", [128, B, NKT, 128], BF16, CK)
        ckl = sb("ckl", [128, B, NKT, 128], BF16, CK)
        mcb = sb("mcb", [128, B, NKT], F32, L1)
        mc8 = sb("mc8", [128, B, 12], U8, L1)
        mt8 = sb("mt8", [128, B], U8, L1)
        mb8 = sb("mb8", [128, S2], U8, L1)
        mbc = sb("mbc", [128, S2], F32, L1)
        ckf = sb("ckf", [128, NKT, 128], F32, L1)
        l_mc = load(mc8[:, :, :], a["mcol"])
        l_mt = load(mt8[0:TAIL, :], a["mtail"])
        l_ck = []
        dve.do(lambda: V.tensor_scalar(mcb[:, :, 0:12], mc8[:, :, :], 1.0, NEG, ALU.subtract, ALU.mult), l_mc)
        dve.do(lambda: V.tensor_scalar(mcb[0:TAIL, :, 12], mt8[0:TAIL, :], 1.0, NEG, ALU.subtract, ALU.mult), l_mt)
        l_ck = {}

        def values(b):
            lk = [load(ckf[:, 0:12, :], a["ctxk"][b, 0:1536, :].rearrange("(k p) d -> p k d", p=128), l_ck.get(b - 1)),
                  load(ckf[0:TAIL, 12, :], a["ctxk"][b, 1536:S2, :])]
            yield
            tk = []
            for m, lo, hi in ((128, 0, 6), (128, 6, 12), (TAIL, 12, 13)):
                th = act.do(lambda: A.copy(ckh[0:m, b, lo:hi, :], ckf[0:m, lo:hi, :]), lk)
                tk.append(pool.do(lambda: G.tensor_tensor(ckl[0:m, b, lo:hi, :], ckf[0:m, lo:hi, :],
                                                          ckh[0:m, b, lo:hi, :], ALU.subtract), th))
                yield
            l_ck[b] = tk
            yield

        ones = sb("ones", [128, 128], F32, L1)
        onb = sb("onb", [128, 128], BF16, L1)
        mrw = sb("mrw", [128, 2, 512], BF16, L1)
        mng = sb("mng", [4, 2, 128], BF16, L1)
        qh = sb("qh", [128, 3, 512], BF16, L1)
        ql = sb("ql", [128, 3, 512], BF16, L1)
        junk = sb("junk", [128, 512], BF16, L1)
        mtl = sb("mtl", [128, 4, TAIL], F32, L1)
        mp1 = sb("mp1", [128, 4, 4], F32, L1)
        mm1 = sb("mm1", [128, 4], F32, L1)
        NR = 4
        P1 = [sb(f"P1_{i}", [128, 512], F32, L1) for i in range(NR)]
        Ph = [sb(f"Ph_{i}", [128, 512], BF16, L1) for i in range(NR)]
        Pl = [sb(f"Pl_{i}", [128, 512], BF16, L1) for i in range(NR)]
        acc = sb("acc", [128, 2, 512], F32, L1)
        dn = sb("dn", [128, 8], F32, L1)
        dg = sb("dg", [128, 4, 128], F32, L1)
        rc = sb("rc", [128, 512], F32, L1)
        oN = sb("oN", [128, H, S], F32, L1)
        tw = [sb(f"tw{i}", [128, 2048], BF16, L1) for i in range(3)]
        wr = sb("wr", [128, 2048], F32, L1)
        qa = sb("qa", [128, 1024], F32, L1)
        qb_ = sb("qb_", [128, 1024], F32, L1)
        asum = sb("asum", [128, 3], F32, L1)
        as4 = sb("as4", [128, 4], F32, L1)
        sc = sb("sc", [128, 3], F32, L1)
        hs_ = sb("hs_", [128, 3, 2], F32, L1)
        on1 = sb("on1", [128, 128], F32, L1)
        t_o1 = pool.do(lambda: G.memset(on1[:, :], 1.0 / (1024 * 256)))
        t_tw = []

        def ternary():
            for i, name in enumerate(("wup", "wgate", "wdown")):
                lw = load(wr[:, :], a[name], t_tw[-1:])
                yield
                for q in range(4):
                    t = dve.do(lambda: V.tensor_reduce(as4[:, q:q + 1], wr[:, 512 * q:512 * q + 512], AX.X, ALU.add,
                                                       apply_absolute_value=True), lw)
                    yield
                t = dve.do(lambda: V.tensor_reduce(asum[:, i:i + 1], as4[:, :], AX.X, ALU.add), t)
                yield
                t = mm(PJ[:, 0:1], on1[:, :], asum[:, i:i + 1], t, t_o1, PJf[0])
                PJf[0] = t = dve.do(lambda: V.tensor_scalar(sc[:, i:i + 1], PJ[:, 0:1], 1e-8, None, ALU.add), t)
                t1 = dve.do(lambda: V.tensor_scalar(hs_[:, i, 0:1], sc[:, i:i + 1], 0.5, None, ALU.mult), t)
                t2 = dve.do(lambda: V.tensor_scalar(hs_[:, i, 1:2], sc[:, i:i + 1], -0.5, None, ALU.mult), t)
                yield
                for c in range(2):
                    w_ = slice(1024 * c, 1024 * c + 1024)
                    tp_ = t_tw[-1:]
                    t3 = dve.do(lambda: V.tensor_scalar(qa[:, :], wr[:, w_], hs_[:, i, 0:1], None, ALU.is_gt), t1, tp_)
                    yield
                    t4 = dve.do(lambda: V.tensor_scalar(qb_[:, :], wr[:, w_], hs_[:, i, 1:2], None, ALU.is_lt), t2, tp_)
                    t_tw.append(pool.do(lambda: G.tensor_tensor(tw[i][:, w_], qa[:, :], qb_[:, :], ALU.subtract), t3,
                                        t4))
                    yield

        t_on = pool.do(lambda: G.memset(ones[:, :], 1.0))
        t_ob = pool.do(lambda: G.memset(onb[:, :], 1.0))
        t_mr0 = pool.do(lambda: G.memset(mrw[:, :, :], 0.0))

        S1, PV1, DN1, PJ = [BANKS[0], BANKS[1]], [BANKS[2], BANKS[3]], BANKS[6], BANKS[7]
        S1f, PV1f, DN1f, PJf = [None, None], [None, None], [None], [None]
        MBf = [None, None]
        mask_tok = {}
        l_m8 = [load(mb8[:, :], a["mrow"][0].partition_broadcast(128))]
        mask_free = [None]
        NG = B * 8
        qf = [None] * 3
        qt1, qt1h = {}, {}
        row1 = [Counted("s_r1a"), Counted("s_r1b")]
        mrf = [None, None]
        mngf = [None, None]
        rowtok = {}

        def mask_load(b):
            mask_tok[b] = dve.do(lambda: V.tensor_scalar(mbc[:, :], mb8[:, :], 1.0, NEG, ALU.subtract, ALU.mult),
                                 l_m8[0], mask_free[0])
            if b + 1 < B:
                l_m8[0] = load(mb8[:, :], a["mrow"][b + 1].partition_broadcast(128), mask_tok[b])

        def qproj(g):
            b, r = g // 8, g % 3
            for j in range(2):
                h = 2 * (g % 8) + j
                for dt in range(2):
                    t = mm(PJ[:, 256 * j:256 * j + 256], M1[:, dt, h, :], xnT[:, dt, S * b:S * b + S], PJf[0],
                           ln1[b],
                           start=(dt == 0), stop=(dt == 1), sig=(dt == 1))
            t1 = act.do(lambda: A.copy(qh[:, r, :], PJ), t, qf[r])
            PJf[0] = t2 = dve.do(lambda: V.tensor_tensor(ql[:, r, :], PJ, qh[:, r, :], ALU.subtract), t1)
            qt1[g], qt1h[g] = t2, t1
            for _ in range(QW):
                yield

        mpc = [None]
        jk = [None]

        def max1(g):
            b, r, par = g // 8, g % 3, g % 2
            if g % 8 == 0:
                mask_load(b)
            last = None
            for u in range(4):
                lhs = qh[:, r, 128 * u:128 * u + 128]
                for c in range(3):
                    i = mi[0] % 2
                    mi[0] += 1
                    t = mm(MB[i][:, :], lhs, cth[:, b, 512 * c:512 * c + 512], MBf[i], qt1h[g])
                    last = MBf[i] = dve.do(lambda: V.tensor_tensor_reduce(
                        out=junk[:, :], in0=MB[i][:, :], in1=mbc[:, 512 * c:512 * c + 512], scale=1.0,
                        scalar=-3e38, op0=ALU.add, op1=ALU.max, accum_out=mp1[:, u, c:c + 1]), t, mask_tok[b], mpc[0],
                        jk[0])
                    jk[0] = last
                    yield
            i = mi[0] % 2
            mi[0] += 1
            for u in range(4):
                t = mm(MB[i][:, TAIL * u:TAIL * u + TAIL], qh[:, r, 128 * u:128 * u + 128], cth[:, b, 1536:S2], MBf[i],
                       sig=(u == 3))
            MBf[i] = t = dve.do(lambda: V.tensor_tensor(
                mtl[:, :, :], MB[i][:, 0:4 * TAIL].rearrange("p (u n) -> p u n", u=4),
                mbc[:, 1536:S2].unsqueeze(1).to_broadcast([128, 4, TAIL]), ALU.add), t)
            t = dve.do(lambda: V.tensor_reduce(mp1[:, :, 3], mtl[:, :, :], AX.X, ALU.max), t)
            mask_free[0] = t
            mpc[0] = t = dve.do(lambda: V.tensor_reduce(mm1[:, :], mp1[:, :, :], AX.X, ALU.max), t, last)
            yield
            for _ in range(MW):
                yield
            t = tp(PJ[0:4, 0:128], mm1[:, :], idn[:, :], t, PJf[0])
            PJf[0] = t = dve.do(lambda: V.tensor_scalar(mng[:, par, :], PJ[0:4, 0:128], -1e20, -1.0, ALU.max, ALU.mult), t,
                                mngf[par])
            yield
            mngf[par] = tw_ = bnc[par].start(rowd[par][0:4, :], mng[:, par, :], t)
            rowtok[g] = row1[par].start(mrw[0:1, par, :], rowd[par][0:4, :].rearrange("(o u) n -> o (u n)", o=1), tw_,
                                        mrf[par], t_mr0)
            yield

        p1f = [None] * NR
        phf = [None] * NR
        LAG = 3
        accf = [None, None]
        p1c = [0]
        rcf = [None]

        def scores1(g, kt):
            b, r, par = g // 8, g % 3, g % 2
            n = 128 if kt < 12 else TAIL
            i = stc[0] % 2
            stc[0] += 1
            ks = slice(128 * kt, 128 * kt + n)
            o = S1[i][0:n, :]
            mm(o, cth[:, b, ks], qh[:, r, :], S1f[i], qt1[g], start=True, stop=False, sig=False)
            mm(o, cth[:, b, ks], ql[:, r, :], start=False, stop=False, sig=False)
            mm(o, ctl[:, b, ks], qh[:, r, :], start=False, stop=False, sig=False)
            t = mm(o, onb[:, 0:n], mrw[:, par, :], rowtok[g], start=False, stop=True)
            if kt == NKT - 1:
                qf[r] = mrf[par] = t
            k = p1c[0] % NR
            p1c[0] += 1
            S1f[i] = te = act.do(lambda: A.activation(
                P1[k][0:n, :], o, ACT.Exp, scale=SCALE1, bias=mcb[0:n, b, kt:kt + 1]), t, p1f[k])
            th = act.do(lambda: A.copy(Ph[k][0:n, :], P1[k][0:n, :]), te, phf[k])
            if kt == 1:
                k0, te0 = hist[-1][0], hist[-1][3]
                accd[g] = hist[-1][4] = pool.do(lambda: G.tensor_tensor(acc[:, par, :], P1[k0][:, :], P1[k][:, :],
                                                                        ALU.add), te, te0, accf[par])
            elif kt > 1:
                accd[g] = pool.do(lambda: G.tensor_tensor(acc[0:n, par, :], acc[0:n, par, :], P1[k][0:n, :], ALU.add),
                                  te, accd[g])
            hist.append([k, n, th, te, accd.get(g)])

        def rest1(s_):
            k, n, th, te, tad = hist[s_]
            tl = dve.do(lambda: V.tensor_tensor(Pl[k][0:n, :], P1[k][0:n, :], Ph[k][0:n, :], ALU.subtract), th, phf[k])
            hist[s_][2] = tl
            p1f[k] = [tl, tad]

        def value1(s_):
            g, kp = s_ // NKT, s_ % NKT
            b, par = g // 8, g % 2
            k, n, tl, te, _ = hist[s_]
            mm(PV1[par], ckh[0:n, b, kp, :], Ph[k][0:n, :], tl, l_ck[b], PV1f[par], start=(kp == 0), stop=False,
               sig=False)
            mm(PV1[par], ckl[0:n, b, kp, :], Ph[k][0:n, :], start=False, stop=False, sig=False)
            phf[k] = pvt[g] = mm(PV1[par], ckh[0:n, b, kp, :], Pl[k][0:n, :], start=False, stop=(kp == NKT - 1))

        hist, accd, pvt = [], {}, {}
        oNf = [None]
        dgf = [None]

        def out1(g):
            b, par = g // 8, g % 2
            ta = accd[g]
            for u in range(4):
                t = mm(DN1[:, 128 * u:128 * u + 128], acc[:, par, 128 * u:128 * u + 128], ones[:, :], ta, DN1f[0],
                       sig=(u == 3))
            accf[par] = t
            t = dve.do(lambda: V.tensor_scalar(dn[:, 0:4], DN1.rearrange("p (u n) -> p u n", u=4)[:, :, 0], 1e-30, None,
                                               ALU.max), t)
            DN1f[0] = t
            t = dve.do(lambda: V.reciprocal(dn[:, 4:8], dn[:, 0:4]), t)
            t = pool.do(lambda: G.tensor_tensor(dg[:, :, :], idn[:, :].unsqueeze(1).to_broadcast([128, 4, 128]),
                                                dn[:, 4:8].unsqueeze(2).to_broadcast([128, 4, 128]), ALU.mult), t, dgf[0])
            yield
            yield
            dgf[0] = t = mm(DN1, ones[:, :], dg[:, :, :].rearrange("p u n -> p (u n)"), t, DN1f[0])
            DN1f[0] = t = act.do(lambda: A.copy(rc[:, :], DN1), t, rcf[0])
            yield
            h = 2 * (g % 8)
            PV1f[par] = rcf[0] = t = dve.do(lambda: V.tensor_tensor(
                oN[:, h:h + 2, :].rearrange("p h n -> p (h n)"), PV1[par], rc[:, :], ALU.mult), t, pvt[g], oNf[0])
            yield
            if g % 8 < 7:
                return
            for t2 in range(2):
                for h in range(H):
                    tt = mm(PJ[:, 0:256], oN[:, h, 128 * t2:128 * t2 + 128], N1[:, h, :], t, PJf[0], start=(h == 0),
                            stop=(h == H - 1), sig=(h == H - 1))
                i = 2 * b + t2
                PJf[0] = x_tok[i] = dve.do(lambda: V.scalar_tensor_tensor(
                    out=x_sb[:, i, :], in0=PJ[:, 0:256], scalar=tg[:, 1:2], in1=x_sb[:, i, :], op0=ALU.mult,
                    op1=ALU.add), tt, x_tok[i])
                yield
            oNf[0] = tt

        for g in range(2):
            for _ in qproj(g):
                pass
        for _ in chain(values(0), max1(0)):
            pass
        ln2 = {}
        bg = chain(values(1), ln_batch(2, PJf, 0, ln1), ln_batch(3, PJf, 0, ln1), values(2), values(3), ternary())
        NS = NG * NKT
        og, nm1 = iter(()), [0]
        mgs = chain(*[gen(g + n) for g in range(NG) for gen, n in ((max1, 1), (qproj, 2)) if g + n < NG])

        def maxima1(half):
            while nm1[0] * 26 < (2 * (s_ + LEAD1) + half) * ITEMS1:
                next(mgs, None)
                nm1[0] += 1

        for s_ in range(NS + LAG + 1):
            g, kt = s_ // NKT, s_ % NKT
            while g < NG and g not in rowtok:
                next(mgs)
                nm1[0] += 1
            if kt == LAG + 2 and s_ > NKT:
                for _ in og:
                    pass
                og = chain(out1(g - 1), ln_batch((g - 1) // 8, PJf, 0, ln2) if g % 8 == 0 else None)
            if s_ < NS:
                scores1(g, kt)
            if 1 <= s_ <= NS:
                rest1(s_ - 1)
            maxima1(1)
            if kt > LAG + 1:
                next(og, None)
            if kt % 4 == 1:
                next(bg, None)
            if LAG <= s_ < NS + LAG:
                value1(s_ - LAG)
            maxima1(2)
        for _ in og:
            pass
        for _ in chain(out1(NG - 1), bg):
            pass
        barrier()

        F1 = Region(base, 107 * KB)
        xh = sb("xh", [128, 2, 2, 512], BF16, F1)
        xlo = sb("xlo", [128, 2, 2, 512], BF16, F1)
        NF = 3
        sg = sb("sg", [128, NF, 512], F32, F1)
        u1 = sb("u1", [128, NF, 512], F32, F1)
        hf = sb("hf", [128, NF, 512], F32, F1)
        hhi = sb("hhi", [128, 2, 8, 512], BF16, F1)
        hlo = sb("hlo", [128, 2, 8, 512], BF16, F1)
        fin = sb("fin", [128, NT, D], F32, F1)
        gs = sb("gs", [128, 1], F32, F1)
        bf = [None] * 8
        t_gs = dve.do(lambda: V.tensor_tensor(gs[:, :], tg[:, 3:4], sc[:, 2:3], ALU.mult))
        up = tw[0][:, :].rearrange("p (c e) -> p c e", c=2)
        ga = tw[1][:, :].rearrange("p (c e) -> p c e", c=2)
        dw = tw[2][:, :].rearrange("p (e d) -> p e d", e=8)
        outd = out.rearrange("b (t p) d -> p b t d", p=128)
        stores, t_x2, t_h2, f1f = [], {}, {}, [[None, None] for _ in range(NF)]

        def halves(ch):
            tok = slice(512 * ch, 512 * ch + 512)
            t = act.do(lambda: A.copy(xh[:, ch, :, :], xnT[:, :, tok]), ln2[2 * ch], ln2[2 * ch + 1])
            t_x2[ch] = t, dve.do(lambda: V.tensor_tensor(xlo[:, ch, :, :], xnT[:, :, tok], xh[:, ch, :, :],
                                                         ALU.subtract), t)
            yield

        def hidden(ch, e, k):
            b0, b1 = 2 * k, 2 * k + 1
            es = slice(128 * e, 128 * e + 128)
            for w, bk in ((up, b0), (ga, b1)):
                for x_, tx, c, s0, s1 in ((xh, 0, 0, True, False), (xh, 0, 1, False, False), (xlo, 1, 0, False, False),
                                          (xlo, 1, 1, False, True)):
                    t = mm(BANKS[bk], w[:, c, es], x_[:, ch, c, :], t_x2[ch][tx], bf[bk], start=s0, stop=s1, sig=s1)
                if w is up:
                    tu = t
            t1 = act.do(lambda: A.activation(sg[:, k, :], BANKS[b0], ACT.Sigmoid, scale=sc[:, 0:1]), tu, f1f[k][0])
            rest()
            bf[b0] = t2 = dve.do(lambda: V.scalar_tensor_tensor(
                out=u1[:, k, :], in0=BANKS[b0], scalar=sc[:, 0:1], in1=sg[:, k, :], op0=ALU.mult, op1=ALU.mult), t1)
            bf[b1] = f1f[k][0] = t3 = dve.do(lambda: V.scalar_tensor_tensor(
                out=hf[:, k, :], in0=BANKS[b1], scalar=sc[:, 1:2], in1=u1[:, k, :], op0=ALU.mult, op1=ALU.mult),
                t2, t, f1f[k][1])
            late.append((ch, e, k, t3))

        late = []

        def rest():
            if not late:
                return
            ch, e, k, t3 = late.pop()
            t4 = act.do(lambda: A.copy(hhi[:, ch, e, :], hf[:, k, :]), t3)
            eng, ob = (pool, G) if e < 6 else (dve, V)
            f1f[k][1] = t5 = eng.do(lambda: ob.tensor_tensor(hlo[:, ch, e, :], hf[:, k, :], hhi[:, ch, e, :],
                                                             ALU.subtract), t4)
            t_h2.setdefault(ch, []).append(t5)

        def project(ch, banks):
            for i in range(4):
                bk, off = banks[i]
                tk = 4 * ch + i
                o = BANKS[bk][:, off:off + 256]
                for e in range(8):
                    for part in (hhi, hlo):
                        t = mm(o, part[:, ch, e, 128 * i:128 * i + 128], dw[:, e, :], t_h2[ch][e], bf[bk],
                               start=(e == 0 and part is hhi), stop=(e == 7 and part is hlo),
                               sig=(e == 7 and part is hlo))
                bf[bk] = tf = dve.do(lambda: V.scalar_tensor_tensor(
                    out=fin[:, tk, :], in0=o, scalar=gs[:, 0:1], in1=x_sb[:, tk, :], op0=ALU.mult, op1=ALU.add), t, t_gs)
                if i % 2:
                    stores.append(load(outd[:, tk // 2, :, :], fin[:, tk - 1:tk + 1, :], tf))
                yield

        side = chain(ln_batch(B - 1, bf, 7, ln2), halves(1))
        for _ in halves(0):
            pass
        next(side)
        next(side)
        for n in range(16):
            ch, e = n // 8, n % 8
            if n == 8:
                for _ in side:
                    pass
                side = project(0, [(6, 0), (7, 0)] * 2)
            hidden(ch, e, n % NF)
            if n in (1, 2, 3, 10, 12, 14):
                next(side, None)
        rest()
        for _ in chain(side, project(1, [(6, 0), (7, 0), (0, 0), (1, 0)])):
            pass
        sp.wait(stores)
        barrier()


def layout(i):
    import numpy as np

    def f(n):
        return np.asarray(i[n])

    def kt(w, c=2):
        return w.reshape(c, 128, -1).transpose(1, 0, 2)

    z, o = np.zeros, np.ones
    g = "L0_xattn_"
    wm = np.concatenate([f(g + "Wk"), f(g + "Wv")], 1).reshape(128, 16, 2, 16)
    bm = np.concatenate([f(g + "bk"), f(g + "bv")], 0).reshape(16, 2, 16)
    wd, bd = f(g + "Wkv_dca"), f(g + "bkv_dca")
    bc = lambda v: np.broadcast_to(v.reshape(1, 1, 256), (128, 1, 256))
    wk0 = np.concatenate([wm[:, :, 0].reshape(128, 1, 256), wd[:, None, 0:256], kt(f(g + "Wq")),
                          bc(bm[:, 0]), bc(bd[0:256]), bc(f(g + "bq"))], 1)
    wv0 = np.concatenate([wm[:, :, 1].reshape(128, 1, 256), wd[:, None, 256:512], bc(bm[:, 1]), bc(bd[256:512])], 1)

    def col(w):
        return np.tile(w, 8)

    fz = z(128, np.float32)
    om, od = fz.copy(), fz.copy()
    om[[48, 112]] = 1
    od[[49, 113]] = 1
    rsel = z((128, 4, 4, 128), np.float32)
    for p in range(4):
        for r in range(2):
            for d in range(16):
                for m, slots in enumerate(((0, 2), (1,), (0, 1), (2,))):
                    for s_ in slots:
                        rsel[16 * (2 * p + r) + d, p, m, 64 * r + 16 * s_ + d] = 1
    ind = (np.arange(128) >= TMAIN).astype(np.float32)
    ahl = np.concatenate([z(64, np.float32), -o(64, np.float32)])
    prm = np.stack([col(f(g + "kn_w")), col(f(g + "kn_b")), col(f(g + "kn_dca_w")), col(f(g + "kn_dca_b")),
                    col(f(g + "qn_w")), col(f(g + "qn_b")), fz, fz, ind, ahl, om, od], 1)
    seld = z((128, 128), np.float32)
    for e in range(16):
        for part in range(3):
            seld[16 * part + e, e] = 1
    ctx = f("ctx_1024")
    mask = f("mask_BxS2_bf1").view(np.uint8)
    mcol = mask[:, :1536].reshape(4, 12, 128).transpose(2, 0, 1)
    h = "L0_ffn_"
    dup = lambda w: np.concatenate([w, w], 0)
    wdT = f(h + "Wdown").T
    j = "L1_xattn_"
    out = {
        "x": f("x").reshape(1024, 256), "ctxT": ctx.transpose(0, 2, 1), "ctxk": ctx, "mrow": mask, "mcol": mcol, "mtail": mask[:, 1536:].T,
        "gates": np.concatenate([f("g_xattn"), f("g_ffn")]),
        "wk0": wk0, "wv0": wv0, "wo0": kt(f(g + "Wo")), "bo0": f(g + "bo"), "prm": prm,
        "sw1T": kt(f(h + "sw1").T), "swgT": kt(f(h + "swg").T), "sw2T": f(h + "sw2").T,
        "rw1T": dup(f(h + "rw1").transpose(2, 0, 1).reshape(64, 2048)),
        "rwgT": dup(f(h + "rwg").transpose(2, 0, 1).reshape(64, 2048)),
        "rw2T": f(h + "rw2").transpose(2, 0, 1), "WgT": kt(f(h + "Wg").T),
        "WdT": kt(np.concatenate([wdT, wdT], 1)), "WuT": dup(f(h + "Wup").T), "bias_e": f(h + "biases"),
        "wqT1": f(j + "Wq").reshape(256, 16, 128).transpose(2, 1, 0),
        "wkT1": f(j + "Wk").reshape(128, 8, 128).transpose(2, 1, 0),
        "wvT1": f(j + "Wv").reshape(128, 8, 128).transpose(2, 1, 0),
        "wo1": f(j + "Wo").reshape(16, 128, 256).transpose(1, 0, 2),
        "wup": kt(f("L1_ffn_W_up").T).reshape(128, 2048), "wgate": kt(f("L1_ffn_W_gate").T).reshape(128, 2048),
        "wdown": kt(f("L1_ffn_W_down").T, 8).reshape(128, 2048),
        "ident": np.eye(128, dtype=np.float32), "seld": seld, "rsel": rsel.reshape(128, 16, 128),
    }
    return {k: np.ascontiguousarray(v) for k, v in out.items()}


def kernel(**inputs):
    import concourse.bacc as _bacc
    from concourse import mybir as _mybir
    from concourse.bass_utils import run_bass_kernel_spmd as _run

    nc = _bacc.Bacc("TRN2", target_bir_lowering=False, num_devices=1)
    laid = layout(inputs)
    arrays, aps = {}, {}
    for name in INS:
        v = laid[name]
        arrays[f"in_{name}"] = v
        aps[name] = nc.dram_tensor(f"in_{name}", v.shape, _mybir.dt.from_np(v.dtype), kind="ExternalInput").ap()
    out = nc.dram_tensor("out_0", (4, 256, 256), _mybir.dt.float32, kind="ExternalOutput").ap()
    program(nc, aps, out)
    r = _run(nc, [arrays], core_ids=[0])
    return r.results[0]["out_0"]
```
